# Optimizing a Trainium2 kernel written in Bass

```python
import numpy as np
import jax
import jax.numpy as jnp

def _softmax(x, axis=-1):
    return jax.nn.softmax(x, axis=axis)

def _gelu(x):
    return jax.nn.gelu(x, approximate=True)

def _silu(x):
    return jax.nn.silu(x)

def _sigmoid(x):
    return jax.nn.sigmoid(x)

def _layernorm(x, axis=-1, eps=1e-05):
    m = jnp.mean(x, axis=axis, keepdims=True)
    v = jnp.var(x, axis=axis, keepdims=True)
    return (x - m) / jnp.sqrt(v + eps)

def _scatter_add(tgt, idx, src, axis=0):
    return tgt.at[idx].add(src)

def _segment_sum(src, seg, n):
    return jax.ops.segment_sum(src, seg, n)
kernel_name = 'mk_gnn_resnorm_d4_gnn_r16_121b8e'

def setup_inputs(seed: int=0):
    np.random.seed(seed)
    _w = jnp.asarray

    def _rec_inputs():
        import jax
        import jax.numpy as jnp
        _gk = jax.random.key(seed)
        x = -0.000202 + 1 * jax.random.normal(jax.random.fold_in(_gk, 1), (6250, 128), jnp.float32)
        src = jax.random.randint(jax.random.fold_in(_gk, 2), (100000,), 0, 6250, jnp.int32)
        dst = jax.random.randint(jax.random.fold_in(_gk, 3), (100000,), 0, 6250, jnp.int32)
        _o = jnp.argsort(dst, stable=True)
        src = src[_o]
        dst = dst[_o]
        edge_weight = jax.random.uniform(jax.random.fold_in(_gk, 12), (100000,), jnp.float32, 0.0, 0.999999)
        return (x, src, dst, edge_weight)
    x, src, dst, edge_weight = _rec_inputs()

    def _L0_gnn_setup():
        import jax, jax.numpy as jnp
        import numpy as np
        NEG_SLOPE = 0.2
        EPS = 1e-16
        key = jax.random.key(seed)
        ks = jax.random.split(key, 6)
        N, F, H, C, E = (3125, 128, 8, 16, 37500)
        node_features = jax.random.normal(ks[0], (N, F), dtype=jnp.float32)
        edge_index = jax.random.randint(ks[1], (2, E), 0, N, dtype=jnp.int64)
        W = jax.random.normal(ks[2], (F, H * C), dtype=jnp.float32) * (1.0 / np.sqrt(F))
        att_src = jax.random.normal(ks[3], (H, C), dtype=jnp.float32)
        att_dst = jax.random.normal(ks[4], (H, C), dtype=jnp.float32)
        bias = jnp.zeros((H * C,), dtype=jnp.float32)
        return {'node_features': node_features, 'edge_index': edge_index, 'W': W, 'att_src': att_src, 'att_dst': att_dst, 'bias': bias}
    _L0_gnn_all = _L0_gnn_setup()
    _L0_gnn_in = {k: v for k, v in _L0_gnn_all.items() if k in ('W', 'att_src', 'att_dst', 'bias')}
    del _L0_gnn_all

    def _L1_gnn_setup():
        import jax, jax.numpy as jnp
        import numpy as np
        N = 6250
        E = 40000
        IN, HID, OUT = (128, 256, 128)

        def _glorot(key, shape):
            fan_in, fan_out = (shape[0], shape[1])
            lim = (6.0 / (fan_in + fan_out)) ** 0.5
            return jax.random.uniform(key, shape, jnp.float32, -lim, lim)
        key = jax.random.key(seed)
        ks = jax.random.split(key, 8)
        x = jax.random.normal(ks[0], (N, IN), jnp.float32)
        edge_index = jax.random.randint(ks[1], (2, E), 0, N, jnp.int64)
        w0a = _glorot(ks[2], (IN, HID))
        b0a = jnp.zeros((HID,), jnp.float32)
        w0b = _glorot(ks[3], (HID, HID))
        b0b = jnp.zeros((HID,), jnp.float32)
        w1a = _glorot(ks[4], (HID, HID))
        b1a = jnp.zeros((HID,), jnp.float32)
        w1b = _glorot(ks[5], (HID, HID))
        b1b = jnp.zeros((HID,), jnp.float32)
        w2a = _glorot(ks[6], (HID, OUT))
        b2a = jnp.zeros((OUT,), jnp.float32)
        w2b = _glorot(ks[7], (OUT, OUT))
        b2b = jnp.zeros((OUT,), jnp.float32)
        return dict(x=x, edge_index=edge_index, w0a=w0a, b0a=b0a, w0b=w0b, b0b=b0b, w1a=w1a, b1a=b1a, w1b=w1b, b1b=b1b, w2a=w2a, b2a=b2a, w2b=w2b, b2b=b2b)
    _L1_gnn_all = _L1_gnn_setup()
    _L1_gnn_in = {k: v for k, v in _L1_gnn_all.items() if k in ('w0a', 'b0a', 'w0b', 'b0b', 'w1a', 'b1a', 'w1b', 'b1b', 'w2a', 'b2a', 'w2b', 'b2b')}
    del _L1_gnn_all

    def _L2_gnn_setup():
        import jax, jax.numpy as jnp
        import numpy as np
        N = 6250
        E = 100000
        D_IN = 128
        D_OUT = 128
        HEADS = 4
        C = D_OUT // HEADS
        NEG_SLOPE = 0.2
        EPS_SOFTMAX = 1e-16
        EPS_LN = 1e-05

        def _gat_edge_conv(x, src, dst, W, att_src, att_dst, gat_bias, skip_W, skip_b, ln_g, ln_b):
            n = x.shape[0]
            h = (x @ W).reshape(n, HEADS, C)
            a_s = jnp.einsum('nhc,hc->nh', h, att_src)
            a_d = jnp.einsum('nhc,hc->nh', h, att_dst)
            e = jax.nn.leaky_relu(a_s[src] + a_d[dst], NEG_SLOPE)
            m = jax.ops.segment_max(e, dst, num_segments=n)
            p = jnp.exp(e - m[dst])
            z = jax.ops.segment_sum(p, dst, num_segments=n)
            alpha = p / (z[dst] + EPS_SOFTMAX)
            msg = h[src] * alpha[:, :, None]
            out = jax.ops.segment_sum(msg, dst, num_segments=n)
            out = out.reshape(n, HEADS * C) + gat_bias
            out = out + x @ skip_W + skip_b
            mu = out.mean(-1, keepdims=True)
            var = ((out - mu) ** 2).mean(-1, keepdims=True)
            return (out - mu) * jax.lax.rsqrt(var + EPS_LN) * ln_g + ln_b
        key = jax.random.key(seed)
        ks = jax.random.split(key, 10)
        x = jax.random.normal(ks[0], (N, D_IN), dtype=jnp.float32)
        edge_index = jax.random.randint(ks[1], (2, E), 0, N, dtype=jnp.int64)
        s = 1.0 / np.sqrt(D_IN)
        W = jax.random.normal(ks[2], (D_IN, HEADS * C), dtype=jnp.float32) * s
        att_src = jax.random.normal(ks[3], (HEADS, C), dtype=jnp.float32) * (1.0 / np.sqrt(C))
        att_dst = jax.random.normal(ks[4], (HEADS, C), dtype=jnp.float32) * (1.0 / np.sqrt(C))
        gat_bias = jax.random.normal(ks[5], (D_OUT,), dtype=jnp.float32) * 0.02
        skip_W = jax.random.normal(ks[6], (D_IN, D_OUT), dtype=jnp.float32) * s
        skip_b = jax.random.normal(ks[7], (D_OUT,), dtype=jnp.float32) * 0.02
        ln_g = jnp.ones((D_OUT,), dtype=jnp.float32)
        ln_b = jnp.zeros((D_OUT,), dtype=jnp.float32)
        return {'x': x, 'edge_index': edge_index, 'W': W, 'att_src': att_src, 'att_dst': att_dst, 'gat_bias': gat_bias, 'skip_W': skip_W, 'skip_b': skip_b, 'ln_g': ln_g, 'ln_b': ln_b}
    _L2_gnn_all = _L2_gnn_setup()
    _L2_gnn_in = {k: v for k, v in _L2_gnn_all.items() if k in ('W', 'att_src', 'att_dst', 'gat_bias', 'skip_W', 'skip_b', 'ln_g', 'ln_b')}
    del _L2_gnn_all

    def _L3_gnn_setup():
        import jax, jax.numpy as jnp
        import numpy as np
        N_NODES = 6250
        N_EDGES = 100000
        C_IN = 128
        C_HID = 128
        C_OUT = 128

        def _gcn_conv(x, row, col, ew, W, b, n_nodes):
            xw = x @ W
            deg = jax.ops.segment_sum(ew, col, num_segments=n_nodes)
            dinv = jnp.where(deg > 0, jax.lax.rsqrt(deg), 0.0)
            norm = dinv[row] * ew * dinv[col]
            msg = xw[row] * norm[:, None]
            out = jax.ops.segment_sum(msg, col, num_segments=n_nodes)
            return out + b
        key = jax.random.key(seed)
        ks = jax.random.split(key, 10)
        x = jax.random.normal(ks[0], (N_NODES, C_IN), dtype=jnp.float32)
        edge_index = jax.random.randint(ks[1], (2, N_EDGES), 0, N_NODES, dtype=jnp.int32)
        edge_weight = jax.random.uniform(ks[2], (N_EDGES,), dtype=jnp.float32)
        s = 1.0 / np.sqrt(C_HID)
        W1 = jax.random.uniform(ks[3], (C_IN, C_HID), minval=-s, maxval=s, dtype=jnp.float32)
        b1 = jnp.zeros((C_HID,), dtype=jnp.float32)
        W2 = jax.random.uniform(ks[4], (C_HID, C_HID), minval=-s, maxval=s, dtype=jnp.float32)
        b2 = jnp.zeros((C_HID,), dtype=jnp.float32)
        W3 = jax.random.uniform(ks[5], (C_HID, C_OUT), minval=-s, maxval=s, dtype=jnp.float32)
        b3 = jnp.zeros((C_OUT,), dtype=jnp.float32)
        return {'x': x, 'edge_index': edge_index, 'edge_weight': edge_weight, 'W1': W1, 'b1': b1, 'W2': W2, 'b2': b2, 'W3': W3, 'b3': b3}
    _L3_gnn_all = _L3_gnn_setup()
    _L3_gnn_in = {k: v for k, v in _L3_gnn_all.items() if k in ('W1', 'b1', 'W2', 'b2', 'W3', 'b3')}
    del _L3_gnn_all
    return {'x': x, 'src': src, 'dst': dst, 'edge_weight': edge_weight, 'L0_gnn_W': _L0_gnn_in['W'], 'L0_gnn_att_src': _L0_gnn_in['att_src'], 'L0_gnn_att_dst': _L0_gnn_in['att_dst'], 'L0_gnn_bias': _L0_gnn_in['bias'], 'L1_gnn_w0a': _L1_gnn_in['w0a'], 'L1_gnn_b0a': _L1_gnn_in['b0a'], 'L1_gnn_w0b': _L1_gnn_in['w0b'], 'L1_gnn_b0b': _L1_gnn_in['b0b'], 'L1_gnn_w1a': _L1_gnn_in['w1a'], 'L1_gnn_b1a': _L1_gnn_in['b1a'], 'L1_gnn_w1b': _L1_gnn_in['w1b'], 'L1_gnn_b1b': _L1_gnn_in['b1b'], 'L1_gnn_w2a': _L1_gnn_in['w2a'], 'L1_gnn_b2a': _L1_gnn_in['b2a'], 'L1_gnn_w2b': _L1_gnn_in['w2b'], 'L1_gnn_b2b': _L1_gnn_in['b2b'], 'L2_gnn_W': _L2_gnn_in['W'], 'L2_gnn_att_src': _L2_gnn_in['att_src'], 'L2_gnn_att_dst': _L2_gnn_in['att_dst'], 'L2_gnn_gat_bias': _L2_gnn_in['gat_bias'], 'L2_gnn_skip_W': _L2_gnn_in['skip_W'], 'L2_gnn_skip_b': _L2_gnn_in['skip_b'], 'L2_gnn_ln_g': _L2_gnn_in['ln_g'], 'L2_gnn_ln_b': _L2_gnn_in['ln_b'], 'L3_gnn_W1': _L3_gnn_in['W1'], 'L3_gnn_b1': _L3_gnn_in['b1'], 'L3_gnn_W2': _L3_gnn_in['W2'], 'L3_gnn_b2': _L3_gnn_in['b2'], 'L3_gnn_W3': _L3_gnn_in['W3'], 'L3_gnn_b3': _L3_gnn_in['b3']}

def reference(x, src, dst, edge_weight, L0_gnn_W, L0_gnn_att_src, L0_gnn_att_dst, L0_gnn_bias, L1_gnn_w0a, L1_gnn_b0a, L1_gnn_w0b, L1_gnn_b0b, L1_gnn_w1a, L1_gnn_b1a, L1_gnn_w1b, L1_gnn_b1b, L1_gnn_w2a, L1_gnn_b2a, L1_gnn_w2b, L1_gnn_b2b, L2_gnn_W, L2_gnn_att_src, L2_gnn_att_dst, L2_gnn_gat_bias, L2_gnn_skip_W, L2_gnn_skip_b, L2_gnn_ln_g, L2_gnn_ln_b, L3_gnn_W1, L3_gnn_b1, L3_gnn_W2, L3_gnn_b2, L3_gnn_W3, L3_gnn_b3):
    import jax
    import jax.numpy as jnp

    def _L0_gnn_ref(node_features, edge_index, W, att_src, att_dst, bias):
        import jax, jax.numpy as jnp
        import numpy as np
        NEG_SLOPE = 0.2
        EPS = 1e-16
        N = node_features.shape[0]
        H, C = att_src.shape
        x = (node_features @ W).reshape(N, H, C)
        loop = jnp.arange(N, dtype=edge_index.dtype)
        src = jnp.concatenate([edge_index[0], loop])
        dst = jnp.concatenate([edge_index[1], loop])
        a_src = jnp.einsum('nhc,hc->nh', x, att_src)
        a_dst = jnp.einsum('nhc,hc->nh', x, att_dst)
        alpha = jax.nn.leaky_relu(a_src[src] + a_dst[dst], NEG_SLOPE)
        amax = jax.ops.segment_max(alpha, dst, num_segments=N)
        alpha = jnp.exp(alpha - amax[dst])
        asum = jax.ops.segment_sum(alpha, dst, num_segments=N)
        alpha = alpha / (asum[dst] + EPS)
        msgs = x[src] * alpha[:, :, None]
        out = jax.ops.segment_sum(msgs, dst, num_segments=N)
        out = out.reshape(N, H * C) + bias
        return jax.nn.selu(out)

    def _L1_gnn_ref(x, edge_index, w0a, b0a, w0b, b0b, w1a, b1a, w1b, b1b, w2a, b2a, w2b, b2b):
        import jax, jax.numpy as jnp
        import numpy as np
        N = 6250
        E = 40000
        IN, HID, OUT = (128, 256, 128)

        def _glorot(key, shape):
            fan_in, fan_out = (shape[0], shape[1])
            lim = (6.0 / (fan_in + fan_out)) ** 0.5
            return jax.random.uniform(key, shape, jnp.float32, -lim, lim)
        src, dst = (edge_index[0], edge_index[1])
        n = x.shape[0]
        layers = [(w0a, b0a, w0b, b0b), (w1a, b1a, w1b, b1b), (w2a, b2a, w2b, b2b)]
        for wa, ba, wb, bb in layers:
            agg = jax.ops.segment_sum(x[src], dst, num_segments=n)
            h = x + agg
            h = jnp.maximum(h @ wa + ba, 0.0) @ wb + bb
            x = jnp.maximum(h, 0.0)
        return x

    def _L2_gnn_ref(x, edge_index, W, att_src, att_dst, gat_bias, skip_W, skip_b, ln_g, ln_b):
        import jax, jax.numpy as jnp
        import numpy as np
        N = 6250
        E = 100000
        D_IN = 128
        D_OUT = 128
        HEADS = 4
        C = D_OUT // HEADS
        NEG_SLOPE = 0.2
        EPS_SOFTMAX = 1e-16
        EPS_LN = 1e-05

        def _gat_edge_conv(x, src, dst, W, att_src, att_dst, gat_bias, skip_W, skip_b, ln_g, ln_b):
            n = x.shape[0]
            h = (x @ W).reshape(n, HEADS, C)
            a_s = jnp.einsum('nhc,hc->nh', h, att_src)
            a_d = jnp.einsum('nhc,hc->nh', h, att_dst)
            e = jax.nn.leaky_relu(a_s[src] + a_d[dst], NEG_SLOPE)
            m = jax.ops.segment_max(e, dst, num_segments=n)
            p = jnp.exp(e - m[dst])
            z = jax.ops.segment_sum(p, dst, num_segments=n)
            alpha = p / (z[dst] + EPS_SOFTMAX)
            msg = h[src] * alpha[:, :, None]
            out = jax.ops.segment_sum(msg, dst, num_segments=n)
            out = out.reshape(n, HEADS * C) + gat_bias
            out = out + x @ skip_W + skip_b
            mu = out.mean(-1, keepdims=True)
            var = ((out - mu) ** 2).mean(-1, keepdims=True)
            return (out - mu) * jax.lax.rsqrt(var + EPS_LN) * ln_g + ln_b
        n = x.shape[0]
        loops = jnp.arange(n, dtype=edge_index.dtype)
        src = jnp.concatenate([edge_index[0], loops])
        dst = jnp.concatenate([edge_index[1], loops])
        return _gat_edge_conv(x, src, dst, W, att_src, att_dst, gat_bias, skip_W, skip_b, ln_g, ln_b)

    def _L3_gnn_ref(x, edge_index, edge_weight, W1, b1, W2, b2, W3, b3):
        import jax, jax.numpy as jnp
        import numpy as np
        N_NODES = 6250
        N_EDGES = 100000
        C_IN = 128
        C_HID = 128
        C_OUT = 128

        def _gcn_conv(x, row, col, ew, W, b, n_nodes):
            xw = x @ W
            deg = jax.ops.segment_sum(ew, col, num_segments=n_nodes)
            dinv = jnp.where(deg > 0, jax.lax.rsqrt(deg), 0.0)
            norm = dinv[row] * ew * dinv[col]
            msg = xw[row] * norm[:, None]
            out = jax.ops.segment_sum(msg, col, num_segments=n_nodes)
            return out + b
        n = x.shape[0]
        loop = jnp.arange(n, dtype=edge_index.dtype)
        row = jnp.concatenate([edge_index[0], loop])
        col = jnp.concatenate([edge_index[1], loop])
        ew = jnp.concatenate([edge_weight, jnp.ones((n,), dtype=edge_weight.dtype)])
        h = _gcn_conv(x, row, col, ew, W1, b1, n)
        h = jax.nn.relu(h)
        h = _gcn_conv(h, row, col, ew, W2, b2, n)
        h = jax.nn.relu(h)
        h = _gcn_conv(h, row, col, ew, W3, b3, n)
        return h
    edge_index = jnp.stack([src, dst])
    x = _layernorm(x + _L0_gnn_ref(x, edge_index, L0_gnn_W, L0_gnn_att_src, L0_gnn_att_dst, L0_gnn_bias), axis=-1)
    x = _layernorm(x + _L1_gnn_ref(x, edge_index, L1_gnn_w0a, L1_gnn_b0a, L1_gnn_w0b, L1_gnn_b0b, L1_gnn_w1a, L1_gnn_b1a, L1_gnn_w1b, L1_gnn_b1b, L1_gnn_w2a, L1_gnn_b2a, L1_gnn_w2b, L1_gnn_b2b), axis=-1)
    x = _layernorm(x + _L2_gnn_ref(x, edge_index, L2_gnn_W, L2_gnn_att_src, L2_gnn_att_dst, L2_gnn_gat_bias, L2_gnn_skip_W, L2_gnn_skip_b, L2_gnn_ln_g, L2_gnn_ln_b), axis=-1)
    x = _layernorm(x + _L3_gnn_ref(x, edge_index, edge_weight, L3_gnn_W1, L3_gnn_b1, L3_gnn_W2, L3_gnn_b2, L3_gnn_W3, L3_gnn_b3), axis=-1)
    return x

_drawn_inputs = setup_inputs


def setup_inputs(seed=0):
    import zlib

    import numpy as np

    out = dict(_drawn_inputs(seed))
    spreads = {'L0_gnn_bias': (0.0, 0.1),
     'L1_gnn_b0a': (0.0, 0.597),
     'L1_gnn_b0b': (0.0, 0.376),
     'L1_gnn_b1a': (0.0, 2.0),
     'L1_gnn_b1b': (0.0, 2.0),
     'L1_gnn_b2a': (0.0, 2.0),
     'L1_gnn_b2b': (0.0, 2.0),
     'L2_gnn_ln_g': (1.0, 0.2),
     'L2_gnn_ln_b': (0.0, 0.1),
     'L3_gnn_b1': (0.0, 0.39),
     'L3_gnn_b2': (0.0, 0.1),
     'L3_gnn_b3': (0.0, 0.1)}
    factors = {'edge_weight': 61.948,
     'L0_gnn_att_dst': 22.664,
     'L2_gnn_att_src': 64.0,
     'L2_gnn_att_dst': 64.0,
     'L2_gnn_gat_bias': 4.778,
     'L2_gnn_skip_b': 5.594}
    for name, (base, spread) in spreads.items():
        noise = np.random.default_rng([zlib.crc32(name.encode()), seed]).standard_normal(out[name].shape)
        drawn = base * np.exp(spread * noise) if base else spread * noise
        out[name] = jnp.asarray(drawn.astype(out[name].dtype))
    for name, factor in factors.items():
        out[name] = (out[name] * factor).astype(out[name].dtype)
    return out
```

```python
from contextlib import ExitStack

import concourse.bass as bass
from concourse import mybir

fp32 = mybir.dt.float32
i32 = mybir.dt.int32
ALU = mybir.AluOpType
ACT = mybir.ActivationFunctionType
AX = mybir.AxisListType
DVE_ONLY = [mybir.EngineType.DVE]

P = 128
N = 6250
D = 128
E = 100000
TILES = -(-N // P)
NPAD = TILES * P
RUNS = -(-E // P)
EPAD = RUNS * P
U = 16
GROUP = 64
GROUPS = -(-(RUNS + TILES - 1) // GROUP)
STEPS = GROUPS * GROUP
TURNS = STEPS // U
BATCH = 7
BATCHES = TILES // BATCH
HID = 256
ACCW = HID + 1
BIG = 1e30
LN_EPS = 1e-5
SOFTMAX_EPS = 1e-16
SLOPE = 0.2
SELU_SCALE = 1.0507009873554805
SELU_ALPHA = 1.6732632423543772
COUNT_ROWS = 125
COUNT_COLS = E // COUNT_ROWS
assert TILES % BATCH == 0 and COUNT_ROWS * COUNT_COLS == E and STEPS % U == 0


class Signal:

    def __init__(self, nc, name):
        self.sem = nc.alloc_semaphore(name)
        self.base = 0

    def at(self, n):
        return self.base + n

    def past(self, n):
        self.base += n


class Memory:

    def __init__(self, nc, ctx):
        def sb(name, shape, dt=fp32):
            return ctx.enter_context(nc.sbuf_tensor(name, shape, dt))

        self.nc = nc
        self.rows = {w: nc.dram_tensor(f"rows_{w}", (NPAD, w), fp32, kind="Internal").ap()
                     for w in (4, 8, 128, 132, 136, 256)}
        self.run_dst = nc.dram_tensor("run_dst", (RUNS, P), i32, kind="Internal").ap()
        self.run_src = nc.dram_tensor("run_src", (RUNS, P), i32, kind="Internal").ap()
        self.run_weight = nc.dram_tensor("run_weight", (RUNS, P), fp32, kind="Internal").ap()
        self.tile_list = nc.dram_tensor("tile_list", (1, STEPS), i32, kind="Internal").ap()
        self.x = sb("x", [P, TILES, D])
        self.acc = sb("acc", [P, TILES + 1, ACCW])
        self.tmp = sb("tmp", [P, TILES, D])
        self.shift = sb("shift", [P, TILES + 1, 16])
        self.top = sb("top", [P, TILES + 1, 8])
        self.self_p = sb("self_p", [P, TILES, 8])
        self.small = sb("small", [P, TILES, 8])
        self.mean = sb("mean", [P, TILES])
        self.var = sb("var", [P, TILES])
        self.dinv = sb("dinv", [P, TILES])
        self.local = sb("local", [P, STEPS])
        self.last = sb("last", [P, STEPS])
        self.src = sb("src", [P, STEPS], i32)
        self.weight = sb("weight", [P, STEPS])
        self.tile_of = sb("tile_of", [1, STEPS], i32)
        self.reset = sb("reset", [GROUP, GROUPS, P])
        self.identity = sb("identity", [P, P])
        self.columns = sb("columns", [P, P])
        self.ones = sb("ones", [P, P])
        self.pick = sb("pick", [P, 2, U // 2], i32)
        self.gathered = sb("gathered", [P, U, HID])
        self.onehot = sb("onehot", [P, 8, P])
        self.turned = sb("turned", [P, 4, P])
        self.here = sb("here", [P, 4, 16])
        self.logit = sb("logit", [P, 4, 8])
        self.logit2 = sb("logit2", [P, 4, 8])
        self.message = sb("message", [P, 4, 136])
        self.stage = sb("stage", [P, BATCH, HID])
        self.stageT = sb("stageT", [P, 2, BATCH * P])
        self.psum = ctx.enter_context(nc.psum_tensor("psum", [P, 8, 512], fp32))
        self.signals = []

        def signal(name):
            self.signals.append(Signal(nc, name))
            return self.signals[-1]

        self.s_chain = signal("s_chain")
        self.s_achain = signal("s_achain")
        self.s_loaded = signal("s_loaded")
        self.s_stored = signal("s_stored")
        self.s_const_ready = signal("s_const_ready")
        self.s_copied = signal("s_copied")
        self.s_turned_up = signal("s_turned_up")
        self.s_turned_copied = signal("s_turned_copied")
        self.s_multiplied = signal("s_multiplied")
        self.s_evacuated = signal("s_evacuated")
        self.s_act_turn = signal("s_act_turn")
        self.s_dve_turn = signal("s_dve_turn")
        self.s_indices_ready = signal("s_indices_ready")
        self.s_picked = signal("s_picked")
        self.s_onehot_ready = signal("s_onehot_ready")
        self.s_degree_put = signal("s_degree_put")
        self.s_summed = signal("s_summed")
        self.s_added = signal("s_added")
        self.s_here_ready = signal("s_here_ready")
        self.s_turned_ready = signal("s_turned_ready")
        self.s_expanded = signal("s_expanded")
        self.s_logits_ready = signal("s_logits_ready")
        self.s_probs_ready = signal("s_probs_ready")
        self.s_message_ready = signal("s_message_ready")
        self.s_heads_turned = signal("s_heads_turned")
        self.s_scanned = signal("s_scanned")
        self.s_turned_back = signal("s_turned_back")
        self.s_maxima_copied = signal("s_maxima_copied")
        self.s_present_ready = signal("s_present_ready")
        self.s_gate = signal("s_gate")
        self.s_rows = [Signal(nc, f"s_rows_{u}") for u in range(U)]


class Chain:

    def __init__(self, engine, done, turn=None, per_turn=0):
        self.engine, self.done, self.turn, self.per_turn, self.n = engine, done, turn, per_turn, 0

    def link(self, instruction):
        self.n += 1
        instruction.then_inc(self.done.sem, 1)
        before = self.done.at(self.n)
        if self.turn is not None:
            before = self.turn * self.per_turn + before
        self.engine.wait_ge(self.done.sem, before)


def start_stage(m):
    with m.nc.Block() as block:

        @block.sync
        def _(sp):
            for raised in m.signals:
                if raised is not m.s_loaded and raised is not m.s_stored:
                    sp.sem_inc(raised.sem, 1)
                    raised.past(1)


def gate(m, engine):
    engine.sem_inc(m.s_gate.sem, 1)


def spread(vector, *shape):
    return vector.partition_broadcast(P)


def over_tiles(ap, width):
    return ap.unsqueeze(2).broadcast_to([P, TILES, width])


def over_nodes(row, width, tiles=TILES):
    return row.unsqueeze(1).broadcast_to([P, tiles, width])


def by_head(ap, heads):
    return ap.rearrange("p t (h c) -> p t h c", h=heads)


def load_stage(m, w, params, x):
    nc = m.nc
    count_dst = m.gathered[0:COUNT_ROWS, 0:4, 0:HID].rearrange("p a b -> p (a b)")[:, 0:COUNT_COLS].bitcast(i32)
    pad = EPAD - E
    with nc.Block() as block:

        @block.sync
        def _(sp):
            n = 0
            full = (TILES - 1) * P
            sp.wait_ge(m.s_const_ready.sem, m.s_const_ready.at(2))
            sp.dma_start(m.x[:, 0:TILES - 1, :], x[0:full, :].rearrange("(t p) d -> p t d", p=P)).then_inc(m.s_loaded.sem, 16)
            sp.dma_start(m.x[0:N - full, TILES - 1, :], x[full:N, :]).then_inc(m.s_loaded.sem, 16)
            sp.dma_start(count_dst, w["dst"].rearrange("(p c) -> p c", c=COUNT_COLS)).then_inc(m.s_loaded.sem, 16)
            n += 3
            whole = RUNS - 1
            for runs, name in ((m.run_dst, "dst"), (m.run_src, "src"), (m.run_weight, "edge_weight")):
                sp.dma_start(runs[0:whole, :], w[name][0:whole * P].rearrange("(r e) -> r e", e=P)).then_inc(m.s_loaded.sem, 16)
                sp.dma_start(runs[whole:RUNS, 0:P - pad], w[name][whole * P:E].rearrange("(r e) -> r e", r=1)).then_inc(m.s_loaded.sem, 16)
                n += 2
            for runs, row in ((m.run_dst, 0), (m.run_src, 1), (m.run_weight, 1)):
                source = m.pick_pad[0:1, row, 0:pad]
                if runs is m.run_weight:
                    source = source.bitcast(fp32)
                sp.dma_start(runs[whole:RUNS, P - pad:P], source).then_inc(m.s_loaded.sem, 16)
                n += 1
            for tile, source in params:
                sp.dma_start(tile, source).then_inc(m.s_loaded.sem, 16)
                n += 1
            sp.wait_ge(m.s_loaded.sem, m.s_loaded.at(16 * n))
            m.s_loaded.past(16 * n)

        @block.vector
        def _(dve):
            nc.vector.memset(m.pick_pad[0:1, 0, :], -1)
            nc.vector.memset(m.pick_pad[0:1, 1, :], 0).then_inc(m.s_const_ready.sem, 1)
            nc.vector.memset(m.ones[:, :], 1.0)
            nc.vector.memset(m.x[:, TILES - 1, :], 0.0).then_inc(m.s_const_ready.sem, 1)

        @block.gpsimd
        def _(pool):
            nc.gpsimd.memset(m.identity[:, :], 0.0).then_inc(m.s_copied.sem, 1)
            pool.wait_ge(m.s_copied.sem, m.s_copied.at(1))
            nc.gpsimd.affine_select(out=m.identity[:, :], in_=m.identity[:, :], compare_op=ALU.not_equal, fill=1.0,
                                    base=0, pattern=[[-1, P]], channel_multiplier=1)
            nc.gpsimd.iota(m.columns_i[:, :], pattern=[[1, P]], base=0, channel_multiplier=0)
            nc.gpsimd.iota(m.step_number_i[:, :], pattern=[[GROUP, GROUPS]], base=0, channel_multiplier=1)

    m.s_const_ready.past(2)
    m.s_copied.past(1)
    return count_dst


def prepare_stage(m, count_dst):
    nc = m.nc
    T1 = TILES + 1
    dstf = m.tmp[0:COUNT_ROWS, 0:7, :].rearrange("p a b -> p (a b)")[:, 0:COUNT_COLS]
    junk = m.tmp[0:COUNT_ROWS, 7:14, :].rearrange("p a b -> p (a b)")[:, 0:COUNT_COLS]
    at = iter(range(14, TILES))

    def scratch(width, dt=fp32):
        s = m.tmp[:, next(at), 0:width]
        return s if dt is fp32 else s.bitcast(dt)

    bounds, below = scratch(T1), scratch(T1)
    start, start_i, first = scratch(T1), scratch(T1, i32), scratch(TILES)
    end_i, final, filled, length = scratch(TILES, i32), scratch(TILES), scratch(TILES), scratch(TILES)
    upto, lead, number = scratch(TILES), scratch(TILES), scratch(TILES)
    step = m.step_number
    tile = scratch(GROUPS)[0:GROUP, :]
    tile_i = scratch(GROUPS, i32)[0:GROUP, :]
    run = scratch(GROUPS)[0:GROUP, :]
    run_i = scratch(GROUPS, i32)[0:GROUP, :]
    tile128 = scratch(GROUPS)[0:GROUP, :]
    match = m.match
    row_i = {name: rows.rearrange("p (g e) -> p g e", g=GROUPS) for name, rows in m.row_i.items()}
    row_f = m.prep_float
    GT = [GROUP, GROUPS, TILES]
    GP = [GROUP, GROUPS, P]

    with nc.Block() as block:

        @block.vector
        def _(dve):
            c = Chain(dve, m.s_chain)
            c.link(nc.vector.tensor_copy(m.columns[:, :], m.columns_i[:, :]))
            c.link(nc.vector.tensor_copy(m.step_number[:, :], m.step_number_i[:, :]))
            c.link(nc.vector.tensor_copy(dstf, count_dst))
            c.link(nc.vector.tensor_scalar(bounds, m.columns[:, 0:T1], float(P), None, ALU.mult))
            c.link(nc.vector.tensor_copy(number, m.columns[:, 0:TILES]))
            c.link(nc.vector.memset(below, 0.0))
            with dve.Fori(0, T1) as t:
                count = Chain(dve, m.s_dve_turn, t, 1)
                count.link(nc.vector.tensor_scalar(junk, dstf, bounds[0:COUNT_ROWS, bass.ds(t, 1)], 0.0, ALU.is_lt, ALU.add,
                                                   accum_out=below[0:COUNT_ROWS, bass.ds(t, 1)]))
            nc.vector.tensor_copy(number, m.columns[:, 0:TILES]).then_inc(m.s_copied.sem, 1)
            dve.wait_ge(m.s_multiplied.sem, m.s_multiplied.at(1))
            c.link(nc.vector.tensor_copy(start, m.psum[:, 0, 0:T1]))
            c.link(nc.vector.tensor_copy(start_i, start))
            c.link(nc.vector.tensor_scalar(start_i, start_i, 7, None, ALU.arith_shift_right))
            c.link(nc.vector.tensor_copy(first, start_i[:, 0:TILES]))
            c.link(nc.vector.tensor_scalar(final, start[:, 1:T1], -1.0, None, ALU.add))
            c.link(nc.vector.tensor_copy(end_i, final))
            c.link(nc.vector.tensor_scalar(end_i, end_i, 7, None, ALU.arith_shift_right))
            c.link(nc.vector.tensor_copy(final, end_i))
            c.link(nc.vector.tensor_tensor(filled, start[:, 1:T1], start[:, 0:TILES], ALU.is_gt))
            c.link(nc.vector.tensor_tensor(length, final, first, ALU.subtract))
            c.link(nc.vector.tensor_scalar(length, length, 1.0, None, ALU.add))
            c.link(nc.vector.tensor_tensor(length, length, filled, ALU.mult))
            c.link(nc.vector.memset(lead, 0.0))
            c.link(nc.vector.tensor_tensor_scan(upto, length, lead, 0.0, ALU.add, ALU.add))
            c.link(nc.vector.tensor_tensor(lead, length, upto, ALU.subtract))
            c.link(nc.vector.tensor_tensor(lead, lead, first, ALU.add))
            steps3 = step[0:GROUP, :].unsqueeze(2).broadcast_to(GT)
            c.link(nc.vector.tensor_tensor(match, upto[0:GROUP, :].unsqueeze(1).broadcast_to(GT), steps3, ALU.is_le))
            c.link(nc.vector.tensor_reduce(tile, match, AX.X, ALU.add))
            c.link(nc.vector.tensor_tensor(match, number[0:GROUP, :].unsqueeze(1).broadcast_to(GT),
                                           tile.unsqueeze(2).broadcast_to(GT), ALU.is_equal))
            c.link(nc.vector.tensor_tensor(match, match, lead[0:GROUP, :].unsqueeze(1).broadcast_to(GT), ALU.mult))
            c.link(nc.vector.tensor_reduce(run, match, AX.X, ALU.add))
            c.link(nc.vector.tensor_tensor(run, run, step[0:GROUP, :], ALU.add))
            c.link(nc.vector.tensor_scalar(run, run, float(RUNS - 1), None, ALU.min))
            c.link(nc.vector.tensor_copy(run_i, run))
            c.link(nc.vector.tensor_copy(tile_i, tile))
            nc.vector.tensor_scalar(tile128, tile, float(P), None, ALU.mult).then_inc(m.s_indices_ready.sem, 1)
            for u in range(U):
                dve.wait_ge(m.s_rows[u].sem, m.s_rows[u].at(16 * len(range(3 * GROUPS)[u::U])))
            c.link(nc.vector.tensor_copy(row_f[:, 0], row_i["dst"]))
            c.link(nc.vector.tensor_copy(row_f[:, 1], row_i["src"]))
            c.link(nc.vector.tensor_copy(row_f[:, 2], row_i["weight"].bitcast(fp32)))
            c.link(nc.vector.memset(m.reset[:, :, 0:1], 0.0))
            c.link(nc.vector.tensor_tensor(m.reset[:, :, 1:P], row_f[:, 0, :, 1:P], row_f[:, 0, :, 0:P - 1], ALU.is_equal))
            c.link(nc.vector.memset(row_f[:, 3], 1.0))
            c.link(nc.vector.tensor_scalar(row_f[:, 3, :, 0:P - 1], m.reset[:, :, 1:P], -1.0, 1.0, ALU.mult, ALU.add))
            c.link(nc.vector.tensor_scalar(m.reset[:, :, :], m.reset[:, :, :], -1.0, BIG, ALU.add, ALU.mult))
            c.link(nc.vector.tensor_tensor(row_f[:, 0], row_f[:, 0], tile128.unsqueeze(2).broadcast_to(GP), ALU.subtract))
            c.link(nc.vector.tensor_scalar(row_f[:, 4], row_f[:, 0], float(2 * NPAD), None, ALU.add))
            c.link(nc.vector.tensor_tensor(row_f[:, 3], row_f[:, 3], row_f[:, 4], ALU.mult))
            nc.vector.tensor_scalar(row_f[:, 3], row_f[:, 3], float(-2 * NPAD), None, ALU.add).then_inc(m.s_copied.sem, 1)
            for a, target in enumerate((m.local, m.src, m.weight, m.last)):
                dve.wait_ge(m.s_turned_up.sem, m.s_turned_up.at(a + 1))
                flat = m.psum[:, 2 * a:2 * a + 2, :].rearrange("p a b -> p (a b)")[:, 0:STEPS]
                nc.vector.tensor_copy(target[:, :], flat).then_inc(m.s_evacuated.sem, 1)
            nc.vector.memset(m.acc[:, :, :], 0.0)
            m.s_chain.past(c.n)

        @block.tensor
        def _(pe):
            pe.wait_ge(m.s_copied.sem, m.s_copied.at(1))
            nc.tensor.matmul(m.psum[:, 0, 0:T1], m.ones[:, :], below[:, :], start=True, stop=True).then_inc(m.s_multiplied.sem, 1)
            pe.wait_ge(m.s_copied.sem, m.s_copied.at(2))
            for a in range(4):
                flat = m.psum[:, 2 * a:2 * a + 2, :].rearrange("p a b -> p (a b)")
                for g in range(GROUPS):
                    turned = nc.tensor.transpose(flat[:, g * GROUP:(g + 1) * GROUP], row_f[:, a, g, :], m.identity[0:GROUP, 0:GROUP])
                turned.then_inc(m.s_turned_up.sem, 1)

        @block.gpsimd
        def _(pool):
            pool.wait_ge(m.s_indices_ready.sem, m.s_indices_ready.at(1))
            for g in range(GROUPS):
                for a, (name, runs) in enumerate((("dst", m.run_dst), ("src", m.run_src), ("weight", m.run_weight_i))):
                    nc.gpsimd.indirect_dma_start(
                        row_i[name][:, g, :], None, runs, bass.IndirectOffsetOnAxis(ap=run_i[:, g:g + 1], axis=0)
                    ).then_inc(m.s_rows[(3 * g + a) % U].sem, 16)

        @block.sync
        def _(sp):
            sp.wait_ge(m.s_indices_ready.sem, m.s_indices_ready.at(1))
            with nc.allow_non_contiguous_dma("a small table"):
                sp.dma_start(m.tile_list.rearrange("o (g p) -> (o p) g", p=GROUP), tile_i,
                             allow_slow_non_contiguous=True).then_inc(m.s_stored.sem, 16)
            sp.wait_ge(m.s_stored.sem, m.s_stored.at(16))
            sp.dma_start(m.tile_of[:, :], m.tile_list).then_inc(m.s_loaded.sem, 16)
            sp.wait_ge(m.s_loaded.sem, m.s_loaded.at(16))

    m.s_dve_turn.past(T1)
    m.s_copied.past(2)
    m.s_multiplied.past(1)
    m.s_indices_ready.past(1)
    for u in range(U):
        m.s_rows[u].past(16 * len(range(3 * GROUPS)[u::U]))
    m.s_turned_up.past(4)
    m.s_evacuated.past(4)
    m.s_stored.past(16)
    m.s_loaded.past(16)


def dense_stage(m, source, blocks, weight, width, target, bias=None, relu=False):
    nc = m.nc
    turned = m.psum[:, 0:4, :].rearrange("p b c -> p (b c)")
    product = m.psum[:, 4:8, :].rearrange("p b c -> p (b c)")

    with nc.Block() as block:

        @block.vector
        def _(dve):
            with dve.Fori(0, BATCHES) as b:
                if True:
                    dve.wait_ge(m.s_turned_up.sem, b + m.s_turned_up.at(0))
                    nc.vector.tensor_scalar(m.stage[:, :, 0:blocks * P], source[:, bass.ds(b * BATCH, BATCH), 0:blocks * P], 1.0, None, ALU.mult).then_inc(m.s_copied.sem, 1)
                    dve.wait_ge(m.s_turned_up.sem, b + m.s_turned_up.at(1))
                    dve.wait_ge(m.s_multiplied.sem, b + m.s_multiplied.at(0))
                    nc.vector.tensor_copy(m.stageT[:, 0:blocks, :], turned[:, 0:blocks * BATCH * P].rearrange("p (k n) -> p k n", k=blocks)).then_inc(m.s_turned_copied.sem, 1)
                    dve.wait_ge(m.s_multiplied.sem, b + m.s_multiplied.at(1))
                    out = target[:, bass.ds(b * BATCH, BATCH), 0:width]
                    got = product[:, 0:BATCH * width].rearrange("p (t n) -> p t n", n=width)
                    if bias is None:
                        nc.vector.tensor_scalar(out, got, 1.0, None, ALU.mult).then_inc(m.s_evacuated.sem, 1)
                    else:
                        nc.vector.tensor_tensor(out, got, over_nodes(bias, width, BATCH), ALU.add).then_inc(m.s_evacuated.sem, 1)
                    if relu:
                        dve.wait_ge(m.s_evacuated.sem, b + m.s_evacuated.at(1))
                        nc.vector.tensor_scalar(out, out, 0.0, None, ALU.max)

        @block.tensor
        def _(pe):
            with pe.Fori(0, BATCHES) as b:
                pe.wait_ge(m.s_copied.sem, b + m.s_copied.at(1))
                for k in range(blocks):
                    for t in range(BATCH):
                        up = nc.tensor.transpose(turned[:, (k * BATCH + t) * P:(k * BATCH + t + 1) * P],
                                                 m.stage[:, t, k * P:(k + 1) * P], m.identity[:, :])
                up.then_inc(m.s_turned_up.sem, 1)
                pe.wait_ge(m.s_turned_copied.sem, b + m.s_turned_copied.at(1))
                pe.wait_ge(m.s_evacuated.sem, b + m.s_evacuated.at(0))
                for t in range(BATCH):
                    for k in range(blocks):
                        mm = nc.tensor.matmul(product[:, t * width:(t + 1) * width], m.stageT[:, k, t * P:(t + 1) * P],
                                              weight[:, k, 0:width], start=(k == 0), stop=(k == blocks - 1))
                mm.then_inc(m.s_multiplied.sem, 1)

    for s in (m.s_copied, m.s_turned_up, m.s_turned_copied, m.s_multiplied, m.s_evacuated):
        s.past(BATCHES)


def store_stage(m, stores):
    nc = m.nc
    with nc.Block() as block:

        @block.sync
        def _(sp):
            for target, source in stores:
                sp.dma_start(target.rearrange("(t p) d -> p t d", p=P), source).then_inc(m.s_stored.sem, 16)
            sp.wait_ge(m.s_stored.sem, m.s_stored.at(16 * len(stores)))

    m.s_stored.past(16 * len(stores))


def pool_gathers(m, pool, table, width):
    nc = m.nc
    half = U // 2
    with pool.Fori(0, TURNS) as i:
        for u in range(U):
            if u % half == 0:
                h = u // half
                for v in range(u, u + half):
                    pool.wait_ge(m.s_rows[v].sem, i * 16 + m.s_rows[v].at(0))
                nc.gpsimd.tensor_copy(m.pick[:, h, :], m.src[:, bass.ds(i * U + u, half)]).then_inc(m.s_picked.sem, 1)
                pool.wait_ge(m.s_picked.sem, i * 2 + m.s_picked.at(h + 1))
            pool.wait_ge(m.s_summed.sem, i * U + m.s_summed.at(u + 1))
            gate(m, pool)
            nc.gpsimd.indirect_dma_start(
                m.gathered[:, u, 0:width], None, table,
                bass.IndirectOffsetOnAxis(ap=m.pick[:, u // half, u % half:u % half + 1], axis=0)
            ).then_inc(m.s_rows[u].sem, 16)


def load_tiles(m, i):
    _, tiles = m.nc.values_load_multi_w_load_instructions(
        m.tile_of[0:1, bass.ds(i * U, U)], engines=DVE_ONLY, min_val=0, max_val=TILES,
        skip_runtime_bounds_check_because="prepare_stage counts the tiles that end before a step: 0 to TILES")
    return tiles


def tile_row(ap, tile, width):
    return ap[:, bass.ds(tile, 1), 0:width].rearrange("p o c -> p (o c)")


def sum_stage(m, table, width, weighted=False, degree=False):
    nc = m.nc
    S, L = 4, 3
    total = width + degree

    with nc.Block() as block:

        @block.gpsimd
        def _(pool):
            pool_gathers(m, pool, table, width)

        @block.vector
        def _(dve):
            dve.sem_inc(m.s_added.sem, S)
            with dve.Fori(0, TURNS) as i:
                tiles = load_tiles(m, i)
                for j in range(U + L):
                    if j < U:
                        dve.wait_ge(m.s_summed.sem, i * U + m.s_summed.at(U + j - S + 1))
                        one = (m.local[:, bass.ds(i * U + j, 1)], ALU.is_equal)
                        if weighted:
                            nc.vector.tensor_scalar(m.onehot[:, j % S, :], m.columns[:, :], one[0],
                                                    m.weight[:, bass.ds(i * U + j, 1)], one[1], ALU.mult).then_inc(m.s_onehot_ready.sem, 1)
                        else:
                            nc.vector.tensor_scalar(m.onehot[:, j % S, :], m.columns[:, :], one[0], None, one[1]).then_inc(m.s_onehot_ready.sem, 1)
                    if j >= L:
                        k = j - L
                        dve.wait_ge(m.s_summed.sem, i * U + m.s_summed.at(U + k + 1))
                        dve.wait_ge(m.s_added.sem, i * U + m.s_added.at(S + k))
                        row = tile_row(m.acc, tiles[k], total)
                        nc.vector.tensor_tensor(row, row, m.psum[:, k % S, 0:total], ALU.add).then_inc(m.s_added.sem, 1)

        if degree:
            @block.scalar
            def _(act):
                with act.Fori(0, TURNS) as i:
                    for u in range(U):
                        act.wait_ge(m.s_summed.sem, i * U + m.s_summed.at(u + 1))
                        nc.scalar.copy(m.gathered[:, u, width:width + 1], m.weight[:, bass.ds(i * U + u, 1)]).then_inc(m.s_degree_put.sem, 1)

        @block.tensor
        def _(pe):
            pe.sem_inc(m.s_summed.sem, U)
            with pe.Fori(0, TURNS) as i:
                for u in range(U):
                    pe.wait_ge(m.s_onehot_ready.sem, i * U + m.s_onehot_ready.at(u + 1))
                    pe.wait_ge(m.s_rows[u].sem, i * 16 + m.s_rows[u].at(16))
                    if degree:
                        pe.wait_ge(m.s_degree_put.sem, i * U + m.s_degree_put.at(u + 1))
                    pe.wait_ge(m.s_added.sem, i * U + m.s_added.at(u + 1))
                    nc.tensor.matmul(m.psum[:, u % S, 0:total], m.onehot[:, u % S, :], m.gathered[:, u, 0:total],
                                     start=True, stop=True).then_inc(m.s_summed.sem, 1)

    m.s_picked.past(2 * TURNS)
    m.s_summed.past(U + STEPS)
    m.s_added.past(S + STEPS)
    m.s_onehot_ready.past(STEPS)
    if degree:
        m.s_degree_put.past(STEPS)
    for s in m.s_rows:
        s.past(16 * TURNS)


def maximum_stage(m, table, heads):
    nc = m.nc
    S, L = 4, 3
    H = heads
    arrived = m.arrived[:, :, 0:H]
    scans = m.scans[:, 0:H, :]
    maxima = m.maxima[:, 0:H + 1, :]
    INNER = GROUP // U

    with nc.Block() as block:

        @block.gpsimd
        def _(pool):
            with pool.Fori(0, GROUPS) as g:
                for v in range(U):
                    pool.wait_ge(m.s_rows[v].sem, g * 16 * INNER + m.s_rows[v].at(0))
                pool.wait_ge(m.s_heads_turned.sem, g + m.s_heads_turned.at(0))
                nc.gpsimd.tensor_copy(m.pick_group[:, :], m.src[:, bass.ds(g * GROUP, GROUP)]).then_inc(m.s_picked.sem, 1)
                pool.wait_ge(m.s_picked.sem, g + m.s_picked.at(1))
                gate(m, pool)
                for v in range(GROUP):
                    nc.gpsimd.indirect_dma_start(
                        arrived[:, v, :], None, table,
                        bass.IndirectOffsetOnAxis(ap=m.pick_group[:, v:v + 1], axis=0)).then_inc(m.s_rows[v % U].sem, 16)

        @block.scalar
        def _(act):
            nc.scalar.copy(maxima[:, H, :], m.ones[:, 0:GROUP]).then_inc(m.s_achain.sem, 1)
            act.wait_ge(m.s_achain.sem, m.s_achain.at(1))
            with act.Fori(0, GROUPS) as g:
                act.wait_ge(m.s_turned_back.sem, g + m.s_turned_back.at(1))
                act.wait_ge(m.s_summed.sem, g * GROUP + m.s_summed.at(S))
                nc.scalar.copy(maxima[:, 0:H, :], m.psum[:, 2, 0:H * GROUP].rearrange("p (h k) -> p h k", h=H)).then_inc(m.s_maxima_copied.sem, 1)

        @block.vector
        def _(dve):
            dve.sem_inc(m.s_added.sem, S)
            with dve.Fori(0, GROUPS) as g:
                dve.wait_ge(m.s_heads_turned.sem, g + m.s_heads_turned.at(1))
                for h in range(H):
                    dve.wait_ge(m.s_turned_back.sem, g + m.s_turned_back.at(0))
                    scan = nc.vector.tensor_tensor_scan(
                        scans[:, h, :], m.reset[:, bass.ds(g, 1), :].rearrange("p o e -> p (o e)"),
                        m.psum[0:GROUP, h // 4, h % 4 * P:(h % 4 + 1) * P], -BIG, ALU.add, ALU.max)
                scan.then_inc(m.s_scanned.sem, 1)
                with dve.Fori(0, INNER) as n:
                    i = g * INNER + n
                    tiles = load_tiles(m, i)
                    for j in range(U + L):
                        if j < U:
                            dve.wait_ge(m.s_summed.sem, i * U + m.s_summed.at(j + 1))
                            nc.vector.tensor_scalar(m.onehot[:, j % S, :], m.columns[:, :], m.last[:, bass.ds(i * U + j, 1)],
                                                    None, ALU.is_equal).then_inc(m.s_onehot_ready.sem, 1)
                        if j >= L:
                            k = j - L
                            dve.wait_ge(m.s_summed.sem, i * U + m.s_summed.at(S + k + 1))
                            dve.wait_ge(m.s_added.sem, i * U + m.s_added.at(S + k))
                            nc.vector.tensor_scalar(m.absent[:, :], m.psum[:, 4 + k % S, H:H + 1], -1.0, BIG,
                                                    ALU.add, ALU.mult).then_inc(m.s_present_ready.sem, 1)
                            dve.wait_ge(m.s_present_ready.sem, i * U + m.s_present_ready.at(k + 1))
                            row = tile_row(m.top, tiles[k], H)
                            nc.vector.scalar_tensor_tensor(row, m.psum[:, 4 + k % S, 0:H], m.absent[:, :], row,
                                                           ALU.add, ALU.max).then_inc(m.s_added.sem, 1)

        @block.tensor
        def _(pe):
            pe.sem_inc(m.s_summed.sem, S)
            with pe.Fori(0, GROUPS) as g:
                for v in range(U):
                    pe.wait_ge(m.s_rows[v].sem, g * 16 * INNER + m.s_rows[v].at(16 * INNER))
                pe.wait_ge(m.s_scanned.sem, g + m.s_scanned.at(0))
                gate(m, pe)
                for h in range(H):
                    up = nc.tensor.transpose(m.psum[0:GROUP, h // 4, h % 4 * P:(h % 4 + 1) * P], arrived[:, :, h], m.identity[:, :])
                up.then_inc(m.s_heads_turned.sem, 1)
                pe.wait_ge(m.s_scanned.sem, g + m.s_scanned.at(1))
                pe.wait_ge(m.s_maxima_copied.sem, g + m.s_maxima_copied.at(0))
                gate(m, pe)
                for h in range(H):
                    back = nc.tensor.transpose(m.psum[:, 2, h * GROUP:(h + 1) * GROUP], scans[:, h, :], m.identity[0:GROUP, 0:GROUP])
                back.then_inc(m.s_turned_back.sem, 1)
                pe.wait_ge(m.s_maxima_copied.sem, g + m.s_maxima_copied.at(1))
                gate(m, pe)
                with pe.Fori(0, INNER) as n:
                    for u in range(U):
                        pe.wait_ge(m.s_onehot_ready.sem, g * GROUP + n * U + m.s_onehot_ready.at(u + 1))
                        pe.wait_ge(m.s_added.sem, g * GROUP + n * U + m.s_added.at(u + 1))
                        nc.tensor.matmul(m.psum[:, 4 + u % S, 0:H + 1], m.onehot[:, u % S, :],
                                         maxima[:, :, bass.ds(n * U + u, 1)].rearrange("p h o -> p (h o)"),
                                         start=True, stop=True).then_inc(m.s_summed.sem, 1)

    for s in m.s_rows:
        s.past(16 * INNER * GROUPS)
    m.s_picked.past(GROUPS)
    m.s_achain.past(1)
    m.s_added.past(S + STEPS)
    m.s_summed.past(S + STEPS)
    m.s_onehot_ready.past(STEPS)
    m.s_present_ready.past(STEPS)
    for s in (m.s_heads_turned, m.s_scanned, m.s_turned_back, m.s_maxima_copied):
        s.past(GROUPS)


def attention_stage(m, table, heads):
    nc = m.nc
    H = heads
    W = D + H
    SO, S = 8, 4
    LOGITS, MESSAGE, ADD = 2, 3, 5

    with nc.Block() as block:

        @block.gpsimd
        def _(pool):
            pool_gathers(m, pool, table, W)

        @block.vector
        def _(dve):
            dve.sem_inc(m.s_added.sem, S)
            dve.sem_inc(m.s_logits_ready.sem, 2)
            with dve.Fori(0, TURNS) as i:
                tiles = load_tiles(m, i)

                def at(signal, n):
                    return i * U + signal.at(n)

                logit_chain = Chain(dve, m.s_chain, i, 3 * U)
                for j in range(U + ADD):
                    if j < U:
                        dve.wait_ge(m.s_summed.sem, at(m.s_summed, U + j - SO + 1))
                        nc.vector.tensor_scalar(m.onehot[:, j % SO, :], m.columns[:, :], m.local[:, bass.ds(i * U + j, 1)],
                                                None, ALU.is_equal).then_inc(m.s_onehot_ready.sem, 1)
                        dve.wait_ge(m.s_expanded.sem, at(m.s_expanded, j + 1))
                        nc.vector.tensor_scalar(m.here[:, j % S, 0:2 * H], tile_row(m.shift, tiles[j], 2 * H), 1.0, None, ALU.mult).then_inc(m.s_here_ready.sem, 1)
                    k = j - LOGITS
                    if 0 <= k < U:
                        s = k % S
                        nodes = m.psum[:, 6 + k % 2, 0:2 * H]
                        dve.wait_ge(m.s_rows[k].sem, i * 16 + m.s_rows[k].at(16))
                        dve.wait_ge(m.s_expanded.sem, at(m.s_expanded, S + k + 1))
                        dve.wait_ge(m.s_probs_ready.sem, at(m.s_probs_ready, k + 1))
                        logit_chain.link(nc.vector.tensor_tensor(m.logit[:, s, 0:H], m.gathered[:, k, D:W], nodes[:, 0:H], ALU.add))
                        logit_chain.link(nc.vector.scalar_tensor_tensor(m.logit2[:, s, 0:H], m.logit[:, s, 0:H], SLOPE, m.logit[:, s, 0:H], ALU.mult, ALU.max))
                        logit_chain.link(nc.vector.tensor_tensor(m.logit[:, s, 0:H], m.logit2[:, s, 0:H], nodes[:, H:2 * H], ALU.subtract))
                        nc.vector.tensor_scalar(m.logit2[:, s, 0:H], m.logit[:, s, 0:H], 0.0, None, ALU.min).then_inc(m.s_logits_ready.sem, 1)
                    k = j - MESSAGE
                    if 0 <= k < U:
                        s = k % S
                        dve.wait_ge(m.s_probs_ready.sem, at(m.s_probs_ready, S + k + 1))
                        dve.wait_ge(m.s_summed.sem, at(m.s_summed, U + k - S + 1))
                        nc.vector.tensor_tensor(
                            m.message[:, s, 0:D].rearrange("p (h c) -> p h c", h=H),
                            m.gathered[:, k, 0:D].rearrange("p (h c) -> p h c", h=H),
                            m.message[:, s, D:W].unsqueeze(2).broadcast_to([P, H, D // H]), ALU.mult).then_inc(m.s_message_ready.sem, 1)
                    k = j - ADD
                    if 0 <= k < U:
                        dve.wait_ge(m.s_summed.sem, at(m.s_summed, U + k + 1))
                        dve.wait_ge(m.s_added.sem, at(m.s_added, S + k))
                        row = tile_row(m.acc, tiles[k], W)
                        nc.vector.tensor_tensor(row, row, m.psum[:, k % S, 0:W], ALU.add).then_inc(m.s_added.sem, 1)

        @block.scalar
        def _(act):
            act.sem_inc(m.s_turned_copied.sem, 2)
            act.sem_inc(m.s_probs_ready.sem, S)
            with act.Fori(0, TURNS) as i:

                def at(signal, n):
                    return i * U + signal.at(n)

                for j in range(U + LOGITS):
                    if j < U:
                        act.wait_ge(m.s_turned_ready.sem, at(m.s_turned_ready, j + 1))
                        act.wait_ge(m.s_expanded.sem, at(m.s_expanded, j + 1))
                        nc.scalar.copy(m.turned[:, j % S, :], m.psum[:, 4 + j % 2, 0:P]).then_inc(m.s_turned_copied.sem, 1)
                    k = j - LOGITS
                    if 0 <= k < U:
                        act.wait_ge(m.s_logits_ready.sem, at(m.s_logits_ready, 2 + k + 1))
                        act.wait_ge(m.s_summed.sem, at(m.s_summed, U + k - S + 1))
                        nc.scalar.activation(m.message[:, k % S, D:W], m.logit2[:, k % S, 0:H], ACT.Exp).then_inc(m.s_probs_ready.sem, 1)

        @block.tensor
        def _(pe):
            pe.sem_inc(m.s_summed.sem, U)
            pe.sem_inc(m.s_expanded.sem, S)
            with pe.Fori(0, TURNS) as i:

                def at(signal, n):
                    return i * U + signal.at(n)

                for j in range(U + 4):
                    if j < U:
                        pe.wait_ge(m.s_onehot_ready.sem, at(m.s_onehot_ready, j + 1))
                        pe.wait_ge(m.s_turned_copied.sem, at(m.s_turned_copied, j + 1))
                        nc.tensor.transpose(m.psum[:, 4 + j % 2, 0:P], m.onehot[:, j % SO, :], m.identity[:, :]).then_inc(m.s_turned_ready.sem, 1)
                    k = j - 1
                    if 0 <= k < U:
                        pe.wait_ge(m.s_turned_copied.sem, at(m.s_turned_copied, 2 + k + 1))
                        pe.wait_ge(m.s_here_ready.sem, at(m.s_here_ready, k + 1))
                        pe.wait_ge(m.s_logits_ready.sem, at(m.s_logits_ready, k + 1))
                        nc.tensor.matmul(m.psum[:, 6 + k % 2, 0:2 * H], m.turned[:, k % S, :], m.here[:, k % S, 0:2 * H],
                                         start=True, stop=True).then_inc(m.s_expanded.sem, 1)
                    k = j - 4
                    if 0 <= k < U:
                        pe.wait_ge(m.s_message_ready.sem, at(m.s_message_ready, k + 1))
                        pe.wait_ge(m.s_added.sem, at(m.s_added, k + 1))
                        nc.tensor.matmul(m.psum[:, k % S, 0:W], m.onehot[:, k % SO, :], m.message[:, k % S, 0:W],
                                         start=True, stop=True).then_inc(m.s_summed.sem, 1)

    m.s_picked.past(2 * TURNS)
    m.s_chain.past(3 * STEPS)
    m.s_added.past(S + STEPS)
    m.s_logits_ready.past(2 + STEPS)
    m.s_summed.past(U + STEPS)
    m.s_expanded.past(S + STEPS)
    m.s_turned_copied.past(2 + STEPS)
    m.s_probs_ready.past(S + STEPS)
    for s in (m.s_onehot_ready, m.s_here_ready, m.s_message_ready, m.s_turned_ready):
        s.past(STEPS)
    for s in m.s_rows:
        s.past(16 * TURNS)


def head_stage(m, att_src, att_dst, heads, narrow, wide):
    nc = m.nc
    H = heads
    h = m.acc[:, 0:TILES, 0:D]
    a_src = m.acc[:, 0:TILES, D:D + H]
    with nc.Block() as block:

        @block.vector
        def _(dve):
            c = Chain(dve, m.s_chain)
            c.link(nc.vector.tensor_tensor(m.tmp[:, :, :], h, over_nodes(att_src, D), ALU.mult))
            c.link(nc.vector.tensor_reduce(a_src, by_head(m.tmp[:, :, :], H), AX.X, ALU.add))
            c.link(nc.vector.tensor_tensor(m.tmp[:, :, :], h, over_nodes(att_dst, D), ALU.mult))
            c.link(nc.vector.memset(m.shift[:, :, :], 0.0))
            c.link(nc.vector.tensor_reduce(m.shift[:, 0:TILES, 0:H], by_head(m.tmp[:, :, :], H), AX.X, ALU.add))
            c.link(nc.vector.memset(m.top[:, :, :], 0.0))
            c.link(nc.vector.tensor_copy(m.top[:, 0:TILES, 0:H], a_src))
            m.s_chain.past(c.n)

        @block.sync
        def _(sp):
            sp.wait_ge(m.s_chain.sem, m.s_chain.at(0))
            sp.dma_start(narrow.rearrange("(t p) d -> p t d", p=P), a_src).then_inc(m.s_stored.sem, 16)
            sp.dma_start(wide.rearrange("(t p) d -> p t d", p=P), m.acc[:, 0:TILES, 0:D + H]).then_inc(m.s_stored.sem, 16)
            sp.wait_ge(m.s_stored.sem, m.s_stored.at(32))

    m.s_stored.past(32)


def shift_stage(m, heads):
    nc = m.nc
    H = heads
    a_dst, maximum = m.shift[:, 0:TILES, 0:H], m.shift[:, 0:TILES, H:2 * H]
    top, small, p = m.top[:, 0:TILES, 0:H], m.small[:, :, 0:H], m.self_p[:, :, 0:H]
    h, a_src = m.acc[:, 0:TILES, 0:D], m.acc[:, 0:TILES, D:D + H]
    with nc.Block() as block:

        @block.vector
        def _(dve):
            c = Chain(dve, m.s_chain)
            c.link(nc.vector.tensor_tensor(top, top, a_dst, ALU.add))
            c.link(nc.vector.tensor_scalar(small, top, SLOPE, None, ALU.mult))
            c.link(nc.vector.tensor_tensor(maximum, small, top, ALU.max))
            c.link(nc.vector.tensor_tensor(p, a_src, a_dst, ALU.add))
            c.link(nc.vector.tensor_scalar(small, p, SLOPE, None, ALU.mult))
            c.link(nc.vector.tensor_tensor(small, small, p, ALU.max))
            c.link(nc.vector.tensor_tensor(small, small, maximum, ALU.subtract))
            dve.wait_ge(m.s_act_turn.sem, m.s_act_turn.at(1))
            c.link(nc.vector.tensor_copy(a_src, p))
            for n in range(H):
                part = slice(n * (D // H), (n + 1) * (D // H))
                c.link(nc.vector.tensor_tensor(h[:, :, part], h[:, :, part], p[:, :, n:n + 1].broadcast_to([P, TILES, D // H]), ALU.mult))
            m.n_shift = c.n

        @block.scalar
        def _(act):
            act.wait_ge(m.s_chain.sem, m.s_chain.at(7))
            nc.scalar.activation(p, small, ACT.Exp).then_inc(m.s_act_turn.sem, 1)

    m.s_chain.past(m.n_shift)
    m.s_act_turn.past(1)


def divide_heads(m, c, heads, bias):
    nc = m.nc
    H = heads
    z, small, out = m.acc[:, 0:TILES, D:D + H], m.small[:, :, 0:H], m.acc[:, 0:TILES, 0:D]
    c.link(nc.vector.tensor_scalar(small, z, SOFTMAX_EPS, None, ALU.add))
    c.link(nc.vector.reciprocal(small, small))
    for n in range(H):
        part = slice(n * (D // H), (n + 1) * (D // H))
        c.link(nc.vector.tensor_tensor(out[:, :, part], out[:, :, part], small[:, :, n:n + 1].broadcast_to([P, TILES, D // H]), ALU.mult))
    c.link(nc.vector.tensor_tensor(out, out, over_nodes(bias, D), ALU.add))


def center(m, c, dve, value):
    nc = m.nc
    c.link(nc.vector.tensor_reduce(m.mean[:, :], value, AX.X, ALU.add))
    c.link(nc.vector.tensor_scalar(m.mean[:, :], m.mean[:, :], 1.0 / D, None, ALU.mult))
    c.link(nc.vector.tensor_tensor(value, value, over_tiles(m.mean[:, :], D), ALU.subtract))
    c.link(nc.vector.tensor_tensor(m.tmp[:, :, :], value, value, ALU.mult))
    c.link(nc.vector.tensor_reduce(m.var[:, :], m.tmp[:, :, :], AX.X, ALU.add))
    nc.vector.tensor_scalar(m.var[:, :], m.var[:, :], 1.0 / D, LN_EPS, ALU.mult, ALU.add).then_inc(m.s_dve_turn.sem, 1)


def rescale(m, c, dve, value, n):
    nc = m.nc
    dve.wait_ge(m.s_act_turn.sem, m.s_act_turn.at(n))
    c.link(nc.vector.reciprocal(m.mean[:, :], m.var[:, :]))
    c.link(nc.vector.tensor_tensor(value, value, over_tiles(m.mean[:, :], D), ALU.mult))


def root(m, act, n):
    act.wait_ge(m.s_dve_turn.sem, m.s_dve_turn.at(n))
    m.nc.scalar.activation(m.var[:, :], m.var[:, :], ACT.Sqrt).then_inc(m.s_act_turn.sem, 1)


def selu_stage(m, bias):
    nc = m.nc
    out, tmp, x = m.acc[:, 0:TILES, 0:D], m.tmp[:, :, :], m.x[:, :, :]
    with nc.Block() as block:

        @block.vector
        def _(dve):
            c = Chain(dve, m.s_chain)
            divide_heads(m, c, 8, bias)
            nc.vector.tensor_scalar(tmp, out, 0.0, None, ALU.min).then_inc(m.s_dve_turn.sem, 1)
            dve.wait_ge(m.s_act_turn.sem, m.s_act_turn.at(1))
            c.link(nc.vector.tensor_scalar(tmp, tmp, -1.0, SELU_SCALE * SELU_ALPHA, ALU.add, ALU.mult))
            c.link(nc.vector.tensor_tensor(x, x, tmp, ALU.add))
            c.link(nc.vector.tensor_scalar(out, out, 0.0, SELU_SCALE, ALU.max, ALU.mult))
            c.link(nc.vector.tensor_tensor(x, x, out, ALU.add))
            center(m, c, dve, x)
            rescale(m, c, dve, x, 2)
            c.link(nc.vector.tensor_copy(m.acc[:, 0:TILES, 0:D], x))
            c.link(nc.vector.memset(m.acc[:, :, D:D + 1], 1.0))
            m.n = c.n

        @block.scalar
        def _(act):
            act.wait_ge(m.s_dve_turn.sem, m.s_dve_turn.at(1))
            nc.scalar.activation(tmp, tmp, ACT.Exp).then_inc(m.s_act_turn.sem, 1)
            root(m, act, 2)

    m.s_chain.past(m.n)
    m.s_dve_turn.past(2)
    m.s_act_turn.past(2)


def degree_stage(m):
    nc = m.nc
    degree = m.acc[:, 0:TILES, D:D + 1].rearrange("p t o -> p (t o)")
    with nc.Block() as block:

        @block.vector
        def _(dve):
            c = Chain(dve, m.s_chain)
            c.link(nc.vector.tensor_scalar(m.mean[:, :], degree, 0.0, None, ALU.is_gt))
            nc.vector.tensor_scalar(m.var[:, :], degree, 1e-30, None, ALU.max).then_inc(m.s_dve_turn.sem, 1)
            dve.wait_ge(m.s_act_turn.sem, m.s_act_turn.at(1))
            c.link(nc.vector.reciprocal(m.dinv[:, :], m.var[:, :]))
            c.link(nc.vector.tensor_tensor(m.dinv[:, :], m.dinv[:, :], m.mean[:, :], ALU.mult))
            m.n = c.n

        @block.scalar
        def _(act):
            root(m, act, 1)

    m.s_chain.past(m.n)
    m.s_dve_turn.past(1)
    m.s_act_turn.past(1)


def bias_relu_stage(m, bias):
    nc = m.nc
    out = m.acc[:, 0:TILES, 0:D]
    with nc.Block() as block:

        @block.vector
        def _(dve):
            c = Chain(dve, m.s_chain)
            c.link(nc.vector.tensor_tensor(out, out, over_nodes(bias, D), ALU.add))
            c.link(nc.vector.tensor_scalar(out, out, 0.0, None, ALU.max))
            m.n = c.n

    m.s_chain.past(m.n)


def residual_stage(m):
    nc = m.nc
    x = m.x[:, :, :]
    with nc.Block() as block:

        @block.vector
        def _(dve):
            c = Chain(dve, m.s_chain)
            c.link(nc.vector.tensor_tensor(x, x, m.acc[:, 0:TILES, 0:D], ALU.add))
            center(m, c, dve, x)
            rescale(m, c, dve, x, 1)
            m.n = c.n

        @block.scalar
        def _(act):
            root(m, act, 1)

    m.s_chain.past(m.n)
    m.s_dve_turn.past(1)
    m.s_act_turn.past(1)


def divide_stage(m, bias):
    nc = m.nc
    with nc.Block() as block:

        @block.vector
        def _(dve):
            c = Chain(dve, m.s_chain)
            divide_heads(m, c, 4, bias)
            m.n = c.n

    m.s_chain.past(m.n)


def skip_norm_stage(m, skip_bias, gain, offset):
    nc = m.nc
    out = m.acc[:, 0:TILES, 0:D]
    with nc.Block() as block:

        @block.vector
        def _(dve):
            c = Chain(dve, m.s_chain)
            c.link(nc.vector.tensor_tensor(out, out, m.tmp[:, :, :], ALU.add))
            c.link(nc.vector.tensor_tensor(out, out, over_nodes(skip_bias, D), ALU.add))
            center(m, c, dve, out)
            rescale(m, c, dve, out, 1)
            c.link(nc.vector.tensor_tensor(out, out, over_nodes(gain, D), ALU.mult))
            c.link(nc.vector.tensor_tensor(out, out, over_nodes(offset, D), ALU.add))
            m.n = c.n

        @block.scalar
        def _(act):
            root(m, act, 1)

    m.s_chain.past(m.n)
    m.s_dve_turn.past(1)
    m.s_act_turn.past(1)


def scale_stage(m, bias=None, relu=False):
    nc = m.nc
    out = m.acc[:, 0:TILES, 0:D]
    with nc.Block() as block:

        @block.vector
        def _(dve):
            c = Chain(dve, m.s_chain)
            c.link(nc.vector.tensor_tensor(out, out, over_tiles(m.dinv[:, :], D), ALU.mult))
            if bias is not None:
                c.link(nc.vector.tensor_tensor(out, out, over_nodes(bias, D), ALU.add))
            if relu:
                c.link(nc.vector.tensor_scalar(out, out, 0.0, None, ALU.max))
            m.n = c.n

    m.s_chain.past(m.n)


def output_stage(m, out):
    nc = m.nc
    full = (TILES - 1) * P
    with nc.Block() as block:

        @block.sync
        def _(sp):
            sp.dma_start(out[0:full, :].rearrange("(t p) d -> p t d", p=P), m.x[:, 0:TILES - 1, :]).then_inc(m.s_stored.sem, 16)
            sp.dma_start(out[full:N, :], m.x[0:N - full, TILES - 1, :]).then_inc(m.s_stored.sem, 16)
            sp.wait_ge(m.s_stored.sem, m.s_stored.at(32))

    m.s_stored.past(32)


def build(nc, w, out):
    with ExitStack() as ctx:
        m = Memory(nc, ctx)

        def sb(name, shape, dt=fp32):
            return ctx.enter_context(nc.sbuf_tensor(name, shape, dt))

        m.run_weight_i = m.run_weight.bitcast(i32)
        m.pick_pad = sb("pick_pad", [1, 2, P], i32)
        m.columns_i = sb("columns_i", [P, P], i32)
        m.step_number_i = sb("step_number_i", [P, GROUPS], i32)
        m.step_number = sb("step_number", [P, GROUPS])
        m.pick_group = sb("pick_group", [P, GROUP], i32)
        m.absent = sb("absent", [P, 1])
        m.arrived = sb("arrived", [P, GROUP, 8])
        m.scans = sb("scans", [GROUP, 8, P])
        m.maxima = sb("maxima", [P, 9, GROUP])
        flat = m.acc[:, :, :].rearrange("p t c -> p (t c)")
        size = GROUPS * P
        m.prep_float = flat[0:GROUP, 0:5 * size].rearrange("p (a g e) -> p a g e", a=5, g=GROUPS)
        loaned = m.gathered[0:GROUP].rearrange("p a b -> p (a b)")
        m.row_i = {"dst": loaned[:, 0:size].bitcast(i32), "src": loaned[:, size:2 * size].bitcast(i32),
                   "weight": flat[0:GROUP, 5 * size:6 * size].bitcast(i32)}
        m.match = m.stage[0:GROUP].rearrange("p a b -> p (a b)")[:, 0:GROUPS * TILES].rearrange("p (g t) -> p g t", g=GROUPS)

        params = []

        def weight(name, inputs, width):
            blocks = inputs // P
            t = sb("w_" + name, [P, blocks, width])
            params.append((t[:, :, :], w[name].rearrange("(k p) n -> p k n", p=P)))
            return t

        def row(name, width=D):
            t = sb("r_" + name, [P, width])
            source = w[name]
            if len(source.shape) == 2:
                source = source.rearrange("h c -> (h c)")
            params.append((t[:, :], spread(source)))
            return t[:, :]

        g0, g1, g2, g3 = "L0_gnn_", "L1_gnn_", "L2_gnn_", "L3_gnn_"
        W0 = weight(g0 + "W", D, D)
        s0, d0, b0 = row(g0 + "att_src"), row(g0 + "att_dst"), row(g0 + "bias")
        w0a, w0b = weight(g1 + "w0a", D, HID), weight(g1 + "w0b", HID, HID)
        w1a, w1b = weight(g1 + "w1a", HID, HID), weight(g1 + "w1b", HID, HID)
        w2a, w2b = weight(g1 + "w2a", HID, D), weight(g1 + "w2b", D, D)
        b0a, b0b = row(g1 + "b0a", HID), row(g1 + "b0b", HID)
        b1a, b1b = row(g1 + "b1a", HID), row(g1 + "b1b", HID)
        b2a, b2b = row(g1 + "b2a"), row(g1 + "b2b")
        W2, skip = weight(g2 + "W", D, D), weight(g2 + "skip_W", D, D)
        s2, d2 = row(g2 + "att_src"), row(g2 + "att_dst")
        gb, sbias, lng, lnb = row(g2 + "gat_bias"), row(g2 + "skip_b"), row(g2 + "ln_g"), row(g2 + "ln_b")
        G = [weight(g3 + f"W{n}", D, D) for n in (1, 2, 3)]
        gbias = [row(g3 + f"b{n}") for n in (1, 2, 3)]

        start_stage(m)
        count_dst = load_stage(m, w, params, w["x"])
        prepare_stage(m, count_dst)

        dense_stage(m, m.x, 1, W0, D, m.acc)
        head_stage(m, s0, d0, 8, m.rows[8], m.rows[136])
        maximum_stage(m, m.rows[8], 8)
        shift_stage(m, 8)
        attention_stage(m, m.rows[136], 8)
        selu_stage(m, b0)

        store_stage(m, [(m.rows[128], m.acc[:, 0:TILES, 0:D])])
        sum_stage(m, m.rows[128], D, degree=True)
        degree_stage(m)
        dense_stage(m, m.acc, 1, w0a, HID, m.acc, b0a, relu=True)
        dense_stage(m, m.acc, 2, w0b, HID, m.acc, b0b, relu=True)
        store_stage(m, [(m.rows[256], m.acc[:, 0:TILES, 0:HID])])
        sum_stage(m, m.rows[256], HID)
        dense_stage(m, m.acc, 2, w1a, HID, m.acc, b1a, relu=True)
        dense_stage(m, m.acc, 2, w1b, HID, m.acc, b1b, relu=True)
        dense_stage(m, m.acc, 2, w2a, D, m.acc)
        store_stage(m, [(m.rows[128], m.acc[:, 0:TILES, 0:D])])
        sum_stage(m, m.rows[128], D)
        bias_relu_stage(m, b2a)
        dense_stage(m, m.acc, 1, w2b, D, m.acc, b2b, relu=True)
        residual_stage(m)

        dense_stage(m, m.x, 1, W2, D, m.acc)
        head_stage(m, s2, d2, 4, m.rows[4], m.rows[132])
        maximum_stage(m, m.rows[4], 4)
        shift_stage(m, 4)
        attention_stage(m, m.rows[132], 4)
        divide_stage(m, gb)
        dense_stage(m, m.x, 1, skip, D, m.tmp)
        skip_norm_stage(m, sbias, lng, lnb)
        residual_stage(m)

        for n in range(3):
            dense_stage(m, m.x if n == 0 else m.acc, 1, G[n], D, m.acc)
            scale_stage(m)
            store_stage(m, [(m.rows[128], m.acc[:, 0:TILES, 0:D])])
            sum_stage(m, m.rows[128], D, weighted=True)
            scale_stage(m, gbias[n], relu=n < 2)
        residual_stage(m)
        output_stage(m, out)


def kernel(**inputs):
    import numpy as _np
    import concourse.bacc as _bacc
    from concourse.bass_utils import run_bass_kernel_spmd as _run

    nc = _bacc.Bacc("TRN2", target_bir_lowering=False, num_devices=1)
    arrays, w = {}, {}
    for name, value in inputs.items():
        a = _np.ascontiguousarray(value)
        arrays[f"in_{name}"] = a
        w[name] = nc.dram_tensor(f"in_{name}", a.shape, mybir.dt.from_np(a.dtype), kind="ExternalInput").ap()
    out = nc.dram_tensor("out_x", (N, D), fp32, kind="ExternalOutput").ap()
    build(nc, w, out)
    return _run(nc, [arrays], core_ids=[0]).results[0]["out_x"]
```

```python
from contextlib import ExitStack

import concourse.bass as bass
from concourse import mybir

fp32 = mybir.dt.float32
bf16 = mybir.dt.bfloat16
i32 = mybir.dt.int32
ALU = mybir.AluOpType
ACT = mybir.ActivationFunctionType
AX = mybir.AxisListType
DVE_ONLY = [mybir.EngineType.DVE]
PE_ONLY = [mybir.EngineType.PE]

P = 128
N = 6250
D = 128
E = 100000
TILES = -(-N // P)
NPAD = TILES * P
RUNS = -(-E // P)
EPAD = RUNS * P
U = 16
QUAD = 4
QUADS = 13
GROUP = QUAD * QUADS
GROUPS = -(-(RUNS + TILES - 1) // GROUP)
STEPS = GROUPS * GROUP
TURNS = STEPS // U
BATCH = 7
BATCHES = TILES // BATCH
HID = 256
ACCW = HID + 1
BIG = 2.0 ** 100
LN_EPS = 1e-5
SOFTMAX_EPS = 1e-16
SLOPE = 0.2
SELU_SCALE = 1.0507009873554805
SELU_ALPHA = 1.6732632423543772
COUNT_ROWS = 125
COUNT_COLS = E // COUNT_ROWS
MOST = 20
SUM_ROW = 16
WIDE = D + 8
assert GROUPS % 2 == 0 and TILES % BATCH == 0 and COUNT_ROWS * COUNT_COLS == E and STEPS % U == 0


class Signal:

    def __init__(self, nc, name):
        self.sem = nc.alloc_semaphore(name)
        self.base = 0

    def at(self, n):
        return self.base + n

    def past(self, n):
        self.base += n


class Parts:

    def __init__(self, room):
        self.room, self.end = room, 0

    def take(self, a, b, c=1):
        begin, self.end = self.end, self.end + a * b * c
        part = self.room[:, begin:self.end]
        if c == 1:
            return part.rearrange("p (a b) -> p a b", a=a)
        return part.rearrange("p (a b c) -> p a b c", a=a, b=b)


class Memory:

    def __init__(self, nc, ctx):
        def sb(name, shape, dt=fp32):
            return ctx.enter_context(nc.sbuf_tensor(name, shape, dt))

        self.nc = nc
        self.rows = {w: nc.dram_tensor(f"rows_{w}", (NPAD, w), fp32, kind="Internal").ap()
                     for w in (128, 132, 136, 256)}
        self.run_dst = nc.dram_tensor("run_dst", (RUNS, P), i32, kind="Internal").ap()
        self.run_src = nc.dram_tensor("run_src", (RUNS, P), i32, kind="Internal").ap()
        self.run_weight = nc.dram_tensor("run_weight", (RUNS, P), fp32, kind="Internal").ap()
        self.tile_list = nc.dram_tensor("tile_list", (1, STEPS), i32, kind="Internal").ap()
        self.x = sb("x", [P, TILES, D])
        acc = sb("acc", [P, (TILES + 1) * ACCW])
        self.acc_flat = acc[:, :]
        self.acc = acc[:, :].rearrange("p (t c) -> p t c", c=ACCW)
        parts = Parts(acc)
        self.sums = parts.take(TILES + 1, WIDE)
        self.new_top = parts.take(TILES + 1, 8)
        self.turned = parts.take(1, QUAD * P).bitcast(bf16).rearrange("p a (b c) -> p (a b) c", b=2)
        self.message = parts.take(2, QUAD, WIDE)
        self.arrived = parts.take(GROUP, 8)
        self.rest = parts.take(8, GROUP)
        self.lastone = parts.take(2 * QUAD, P).bitcast(bf16).rearrange("p a (b c) -> p (a b) c", b=2)
        self.scans = parts.take(8, P)[0:GROUP]
        room = sb("room", [P, 2 * GROUP * WIDE])
        self.wide = room[:, :].rearrange("p (b s w) -> p b s w", b=2, w=WIDE)
        parts = Parts(room)
        self.tmp = parts.take(TILES, D)
        self.stage = parts.take(BATCH, HID)
        self.stageT = parts.take(2, BATCH * P)
        self.gathered = parts.take(U, HID)
        self.shift = sb("shift", [P, TILES + 1, 16])
        self.top = sb("top", [P, TILES + 1, 8])
        self.self_a = sb("self_a", [P, TILES, 8])
        self.self_p = sb("self_p", [P, TILES, 8])
        self.small = sb("small", [P, TILES + 1, 8])
        self.mean = sb("mean", [P, TILES])
        self.var = sb("var", [P, TILES])
        self.dinv = sb("dinv", [P, TILES])
        self.local = sb("local", [P, STEPS])
        self.last = sb("last", [P, STEPS])
        self.src = sb("src", [P, STEPS], i32)
        self.weight = sb("weight", [P, STEPS])
        self.tile_of = sb("tile_of", [1, STEPS], i32)
        self.reset = sb("reset", [GROUP, GROUPS, P])
        self.identity = sb("identity", [P, P])
        self.columns = sb("columns", [P, P])
        self.ones = sb("ones", [P, P])
        self.pick = sb("pick", [P, 2, U // 2], i32)
        self.onehot = sb("onehot", [P, 4 * QUAD, P])
        self.columns_b = sb("columns_b", [P, P], bf16)
        self.maxima = sb("maxima", [P, 3, 8, GROUP], bf16)
        self.shift3 = sb("shift3", [P, TILES + 1, 3, 16], bf16)
        self.identity_b = sb("identity_b", [P, P], bf16)
        self.floor = sb("floor", [P, 8], bf16)
        self.lift = sb("lift", [P, 8], bf16)
        self.group_local = sb("group_local", [P, GROUP])
        self.group_last = sb("group_last", [P, GROUP])
        self.nodes = sb("nodes", [P, 2, QUAD, 16])
        self.logit = sb("logit", [P, 2, QUAD, 8])
        self.logit2 = sb("logit2", [P, 2, QUAD, 8])
        self.below = sb("below", [P, 2, QUAD, 8])
        self.factor = sb("factor", [P, 8])
        self.psum = ctx.enter_context(nc.psum_tensor("psum", [P, 8, 512], fp32))
        self.signals = []

        def signal(name):
            self.signals.append(Signal(nc, name))
            return self.signals[-1]

        self.s_chain = signal("s_chain")
        self.s_loaded = signal("s_loaded")
        self.s_stored = signal("s_stored")
        self.s_const_ready = signal("s_const_ready")
        self.s_copied = signal("s_copied")
        self.s_turned_up = signal("s_turned_up")
        self.s_turned_copied = signal("s_turned_copied")
        self.s_multiplied = signal("s_multiplied")
        self.s_evacuated = signal("s_evacuated")
        self.s_act_turn = signal("s_act_turn")
        self.s_dve_turn = signal("s_dve_turn")
        self.s_indices_ready = signal("s_indices_ready")
        self.s_picked = signal("s_picked")
        self.s_onehot_ready = signal("s_onehot_ready")
        self.s_degree_put = signal("s_degree_put")
        self.s_summed = signal("s_summed")
        self.s_added = signal("s_added")
        self.s_turned_ready = signal("s_turned_ready")
        self.s_expanded = signal("s_expanded")
        self.s_logits_ready = signal("s_logits_ready")
        self.s_probs_ready = signal("s_probs_ready")
        self.s_message_ready = signal("s_message_ready")
        self.s_heads_turned = signal("s_heads_turned")
        self.s_scanned = signal("s_scanned")
        self.s_turned_back = signal("s_turned_back")
        self.s_group_free = signal("s_group_free")
        self.s_arrived = signal("s_arrived")
        self.s_last_ready = signal("s_last_ready")
        self.s_max_summed = signal("s_max_summed")
        self.s_max_added = signal("s_max_added")
        self.s_high = signal("s_high")
        self.s_middle = signal("s_middle")
        self.s_rest = signal("s_rest")
        self.s_split = signal("s_split")
        self.s_below = signal("s_below")
        self.s_top = signal("s_top")
        self.s_factor = signal("s_factor")
        self.s_gate = signal("s_gate")
        self.s_rows = [Signal(nc, f"s_rows_{u}") for u in range(U)]


class Chain:

    def __init__(self, engine, done, turn=None, per_turn=0):
        self.engine, self.done, self.turn, self.per_turn, self.n = engine, done, turn, per_turn, 0

    def link(self, instruction):
        self.start(instruction)
        self.wait()

    def start(self, instruction):
        self.n += 1
        instruction.then_inc(self.done.sem, 1)

    def wait(self):
        before = self.done.at(self.n)
        if self.turn is not None:
            before = self.turn * self.per_turn + before
        self.engine.wait_ge(self.done.sem, before)


def start_stage(m):
    with m.nc.Block() as block:

        @block.sync
        def _(sp):
            for raised in m.signals:
                if raised is not m.s_loaded and raised is not m.s_stored:
                    sp.sem_inc(raised.sem, 1)
                    raised.past(1)


def gate(m, engine):
    engine.sem_inc(m.s_gate.sem, 1)


def spread(vector, *shape):
    return vector.partition_broadcast(P)


def over_tiles(ap, width):
    return ap.unsqueeze(2).broadcast_to([P, TILES, width])


def over_nodes(row, width, tiles=TILES):
    return row.unsqueeze(1).broadcast_to([P, tiles, width])


def by_head(ap, heads):
    return ap.rearrange("p t (h c) -> p t h c", h=heads)


def load_stage(m, w, params, x):
    nc = m.nc
    count_dst = m.gathered[0:COUNT_ROWS, 0:4, 0:HID].rearrange("p a b -> p (a b)")[:, 0:COUNT_COLS].bitcast(i32)
    pad = EPAD - E
    with nc.Block() as block:

        @block.sync
        def _(sp):
            n = 0
            full = (TILES - 1) * P
            sp.wait_ge(m.s_const_ready.sem, m.s_const_ready.at(2))
            sp.dma_start(m.x[:, 0:TILES - 1, :], x[0:full, :].rearrange("(t p) d -> p t d", p=P)).then_inc(m.s_loaded.sem, 16)
            sp.dma_start(m.x[0:N - full, TILES - 1, :], x[full:N, :]).then_inc(m.s_loaded.sem, 16)
            sp.dma_start(count_dst, w["dst"].rearrange("(p c) -> p c", c=COUNT_COLS)).then_inc(m.s_loaded.sem, 16)
            n += 3
            whole = RUNS - 1
            for runs, name in ((m.run_dst, "dst"), (m.run_src, "src"), (m.run_weight, "edge_weight")):
                sp.dma_start(runs[0:whole, :], w[name][0:whole * P].rearrange("(r e) -> r e", e=P)).then_inc(m.s_loaded.sem, 16)
                sp.dma_start(runs[whole:RUNS, 0:P - pad], w[name][whole * P:E].rearrange("(r e) -> r e", r=1)).then_inc(m.s_loaded.sem, 16)
                n += 2
            for runs, row in ((m.run_dst, 0), (m.run_src, 1), (m.run_weight, 1)):
                source = m.pick_pad[0:1, row, 0:pad]
                if runs is m.run_weight:
                    source = source.bitcast(fp32)
                sp.dma_start(runs[whole:RUNS, P - pad:P], source).then_inc(m.s_loaded.sem, 16)
                n += 1
            for tile, source in params:
                sp.dma_start(tile, source).then_inc(m.s_loaded.sem, 16)
                n += 1
            sp.wait_ge(m.s_loaded.sem, m.s_loaded.at(16 * n))
            m.s_loaded.past(16 * n)

        @block.vector
        def _(dve):
            nc.vector.memset(m.pick_pad[0:1, 0, :], -1)
            nc.vector.memset(m.pick_pad[0:1, 1, :], 0).then_inc(m.s_const_ready.sem, 1)
            nc.vector.memset(m.ones[:, :], 1.0)
            nc.vector.memset(m.x[:, TILES - 1, :], 0.0).then_inc(m.s_const_ready.sem, 1)

        @block.gpsimd
        def _(pool):
            nc.gpsimd.memset(m.identity[:, :], 0.0).then_inc(m.s_copied.sem, 1)
            pool.wait_ge(m.s_copied.sem, m.s_copied.at(1))
            nc.gpsimd.affine_select(out=m.identity[:, :], in_=m.identity[:, :], compare_op=ALU.not_equal, fill=1.0,
                                    base=0, pattern=[[-1, P]], channel_multiplier=1)
            nc.gpsimd.iota(m.columns_i[:, :], pattern=[[1, P]], base=0, channel_multiplier=0)
            nc.gpsimd.iota(m.step_number_i[:, :], pattern=[[GROUP, GROUPS]], base=0, channel_multiplier=1)

    m.s_const_ready.past(2)
    m.s_copied.past(1)
    return count_dst


def prepare_stage(m, count_dst):
    nc = m.nc
    T1 = TILES + 1
    dstf = m.tmp[0:COUNT_ROWS, 0:7, :].rearrange("p a b -> p (a b)")[:, 0:COUNT_COLS]
    junk = m.tmp[0:COUNT_ROWS, 7:14, :].rearrange("p a b -> p (a b)")[:, 0:COUNT_COLS]
    at = iter(range(14, TILES))

    def scratch(width, dt=fp32):
        s = m.tmp[:, next(at), 0:width]
        return s if dt is fp32 else s.bitcast(dt)

    bounds, below = scratch(T1), scratch(T1)
    start, start_i, first = scratch(T1), scratch(T1, i32), scratch(TILES)
    end_i, final, filled, length = scratch(TILES, i32), scratch(TILES), scratch(TILES), scratch(TILES)
    upto, lead, number = scratch(TILES), scratch(TILES), scratch(TILES)
    step = m.step_number
    tile = scratch(GROUPS)[0:GROUP, :]
    tile_i = scratch(GROUPS, i32)[0:GROUP, :]
    run = scratch(GROUPS)[0:GROUP, :]
    run_i = scratch(GROUPS, i32)[0:GROUP, :]
    tile128 = scratch(GROUPS)[0:GROUP, :]
    match = m.match
    row_i = {name: rows.rearrange("p (g e) -> p g e", g=GROUPS) for name, rows in m.row_i.items()}
    row_f = m.prep_float
    GT = [GROUP, GROUPS, TILES]
    GP = [GROUP, GROUPS, P]

    with nc.Block() as block:

        @block.vector
        def _(dve):
            c = Chain(dve, m.s_chain)
            c.link(nc.vector.tensor_copy(m.columns[:, :], m.columns_i[:, :]))
            c.link(nc.vector.tensor_copy(m.columns_b[:, :], m.columns_i[:, :]))
            c.link(nc.vector.tensor_copy(m.step_number[:, :], m.step_number_i[:, :]))
            c.link(nc.vector.tensor_copy(dstf, count_dst))
            c.link(nc.vector.tensor_scalar(bounds, m.columns[:, 0:T1], float(P), None, ALU.mult))
            c.link(nc.vector.tensor_copy(number, m.columns[:, 0:TILES]))
            c.link(nc.vector.memset(below, 0.0))
            with dve.Fori(0, T1) as t:
                count = Chain(dve, m.s_dve_turn, t, 1)
                count.link(nc.vector.tensor_scalar(junk, dstf, bounds[0:COUNT_ROWS, bass.ds(t, 1)], 0.0, ALU.is_lt, ALU.add,
                                                   accum_out=below[0:COUNT_ROWS, bass.ds(t, 1)]))
            nc.vector.tensor_copy(number, m.columns[:, 0:TILES]).then_inc(m.s_copied.sem, 1)
            dve.wait_ge(m.s_multiplied.sem, m.s_multiplied.at(1))
            c.link(nc.vector.tensor_copy(start, m.psum[:, 0, 0:T1]))
            c.link(nc.vector.tensor_copy(start_i, start))
            c.link(nc.vector.tensor_scalar(start_i, start_i, 7, None, ALU.arith_shift_right))
            c.link(nc.vector.tensor_copy(first, start_i[:, 0:TILES]))
            c.link(nc.vector.tensor_scalar(final, start[:, 1:T1], -1.0, None, ALU.add))
            c.link(nc.vector.tensor_copy(end_i, final))
            c.link(nc.vector.tensor_scalar(end_i, end_i, 7, None, ALU.arith_shift_right))
            c.link(nc.vector.tensor_copy(final, end_i))
            c.link(nc.vector.tensor_tensor(filled, start[:, 1:T1], start[:, 0:TILES], ALU.is_gt))
            c.link(nc.vector.tensor_tensor(length, final, first, ALU.subtract))
            c.link(nc.vector.tensor_scalar(length, length, 1.0, None, ALU.add))
            c.link(nc.vector.tensor_tensor(length, length, filled, ALU.mult))
            c.link(nc.vector.memset(lead, 0.0))
            c.link(nc.vector.tensor_tensor_scan(upto, length, lead, 0.0, ALU.add, ALU.add))
            c.link(nc.vector.tensor_tensor(lead, length, upto, ALU.subtract))
            c.link(nc.vector.tensor_tensor(lead, lead, first, ALU.add))
            steps3 = step[0:GROUP, :].unsqueeze(2).broadcast_to(GT)
            c.link(nc.vector.tensor_tensor(match, upto[0:GROUP, :].unsqueeze(1).broadcast_to(GT), steps3, ALU.is_le))
            c.link(nc.vector.tensor_reduce(tile, match, AX.X, ALU.add))
            c.link(nc.vector.tensor_tensor(match, number[0:GROUP, :].unsqueeze(1).broadcast_to(GT),
                                           tile.unsqueeze(2).broadcast_to(GT), ALU.is_equal))
            c.link(nc.vector.tensor_tensor(match, match, lead[0:GROUP, :].unsqueeze(1).broadcast_to(GT), ALU.mult))
            c.link(nc.vector.tensor_reduce(run, match, AX.X, ALU.add))
            c.link(nc.vector.tensor_tensor(run, run, step[0:GROUP, :], ALU.add))
            c.link(nc.vector.tensor_scalar(run, run, float(RUNS - 1), None, ALU.min))
            c.link(nc.vector.tensor_copy(run_i, run))
            c.link(nc.vector.tensor_copy(tile_i, tile))
            nc.vector.tensor_scalar(tile128, tile, float(P), None, ALU.mult).then_inc(m.s_indices_ready.sem, 1)
            for u in range(U):
                dve.wait_ge(m.s_rows[u].sem, m.s_rows[u].at(16 * len(range(3 * GROUPS)[u::U])))
            c.link(nc.vector.tensor_copy(row_f[:, 0], row_i["dst"]))
            c.link(nc.vector.tensor_copy(row_f[:, 1], row_i["src"]))
            c.link(nc.vector.tensor_copy(row_f[:, 2], row_i["weight"].bitcast(fp32)))
            c.link(nc.vector.memset(m.reset[:, :, 0:1], 0.0))
            c.link(nc.vector.tensor_tensor(m.reset[:, :, 1:P], row_f[:, 0, :, 1:P], row_f[:, 0, :, 0:P - 1], ALU.is_equal))
            c.link(nc.vector.memset(row_f[:, 3], 1.0))
            c.link(nc.vector.tensor_scalar(row_f[:, 3, :, 0:P - 1], m.reset[:, :, 1:P], -1.0, 1.0, ALU.mult, ALU.add))
            c.link(nc.vector.tensor_scalar(m.reset[:, :, :], m.reset[:, :, :], -1.0, BIG, ALU.add, ALU.mult))
            c.link(nc.vector.tensor_tensor(row_f[:, 0], row_f[:, 0], tile128.unsqueeze(2).broadcast_to(GP), ALU.subtract))
            c.link(nc.vector.tensor_scalar(row_f[:, 4], row_f[:, 0], float(2 * NPAD), None, ALU.add))
            c.link(nc.vector.tensor_tensor(row_f[:, 3], row_f[:, 3], row_f[:, 4], ALU.mult))
            nc.vector.tensor_scalar(row_f[:, 3], row_f[:, 3], float(-2 * NPAD), None, ALU.add).then_inc(m.s_copied.sem, 1)
            for a, target in enumerate((m.local, m.src, m.weight, m.last)):
                dve.wait_ge(m.s_turned_up.sem, m.s_turned_up.at(a + 1))
                nc.vector.tensor_copy(target[:, :].rearrange("p (a b) -> p a b", a=2),
                                      m.psum[:, 2 * a:2 * a + 2, 0:STEPS // 2]).then_inc(m.s_evacuated.sem, 1)
            nc.vector.memset(m.acc[:, :, :], 0.0)
            m.s_chain.past(c.n)

        @block.tensor
        def _(pe):
            pe.wait_ge(m.s_copied.sem, m.s_copied.at(1))
            nc.tensor.matmul(m.psum[:, 0, 0:T1], m.ones[:, :], below[:, :], start=True, stop=True).then_inc(m.s_multiplied.sem, 1)
            pe.wait_ge(m.s_copied.sem, m.s_copied.at(2))
            for a in range(4):
                for g in range(GROUPS):
                    at = g % (GROUPS // 2) * GROUP
                    turned = nc.tensor.transpose(m.psum[:, 2 * a + g // (GROUPS // 2), at:at + GROUP], row_f[:, a, g, :],
                                                 m.identity[0:GROUP, 0:GROUP])
                turned.then_inc(m.s_turned_up.sem, 1)

        @block.gpsimd
        def _(pool):
            pool.wait_ge(m.s_indices_ready.sem, m.s_indices_ready.at(1))
            for g in range(GROUPS):
                for a, (name, runs) in enumerate((("dst", m.run_dst), ("src", m.run_src), ("weight", m.run_weight_i))):
                    nc.gpsimd.indirect_dma_start(
                        row_i[name][:, g, :], None, runs, bass.IndirectOffsetOnAxis(ap=run_i[:, g:g + 1], axis=0)
                    ).then_inc(m.s_rows[(3 * g + a) % U].sem, 16)

        @block.sync
        def _(sp):
            sp.wait_ge(m.s_indices_ready.sem, m.s_indices_ready.at(1))
            with nc.allow_non_contiguous_dma("a small table"):
                sp.dma_start(m.tile_list.rearrange("o (g p) -> (o p) g", p=GROUP), tile_i,
                             allow_slow_non_contiguous=True).then_inc(m.s_stored.sem, 16)
            sp.wait_ge(m.s_stored.sem, m.s_stored.at(16))
            sp.dma_start(m.tile_of[:, :], m.tile_list).then_inc(m.s_loaded.sem, 16)
            sp.wait_ge(m.s_loaded.sem, m.s_loaded.at(16))

    m.s_dve_turn.past(T1)
    m.s_copied.past(2)
    m.s_multiplied.past(1)
    m.s_indices_ready.past(1)
    for u in range(U):
        m.s_rows[u].past(16 * len(range(3 * GROUPS)[u::U]))
    m.s_turned_up.past(4)
    m.s_evacuated.past(4)
    m.s_stored.past(16)
    m.s_loaded.past(16)


def dense_stage(m, source, blocks, weight, width, target, bias=None, relu=False):
    nc = m.nc
    turned = m.psum[:, 0:4, :].rearrange("p b c -> p (b c)")
    product = m.psum[:, 4:8, :].rearrange("p b c -> p (b c)")

    with nc.Block() as block:

        @block.vector
        def _(dve):
            with dve.Fori(0, BATCHES) as b:
                if True:
                    dve.wait_ge(m.s_turned_up.sem, b + m.s_turned_up.at(0))
                    nc.vector.tensor_scalar(m.stage[:, :, 0:blocks * P], source[:, bass.ds(b * BATCH, BATCH), 0:blocks * P], 1.0, None, ALU.mult).then_inc(m.s_copied.sem, 1)
                    dve.wait_ge(m.s_turned_up.sem, b + m.s_turned_up.at(1))
                    dve.wait_ge(m.s_multiplied.sem, b + m.s_multiplied.at(0))
                    nc.vector.tensor_copy(m.stageT[:, 0:blocks, :], turned[:, 0:blocks * BATCH * P].rearrange("p (k n) -> p k n", k=blocks)).then_inc(m.s_turned_copied.sem, 1)
                    dve.wait_ge(m.s_multiplied.sem, b + m.s_multiplied.at(1))
                    out = target[:, bass.ds(b * BATCH, BATCH), 0:width]
                    got = product[:, 0:BATCH * width].rearrange("p (t n) -> p t n", n=width)
                    if bias is None:
                        nc.vector.tensor_scalar(out, got, 1.0, None, ALU.mult).then_inc(m.s_evacuated.sem, 1)
                    else:
                        nc.vector.tensor_tensor(out, got, over_nodes(bias, width, BATCH), ALU.add).then_inc(m.s_evacuated.sem, 1)
                    if relu:
                        dve.wait_ge(m.s_evacuated.sem, b + m.s_evacuated.at(1))
                        nc.vector.tensor_scalar(out, out, 0.0, None, ALU.max)

        @block.tensor
        def _(pe):
            with pe.Fori(0, BATCHES) as b:
                pe.wait_ge(m.s_copied.sem, b + m.s_copied.at(1))
                for k in range(blocks):
                    for t in range(BATCH):
                        up = nc.tensor.transpose(turned[:, (k * BATCH + t) * P:(k * BATCH + t + 1) * P],
                                                 m.stage[:, t, k * P:(k + 1) * P], m.identity[:, :])
                up.then_inc(m.s_turned_up.sem, 1)
                pe.wait_ge(m.s_turned_copied.sem, b + m.s_turned_copied.at(1))
                pe.wait_ge(m.s_evacuated.sem, b + m.s_evacuated.at(0))
                for t in range(BATCH):
                    for k in range(blocks):
                        mm = nc.tensor.matmul(product[:, t * width:(t + 1) * width], m.stageT[:, k, t * P:(t + 1) * P],
                                              weight[:, k, 0:width], start=(k == 0), stop=(k == blocks - 1))
                mm.then_inc(m.s_multiplied.sem, 1)

    for s in (m.s_copied, m.s_turned_up, m.s_turned_copied, m.s_multiplied, m.s_evacuated):
        s.past(BATCHES)


def store_stage(m, stores):
    nc = m.nc
    with nc.Block() as block:

        @block.sync
        def _(sp):
            for target, source in stores:
                sp.dma_start(target.rearrange("(t p) d -> p t d", p=P), source).then_inc(m.s_stored.sem, 16)
            sp.wait_ge(m.s_stored.sem, m.s_stored.at(16 * len(stores)))

    m.s_stored.past(16 * len(stores))


def pool_gathers(m, pool, table, width):
    nc = m.nc
    half = U // 2
    with pool.Fori(0, TURNS) as i:
        for u in range(U):
            if u % half == 0:
                h = u // half
                for v in range(u, u + half):
                    pool.wait_ge(m.s_rows[v].sem, i * 16 + m.s_rows[v].at(0))
                nc.gpsimd.tensor_copy(m.pick[:, h, :], m.src[:, bass.ds(i * U + u, half)]).then_inc(m.s_picked.sem, 1)
                pool.wait_ge(m.s_picked.sem, i * 2 + m.s_picked.at(h + 1))
            pool.wait_ge(m.s_summed.sem, i * U + m.s_summed.at(u + 1))
            gate(m, pool)
            nc.gpsimd.indirect_dma_start(
                m.gathered[:, u, 0:width], None, table,
                bass.IndirectOffsetOnAxis(ap=m.pick[:, u // half, u % half:u % half + 1], axis=0)
            ).then_inc(m.s_rows[u].sem, 16)


def load_tiles(m, start, count=U, engines=DVE_ONLY):
    _, tiles = m.nc.values_load_multi_w_load_instructions(
        m.tile_of[0:1, bass.ds(start, count)], engines=engines, min_val=0, max_val=TILES,
        skip_runtime_bounds_check_because="prepare_stage counts the tiles that end before a step: 0 to TILES")
    return tiles


def tile_row(ap, tile, width):
    return ap[:, bass.ds(tile, 1), 0:width].rearrange("p o c -> p (o c)")


def sum_stage(m, table, width, weighted=False, degree=False):
    nc = m.nc
    S, L = 4, 3
    total = width + degree

    with nc.Block() as block:

        @block.gpsimd
        def _(pool):
            pool_gathers(m, pool, table, width)

        @block.vector
        def _(dve):
            dve.sem_inc(m.s_added.sem, S)
            with dve.Fori(0, TURNS) as i:
                tiles = load_tiles(m, i * U)
                for j in range(U + L):
                    if j < U:
                        dve.wait_ge(m.s_summed.sem, i * U + m.s_summed.at(U + j - S + 1))
                        one = (m.local[:, bass.ds(i * U + j, 1)], ALU.is_equal)
                        if weighted:
                            nc.vector.tensor_scalar(m.onehot[:, j % S, :], m.columns[:, :], one[0],
                                                    m.weight[:, bass.ds(i * U + j, 1)], one[1], ALU.mult).then_inc(m.s_onehot_ready.sem, 1)
                        else:
                            nc.vector.tensor_scalar(m.onehot[:, j % S, :], m.columns[:, :], one[0], None, one[1]).then_inc(m.s_onehot_ready.sem, 1)
                    if j >= L:
                        k = j - L
                        dve.wait_ge(m.s_summed.sem, i * U + m.s_summed.at(U + k + 1))
                        dve.wait_ge(m.s_added.sem, i * U + m.s_added.at(S + k))
                        row = tile_row(m.acc, tiles[k], total)
                        nc.vector.tensor_tensor(row, row, m.psum[:, k % S, 0:total], ALU.add).then_inc(m.s_added.sem, 1)

        if degree:
            @block.scalar
            def _(act):
                with act.Fori(0, TURNS) as i:
                    for u in range(U):
                        act.wait_ge(m.s_summed.sem, i * U + m.s_summed.at(u + 1))
                        nc.scalar.copy(m.gathered[:, u, width:width + 1], m.weight[:, bass.ds(i * U + u, 1)]).then_inc(m.s_degree_put.sem, 1)

        @block.tensor
        def _(pe):
            pe.sem_inc(m.s_summed.sem, U)
            with pe.Fori(0, TURNS) as i:
                for u in range(U):
                    pe.wait_ge(m.s_onehot_ready.sem, i * U + m.s_onehot_ready.at(u + 1))
                    pe.wait_ge(m.s_rows[u].sem, i * 16 + m.s_rows[u].at(16))
                    if degree:
                        pe.wait_ge(m.s_degree_put.sem, i * U + m.s_degree_put.at(u + 1))
                    pe.wait_ge(m.s_added.sem, i * U + m.s_added.at(u + 1))
                    nc.tensor.matmul(m.psum[:, u % S, 0:total], m.onehot[:, u % S, :], m.gathered[:, u, 0:total],
                                     start=True, stop=True).then_inc(m.s_summed.sem, 1)

    m.s_picked.past(2 * TURNS)
    m.s_summed.past(U + STEPS)
    m.s_added.past(S + STEPS)
    m.s_onehot_ready.past(STEPS)
    if degree:
        m.s_degree_put.past(STEPS)
    for s in m.s_rows:
        s.past(16 * TURNS)


def attention_stage(m, table, heads):
    nc = m.nc
    H = heads
    W = D + H
    C = D // H
    SLOTS = 4
    ROWS = U // 2
    LOGITS, MESSAGE, ADD = 1, 2, 3
    TAKE = 2
    LINKS = 6 + 3 * QUADS
    arrived = m.arrived[:, :, 0:H]
    scanned = m.psum[:, 6, 0:H * GROUP].rearrange("p (h k) -> p h k", h=H)
    rest = m.rest[:, 0:H, :]

    def columns(bank, width):
        return m.psum[:, bank, 0:QUAD * SUM_ROW].rearrange("p (j n) -> p j n", n=SUM_ROW)[:, :, 0:width]

    def expanded(bank):
        return m.psum[:, bank, 0:QUAD * 6 * H].rearrange("p (j a c) -> p j a c", j=QUAD, a=3)

    def at(signal, g, per_group, n):
        return g * per_group + signal.at(n)

    def gathers(r):
        return len(range(GROUP)[r::ROWS])

    with nc.Block() as block:

        @block.gpsimd
        def _(pool):
            with pool.Fori(0, GROUPS // 2) as pair:
                for b in range(2):
                    g = pair * 2 + b
                    pool.wait_ge(m.s_group_free.sem, at(m.s_group_free, g, 1, 1))
                    gate(m, pool)
                    nc.gpsimd.tensor_copy(m.pick_group[:, b, :], m.src[:, bass.ds(g * GROUP, GROUP)]).then_inc(m.s_picked.sem, 1)
                    pool.wait_ge(m.s_picked.sem, at(m.s_picked, g, 1, 1))
                    gate(m, pool)
                    for v in range(GROUP):
                        nc.gpsimd.indirect_dma_start(
                            m.wide[:, b, v, 0:W], None, table,
                            bass.IndirectOffsetOnAxis(ap=m.pick_group[:, b, v:v + 1], axis=0)).then_inc(m.s_rows[b * ROWS + v % ROWS].sem, 16)

        @block.scalar
        def _(act):
            act.sem_inc(m.s_turned_copied.sem, 2)
            act.sem_inc(m.s_probs_ready.sem, 2)
            with act.Fori(0, GROUPS // 2) as pair:
                for b in range(2):
                    g = pair * 2 + b
                    for r in range(ROWS):
                        landed = m.s_rows[b * ROWS + r]
                        act.wait_ge(landed.sem, pair * 16 * gathers(r) + landed.at(16 * gathers(r)))
                    act.wait_ge(m.s_heads_turned.sem, at(m.s_heads_turned, g, 1, 0))
                    gate(m, act)
                    nc.scalar.copy(arrived, m.wide[:, b, :, D:W]).then_inc(m.s_arrived.sem, 1)
                    act.wait_ge(m.s_turned_back.sem, at(m.s_turned_back, g, 1, 1))
                    nc.scalar.copy(m.maxima[:, 0, 0:H, :], scanned).then_inc(m.s_high.sem, 1)
                    act.wait_ge(m.s_rest.sem, at(m.s_rest, g, 2, 1))
                    nc.scalar.copy(m.maxima[:, 1, 0:H, :], rest).then_inc(m.s_middle.sem, 1)
                    act.wait_ge(m.s_dve_turn.sem, at(m.s_dve_turn, g, 1, 1))
                    nc.scalar.copy(m.shift3[:, :, 0, H:2 * H], m.shift[:, :, H:2 * H]).then_inc(m.s_high.sem, 1)
                    nc.scalar.activation(m.factor[:, 0:H], m.factor[:, 0:H], ACT.Exp).then_inc(m.s_act_turn.sem, 1)
                    act.wait_ge(m.s_rest.sem, at(m.s_rest, g, 2, 2))
                    nc.scalar.copy(m.shift3[:, :, 1, H:2 * H], m.new_top[:, :, 0:H]).then_inc(m.s_middle.sem, 1)
                    for j in range(QUADS + LOGITS):
                        if j < QUADS:
                            act.wait_ge(m.s_turned_ready.sem, at(m.s_turned_ready, g, QUADS, j + 1))
                            act.wait_ge(m.s_expanded.sem, at(m.s_expanded, g, QUADS, j + 1))
                            nc.scalar.copy(m.turned[:, j % 2, :], m.psum[:, 4 + j % 2, :]).then_inc(m.s_turned_copied.sem, 1)
                        q = j - LOGITS
                        if q >= 0:
                            act.wait_ge(m.s_logits_ready.sem, at(m.s_logits_ready, g, QUADS, 2 + q + 1))
                            act.wait_ge(m.s_summed.sem, at(m.s_summed, g, GROUP, QUAD * (SLOTS + q - 1)))
                            nc.scalar.activation(m.below[:, q % 2, :, 0:H], m.logit[:, q % 2, :, 0:H], ACT.Relu, scale=-1.0).then_inc(m.s_below.sem, 1)
                            act.wait_ge(m.s_below.sem, at(m.s_below, g, QUADS, q + 1))
                            nc.scalar.activation(m.message[:, q % 2, :, D:W], m.below[:, q % 2, :, 0:H], ACT.Exp, scale=-1.0).then_inc(m.s_probs_ready.sem, 1)

        @block.vector
        def _(dve):
            dve.sem_inc(m.s_added.sem, QUAD)
            dve.sem_inc(m.s_logits_ready.sem, 2)
            dve.sem_inc(m.s_max_added.sem, 2)
            dve.sem_inc(m.s_group_free.sem, 2)
            with dve.Fori(0, GROUPS // 2) as pair, dve.Fori(0, 2) as b:
                g = pair * 2 + b
                c = Chain(dve, m.s_chain, g, LINKS)
                c.link(nc.vector.tensor_scalar(m.group_last[:, :], m.last[:, bass.ds(g * GROUP, GROUP)], 1.0, None, ALU.mult))
                c.link(nc.vector.tensor_scalar(m.group_local[:, :], m.local[:, bass.ds(g * GROUP, GROUP)], 1.0, None, ALU.mult))
                dve.wait_ge(m.s_heads_turned.sem, at(m.s_heads_turned, g, 1, 1))
                for h in range(H):
                    scan = nc.vector.tensor_tensor_scan(
                        m.scans[:, h, :], m.reset[:, bass.ds(g, 1), :].rearrange("p o e -> p (o e)"),
                        m.psum[0:GROUP, 4 + h // 4, h % 4 * P:(h % 4 + 1) * P], -BIG, ALU.add, ALU.max)
                scan.then_inc(m.s_scanned.sem, 1)
                dve.wait_ge(m.s_high.sem, at(m.s_high, g, 2, 1))
                nc.vector.tensor_tensor(rest, scanned, m.maxima[:, 0, 0:H, :], ALU.subtract).then_inc(m.s_rest.sem, 1)
                dve.wait_ge(m.s_middle.sem, at(m.s_middle, g, 2, 1))
                nc.vector.tensor_tensor(m.maxima[:, 2, 0:H, :], rest, m.maxima[:, 1, 0:H, :], ALU.subtract).then_inc(m.s_split.sem, 1)
                for j in range(QUADS + TAKE):
                    q = j - TAKE
                    if j < QUADS:
                        dve.wait_ge(m.s_max_summed.sem, at(m.s_max_summed, g, QUADS, j + 1))
                    if q >= 0:
                        if q * QUAD % MOST == 0:
                            tiles = load_tiles(m, g * GROUP + q * QUAD, min(MOST, GROUP - q * QUAD))
                        dve.wait_ge(m.s_max_summed.sem, at(m.s_max_summed, g, QUADS, SLOTS + q + 1))
                    for u in range(QUAD):
                        if q >= 0:
                            row = tile_row(m.top, tiles[(q * QUAD + u) % MOST], H)
                            dve.wait_ge(m.s_top.sem, at(m.s_top, g, GROUP, q * QUAD + u))
                            nc.vector.tensor_tensor(row, columns(q % 2, H)[:, u, :], row, ALU.max).then_inc(m.s_top.sem, 1)
                        if j < QUADS:
                            one = nc.vector.tensor_scalar(m.lastone[:, j % SLOTS * QUAD + u, :], m.columns_b[:, :],
                                                          m.group_last[:, j * QUAD + u:j * QUAD + u + 1], None, ALU.is_equal)
                            if u == QUAD - 1:
                                one.then_inc(m.s_last_ready.sem, 1)
                    if q >= 0:
                        dve.wait_ge(m.s_top.sem, at(m.s_top, g, GROUP, (q + 1) * QUAD))
                        dve.sem_inc(m.s_max_added.sem, 1)
                tiles = load_tiles(m, g * GROUP, 1)
                c.link(nc.vector.tensor_tensor(m.new_top[:, :, 0:H], m.top[:, :, 0:H], m.shift[:, :, 0:H], ALU.add))
                c.link(nc.vector.scalar_tensor_tensor(m.new_top[:, :, 0:H], m.new_top[:, :, 0:H], SLOPE, m.new_top[:, :, 0:H],
                                                      ALU.mult, ALU.max))
                old = m.shift[:, bass.ds(tiles[0], 1), H:2 * H].rearrange("p o h -> p (o h)")
                nc.vector.tensor_tensor(m.factor[:, 0:H], old, tile_row(m.new_top, tiles[0], H), ALU.subtract).then_inc(m.s_factor.sem, 1)
                dve.wait_ge(m.s_factor.sem, at(m.s_factor, g, 1, 1))
                nc.vector.tensor_copy(m.shift[:, :, H:2 * H], m.new_top[:, :, 0:H]).then_inc(m.s_dve_turn.sem, 1)
                dve.wait_ge(m.s_dve_turn.sem, at(m.s_dve_turn, g, 1, 1))
                dve.wait_ge(m.s_high.sem, at(m.s_high, g, 2, 2))
                nc.vector.tensor_tensor(m.new_top[:, :, 0:H], m.shift[:, :, H:2 * H], m.shift3[:, :, 0, H:2 * H], ALU.subtract).then_inc(m.s_rest.sem, 1)
                dve.wait_ge(m.s_act_turn.sem, at(m.s_act_turn, g, 1, 1))
                dve.wait_ge(m.s_added.sem, at(m.s_added, g, GROUP, QUAD))
                row = tile_row(m.sums, tiles[0], D).rearrange("p (h c) -> p h c", h=H)
                c.link(nc.vector.tensor_tensor(row, row, m.factor[:, 0:H].unsqueeze(2).broadcast_to([P, H, C]), ALU.mult))
                row = m.sums[:, bass.ds(tiles[0], 1), D:W].rearrange("p o c -> p (o c)")
                c.link(nc.vector.tensor_tensor(row, row, m.factor[:, 0:H], ALU.mult))
                dve.wait_ge(m.s_middle.sem, at(m.s_middle, g, 2, 2))
                nc.vector.tensor_tensor(m.shift3[:, :, 2, H:2 * H], m.new_top[:, :, 0:H], m.shift3[:, :, 1, H:2 * H], ALU.subtract).then_inc(m.s_split.sem, 1)

                for j in range(QUADS + ADD):
                    q = j - ADD
                    if j < QUADS:
                        dve.wait_ge(m.s_summed.sem, at(m.s_summed, g, GROUP, QUAD * (j + 1)))
                    if q >= 0 and q * QUAD % MOST == 0:
                        tiles = load_tiles(m, g * GROUP + q * QUAD, min(MOST, GROUP - q * QUAD))
                    for u in range(QUAD):
                        if j < QUADS:
                            one = nc.vector.tensor_scalar(m.onehot[:, j % SLOTS * QUAD + u, :], m.columns[:, :],
                                                          m.group_local[:, j * QUAD + u:j * QUAD + u + 1], None, ALU.is_equal)
                            if u == QUAD - 1:
                                one.then_inc(m.s_onehot_ready.sem, 1)
                        if q >= 0:
                            k = q * QUAD + u
                            dve.wait_ge(m.s_summed.sem, at(m.s_summed, g, GROUP, SLOTS * QUAD + k + 1))
                            dve.wait_ge(m.s_added.sem, at(m.s_added, g, GROUP, QUAD + k))
                            row = tile_row(m.sums, tiles[k % MOST], W)
                            nc.vector.tensor_tensor(row, row, m.psum[:, u, 0:W], ALU.add).then_inc(m.s_added.sem, 1)
                    q = j - LOGITS
                    if 0 <= q < QUADS:
                        logit, logit2 = m.logit[:, q % 2, :, 0:H], m.logit2[:, q % 2, :, 0:H]
                        nodes = m.nodes[:, q % 2, :, 0:2 * H]
                        a_src = m.wide[:, bass.ds(b, 1), q * QUAD:(q + 1) * QUAD, D:W].rearrange("p o s h -> p (o s) h")
                        dve.wait_ge(m.s_expanded.sem, at(m.s_expanded, g, QUADS, 2 + q + 1))
                        dve.wait_ge(m.s_probs_ready.sem, at(m.s_probs_ready, g, QUADS, q + 1))
                        c.link(nc.vector.tensor_reduce(nodes, expanded(6 + q % 2).rearrange("p j a c -> p j c a"), AX.X, ALU.add))
                        c.link(nc.vector.tensor_tensor(logit, a_src, nodes[:, :, 0:H], ALU.add))
                        c.link(nc.vector.scalar_tensor_tensor(logit2, logit, SLOPE, logit, ALU.mult, ALU.max))
                        nc.vector.tensor_tensor(logit, logit2, nodes[:, :, H:2 * H], ALU.subtract).then_inc(m.s_logits_ready.sem, 1)
                    q = j - MESSAGE
                    if 0 <= q < QUADS:
                        dve.wait_ge(m.s_probs_ready.sem, at(m.s_probs_ready, g, QUADS, 2 + q + 1))
                        rows = m.wide[:, bass.ds(b, 1), q * QUAD:(q + 1) * QUAD, 0:D].rearrange("p o s (h c) -> p (o s) h c", h=H)
                        nc.vector.tensor_tensor(
                            m.message[:, q % 2, :, 0:D].rearrange("p s (h c) -> p s h c", h=H), rows,
                            m.message[:, q % 2, :, D:W].unsqueeze(3).broadcast_to([P, QUAD, H, C]),
                            ALU.mult).then_inc(m.s_message_ready.sem, 1)
                        if q == QUADS - 1:
                            dve.wait_ge(m.s_message_ready.sem, at(m.s_message_ready, g, QUADS, QUADS))
                            dve.sem_inc(m.s_group_free.sem, 1)
                assert c.n == LINKS, c.n

        @block.tensor
        def _(pe):
            pe.sem_inc(m.s_summed.sem, SLOTS * QUAD)
            pe.sem_inc(m.s_expanded.sem, 2)
            pe.sem_inc(m.s_max_summed.sem, SLOTS)
            with pe.Fori(0, GROUPS) as g:
                pe.wait_ge(m.s_arrived.sem, at(m.s_arrived, g, 1, 1))
                gate(m, pe)
                for h in range(H):
                    up = nc.tensor.transpose(m.psum[0:GROUP, 4 + h // 4, h % 4 * P:(h % 4 + 1) * P], arrived[:, :, h], m.identity[:, :])
                up.then_inc(m.s_heads_turned.sem, 1)
                pe.wait_ge(m.s_scanned.sem, at(m.s_scanned, g, 1, 1))
                gate(m, pe)
                for h in range(H):
                    back = nc.tensor.transpose(m.psum[:, 6, h * GROUP:(h + 1) * GROUP], m.scans[:, h, :], m.identity[0:GROUP, 0:GROUP])
                back.then_inc(m.s_turned_back.sem, 1)
                pe.wait_ge(m.s_split.sem, at(m.s_split, g, 2, 1))
                for q in range(QUADS):
                    pe.wait_ge(m.s_last_ready.sem, at(m.s_last_ready, g, QUADS, q + 1))
                    pe.wait_ge(m.s_max_added.sem, at(m.s_max_added, g, QUADS, q + 1))
                    for u in range(QUAD):
                        nc.tensor.matmul(columns(q % 2, H)[:, u, :], m.identity_b[:, :], m.floor[:, 0:H], start=True, stop=False)
                        nc.tensor.matmul(columns(q % 2, H)[:, u, :], m.lastone[:, q % SLOTS * QUAD + u, :], m.lift[:, 0:H],
                                         start=False, stop=False)
                        for part in range(3):
                            mm = nc.tensor.matmul(columns(q % 2, H)[:, u, :], m.lastone[:, q % SLOTS * QUAD + u, :],
                                                  m.maxima[:, part, 0:H, q * QUAD + u], start=False, stop=(part == 2))
                    mm.then_inc(m.s_max_summed.sem, 1)
                for j in range(QUADS + MESSAGE):
                    q = j - LOGITS
                    if 0 <= q < QUADS:
                        if q * QUAD % MOST == 0:
                            tiles = load_tiles(m, g * GROUP + q * QUAD, min(MOST, GROUP - q * QUAD), PE_ONLY)
                        pe.wait_ge(m.s_turned_copied.sem, at(m.s_turned_copied, g, QUADS, 2 + q + 1))
                        pe.wait_ge(m.s_logits_ready.sem, at(m.s_logits_ready, g, QUADS, q + 1))
                        if q == 0:
                            pe.wait_ge(m.s_split.sem, at(m.s_split, g, 2, 2))
                        for u in range(QUAD):
                            parts = m.shift3[:, bass.ds(tiles[(q * QUAD + u) % MOST], 1), :, 0:2 * H].rearrange("p o a c -> p (o a) c")
                            mm = nc.tensor.matmul(expanded(6 + q % 2)[:, u], m.turned[:, q % 2, u * P:(u + 1) * P], parts,
                                                  start=True, stop=True)
                        mm.then_inc(m.s_expanded.sem, 1)
                    if j < QUADS:
                        pe.wait_ge(m.s_onehot_ready.sem, at(m.s_onehot_ready, g, QUADS, j + 1))
                        pe.wait_ge(m.s_turned_copied.sem, at(m.s_turned_copied, g, QUADS, j + 1))
                        for u in range(QUAD):
                            up = nc.tensor.transpose(m.psum[:, 4 + j % 2, u * P:(u + 1) * P], m.onehot[:, j % SLOTS * QUAD + u, :], m.identity[:, :])
                        up.then_inc(m.s_turned_ready.sem, 1)
                    q = j - MESSAGE
                    if 0 <= q < QUADS:
                        pe.wait_ge(m.s_message_ready.sem, at(m.s_message_ready, g, QUADS, q + 1))
                        for u in range(QUAD):
                            pe.wait_ge(m.s_added.sem, at(m.s_added, g, GROUP, q * QUAD + u + 1))
                            nc.tensor.matmul(m.psum[:, u, 0:W], m.onehot[:, q % SLOTS * QUAD + u, :], m.message[:, q % 2, u, 0:W],
                                             start=True, stop=True).then_inc(m.s_summed.sem, 1)

    for a, landed in enumerate(m.s_rows):
        landed.past(16 * gathers(a % ROWS) * (GROUPS // 2))
    m.s_picked.past(GROUPS)
    m.s_chain.past(LINKS * GROUPS)
    for s in (m.s_arrived, m.s_heads_turned, m.s_scanned, m.s_turned_back, m.s_factor, m.s_dve_turn, m.s_act_turn):
        s.past(GROUPS)
    for s in (m.s_high, m.s_middle, m.s_rest, m.s_split):
        s.past(2 * GROUPS)
    m.s_top.past(GROUP * GROUPS)
    m.s_group_free.past(2 + GROUPS)
    m.s_summed.past(SLOTS * QUAD + STEPS)
    m.s_added.past(QUAD + STEPS)
    m.s_max_summed.past(SLOTS + QUADS * GROUPS)
    for s in (m.s_max_added, m.s_turned_copied, m.s_expanded, m.s_logits_ready, m.s_probs_ready):
        s.past(2 + QUADS * GROUPS)
    for s in (m.s_below, m.s_last_ready, m.s_onehot_ready, m.s_message_ready, m.s_turned_ready):
        s.past(QUADS * GROUPS)


def head_stage(m, att_src, att_dst, heads, wide):
    nc = m.nc
    H = heads
    h = m.acc[:, 0:TILES, 0:D]
    a_src, a_dst = m.acc[:, 0:TILES, D:D + H], m.shift[:, 0:TILES, 0:H]
    maximum, small = m.shift[:, 0:TILES, H:2 * H], m.small[:, 0:TILES, 0:H]
    with nc.Block() as block:

        @block.vector
        def _(dve):
            c = Chain(dve, m.s_chain)
            c.link(nc.vector.tensor_tensor(m.tmp[:, :, :], h, over_nodes(att_src, D), ALU.mult))
            nc.vector.tensor_reduce(a_src, by_head(m.tmp[:, :, :], H), AX.X, ALU.add).then_inc(m.s_dve_turn.sem, 1)
            dve.wait_ge(m.s_dve_turn.sem, m.s_dve_turn.at(1))
            c.link(nc.vector.tensor_tensor(m.tmp[:, :, :], h, over_nodes(att_dst, D), ALU.mult))
            c.link(nc.vector.memset(m.shift[:, :, :], 0.0))
            c.link(nc.vector.tensor_reduce(a_dst, by_head(m.tmp[:, :, :], H), AX.X, ALU.add))
            c.link(nc.vector.memset(m.top[:, :, :], 0.0))
            c.link(nc.vector.tensor_copy(m.top[:, 0:TILES, 0:H], a_src))
            c.link(nc.vector.tensor_copy(m.self_a[:, :, 0:H], a_src))
            c.link(nc.vector.tensor_copy(m.identity_b[:, :], m.identity[:, :]))
            c.link(nc.vector.memset(m.floor[:, :], -BIG))
            c.link(nc.vector.memset(m.lift[:, :], BIG))
            a_dst_all = m.shift[:, :, 0:H]
            c.link(nc.vector.tensor_copy(m.shift3[:, :, 0, 0:H], a_dst_all))
            c.link(nc.vector.tensor_tensor(m.small[:, :, 0:H], a_dst_all, m.shift3[:, :, 0, 0:H], ALU.subtract))
            c.link(nc.vector.tensor_copy(m.shift3[:, :, 1, 0:H], m.small[:, :, 0:H]))
            c.link(nc.vector.tensor_tensor(m.shift3[:, :, 2, 0:H], m.small[:, :, 0:H], m.shift3[:, :, 1, 0:H], ALU.subtract))
            c.link(nc.vector.tensor_tensor(small, a_src, a_dst, ALU.add))
            c.link(nc.vector.scalar_tensor_tensor(maximum, small, SLOPE, small, ALU.mult, ALU.max))
            dve.wait_ge(m.s_stored.sem, m.s_stored.at(16))
            nc.vector.memset(m.sums[:, :, :], 0.0)
            m.n = c.n

        @block.sync
        def _(sp):
            sp.wait_ge(m.s_dve_turn.sem, m.s_dve_turn.at(1))
            sp.dma_start(wide.rearrange("(t p) d -> p t d", p=P), m.acc[:, 0:TILES, 0:D + H]).then_inc(m.s_stored.sem, 16)
            sp.wait_ge(m.s_stored.sem, m.s_stored.at(16))

    m.s_chain.past(m.n)
    m.s_dve_turn.past(1)
    m.s_stored.past(16)


def loop_stage(m, heads, wide):
    nc = m.nc
    H = heads
    a_dst, maximum = m.shift[:, 0:TILES, 0:H], m.shift[:, 0:TILES, H:2 * H]
    small, p = m.small[:, 0:TILES, 0:H], m.self_p[:, :, 0:H]
    h = m.tmp[:, :, :]
    with nc.Block() as block:

        @block.sync
        def _(sp):
            sp.dma_start(h, wide.rearrange("(t p) d -> p t d", p=P)[:, :, 0:D]).then_inc(m.s_loaded.sem, 16)
            sp.wait_ge(m.s_loaded.sem, m.s_loaded.at(16))

        @block.vector
        def _(dve):
            c = Chain(dve, m.s_chain)
            c.link(nc.vector.tensor_tensor(p, m.self_a[:, :, 0:H], a_dst, ALU.add))
            c.link(nc.vector.scalar_tensor_tensor(small, p, SLOPE, p, ALU.mult, ALU.max))
            c.link(nc.vector.tensor_tensor(small, small, maximum, ALU.subtract))
            dve.wait_ge(m.s_act_turn.sem, m.s_act_turn.at(1))
            dve.wait_ge(m.s_loaded.sem, m.s_loaded.at(16))
            c.link(nc.vector.tensor_tensor(m.sums[:, 0:TILES, D:D + H], m.sums[:, 0:TILES, D:D + H], p, ALU.add))
            c.link(nc.vector.tensor_tensor(by_head(h, H), by_head(h, H), p.unsqueeze(3).broadcast_to([P, TILES, H, D // H]), ALU.mult))
            c.link(nc.vector.tensor_tensor(m.sums[:, 0:TILES, 0:D], m.sums[:, 0:TILES, 0:D], h, ALU.add))
            m.n = c.n

        @block.scalar
        def _(act):
            act.wait_ge(m.s_chain.sem, m.s_chain.at(3))
            nc.scalar.activation(p, small, ACT.Exp).then_inc(m.s_act_turn.sem, 1)

    m.s_chain.past(m.n)
    m.s_act_turn.past(1)
    m.s_loaded.past(16)


def divide_heads(m, c, heads, bias):
    nc = m.nc
    H = heads
    z, small, out = m.sums[:, 0:TILES, D:D + H], m.small[:, 0:TILES, 0:H], m.sums[:, 0:TILES, 0:D]
    c.link(nc.vector.tensor_scalar(small, z, SOFTMAX_EPS, None, ALU.add))
    c.link(nc.vector.reciprocal(small, small))
    c.link(nc.vector.tensor_tensor(by_head(out, H), by_head(out, H), small.unsqueeze(3).broadcast_to([P, TILES, H, D // H]), ALU.mult))
    c.link(nc.vector.tensor_tensor(out, out, over_nodes(bias, D), ALU.add))


def center(m, c, dve, value):
    nc = m.nc
    c.link(nc.vector.tensor_reduce(m.mean[:, :], value, AX.X, ALU.add))
    c.link(nc.vector.tensor_scalar(m.mean[:, :], m.mean[:, :], 1.0 / D, None, ALU.mult))
    c.link(nc.vector.tensor_tensor(value, value, over_tiles(m.mean[:, :], D), ALU.subtract))
    c.link(nc.vector.tensor_tensor(m.tmp[:, :, :], value, value, ALU.mult))
    c.link(nc.vector.tensor_reduce(m.var[:, :], m.tmp[:, :, :], AX.X, ALU.add))
    nc.vector.tensor_scalar(m.var[:, :], m.var[:, :], 1.0 / D, LN_EPS, ALU.mult, ALU.add).then_inc(m.s_dve_turn.sem, 1)


def rescale(m, c, dve, value, n):
    nc = m.nc
    dve.wait_ge(m.s_act_turn.sem, m.s_act_turn.at(n))
    c.link(nc.vector.reciprocal(m.mean[:, :], m.var[:, :]))
    c.link(nc.vector.tensor_tensor(value, value, over_tiles(m.mean[:, :], D), ALU.mult))


def root(m, act, n):
    act.wait_ge(m.s_dve_turn.sem, m.s_dve_turn.at(n))
    m.nc.scalar.activation(m.var[:, :], m.var[:, :], ACT.Sqrt).then_inc(m.s_act_turn.sem, 1)


def selu_stage(m, bias):
    nc = m.nc
    out, tmp, x = m.sums[:, 0:TILES, 0:D], m.tmp[:, :, :], m.x[:, :, :]
    with nc.Block() as block:

        @block.vector
        def _(dve):
            c = Chain(dve, m.s_chain)
            divide_heads(m, c, 8, bias)
            nc.vector.tensor_scalar(tmp, out, 0.0, None, ALU.min).then_inc(m.s_dve_turn.sem, 1)
            dve.wait_ge(m.s_act_turn.sem, m.s_act_turn.at(1))
            c.link(nc.vector.tensor_scalar(tmp, tmp, -1.0, SELU_SCALE * SELU_ALPHA, ALU.add, ALU.mult))
            c.link(nc.vector.tensor_tensor(x, x, tmp, ALU.add))
            c.link(nc.vector.tensor_scalar(out, out, 0.0, SELU_SCALE, ALU.max, ALU.mult))
            c.link(nc.vector.tensor_tensor(x, x, out, ALU.add))
            center(m, c, dve, x)
            rescale(m, c, dve, x, 2)
            c.link(nc.vector.tensor_copy(m.acc[:, 0:TILES, 0:D], x))
            c.link(nc.vector.memset(m.acc[:, :, D:D + 1], 1.0))
            m.n = c.n

        @block.scalar
        def _(act):
            act.wait_ge(m.s_dve_turn.sem, m.s_dve_turn.at(1))
            nc.scalar.activation(tmp, tmp, ACT.Exp).then_inc(m.s_act_turn.sem, 1)
            root(m, act, 2)

    m.s_chain.past(m.n)
    m.s_dve_turn.past(2)
    m.s_act_turn.past(2)


def degree_stage(m):
    nc = m.nc
    degree = m.acc[:, 0:TILES, D:D + 1].rearrange("p t o -> p (t o)")
    with nc.Block() as block:

        @block.vector
        def _(dve):
            c = Chain(dve, m.s_chain)
            c.link(nc.vector.tensor_scalar(m.mean[:, :], degree, 0.0, None, ALU.is_gt))
            nc.vector.tensor_scalar(m.var[:, :], degree, 1e-30, None, ALU.max).then_inc(m.s_dve_turn.sem, 1)
            dve.wait_ge(m.s_act_turn.sem, m.s_act_turn.at(1))
            c.link(nc.vector.reciprocal(m.dinv[:, :], m.var[:, :]))
            c.link(nc.vector.tensor_tensor(m.dinv[:, :], m.dinv[:, :], m.mean[:, :], ALU.mult))
            m.n = c.n

        @block.scalar
        def _(act):
            root(m, act, 1)

    m.s_chain.past(m.n)
    m.s_dve_turn.past(1)
    m.s_act_turn.past(1)


def bias_relu_stage(m, bias):
    nc = m.nc
    out = m.acc[:, 0:TILES, 0:D]
    with nc.Block() as block:

        @block.vector
        def _(dve):
            c = Chain(dve, m.s_chain)
            c.link(nc.vector.tensor_tensor(out, out, over_nodes(bias, D), ALU.add))
            c.link(nc.vector.tensor_scalar(out, out, 0.0, None, ALU.max))
            m.n = c.n

    m.s_chain.past(m.n)


def residual_stage(m, value):
    nc = m.nc
    x = m.x[:, :, :]
    with nc.Block() as block:

        @block.vector
        def _(dve):
            c = Chain(dve, m.s_chain)
            c.link(nc.vector.tensor_tensor(x, x, value[:, 0:TILES, 0:D], ALU.add))
            center(m, c, dve, x)
            rescale(m, c, dve, x, 1)
            m.n = c.n

        @block.scalar
        def _(act):
            root(m, act, 1)

    m.s_chain.past(m.n)
    m.s_dve_turn.past(1)
    m.s_act_turn.past(1)


def divide_stage(m, bias):
    nc = m.nc
    with nc.Block() as block:

        @block.vector
        def _(dve):
            c = Chain(dve, m.s_chain)
            divide_heads(m, c, 4, bias)
            m.n = c.n

    m.s_chain.past(m.n)


def skip_norm_stage(m, skip_bias, gain, offset):
    nc = m.nc
    out = m.sums[:, 0:TILES, 0:D]
    with nc.Block() as block:

        @block.vector
        def _(dve):
            c = Chain(dve, m.s_chain)
            c.link(nc.vector.tensor_tensor(out, out, m.tmp[:, :, :], ALU.add))
            c.link(nc.vector.tensor_tensor(out, out, over_nodes(skip_bias, D), ALU.add))
            center(m, c, dve, out)
            rescale(m, c, dve, out, 1)
            c.link(nc.vector.tensor_tensor(out, out, over_nodes(gain, D), ALU.mult))
            c.link(nc.vector.tensor_tensor(out, out, over_nodes(offset, D), ALU.add))
            m.n = c.n

        @block.scalar
        def _(act):
            root(m, act, 1)

    m.s_chain.past(m.n)
    m.s_dve_turn.past(1)
    m.s_act_turn.past(1)


def scale_stage(m, bias=None, relu=False):
    nc = m.nc
    out = m.acc[:, 0:TILES, 0:D]
    with nc.Block() as block:

        @block.vector
        def _(dve):
            c = Chain(dve, m.s_chain)
            c.link(nc.vector.tensor_tensor(out, out, over_tiles(m.dinv[:, :], D), ALU.mult))
            if bias is not None:
                c.link(nc.vector.tensor_tensor(out, out, over_nodes(bias, D), ALU.add))
            if relu:
                c.link(nc.vector.tensor_scalar(out, out, 0.0, None, ALU.max))
            m.n = c.n

    m.s_chain.past(m.n)


def output_stage(m, out):
    nc = m.nc
    full = (TILES - 1) * P
    with nc.Block() as block:

        @block.sync
        def _(sp):
            sp.dma_start(out[0:full, :].rearrange("(t p) d -> p t d", p=P), m.x[:, 0:TILES - 1, :]).then_inc(m.s_stored.sem, 16)
            sp.dma_start(out[full:N, :], m.x[0:N - full, TILES - 1, :]).then_inc(m.s_stored.sem, 16)
            sp.wait_ge(m.s_stored.sem, m.s_stored.at(32))

    m.s_stored.past(32)


def build(nc, w, out):
    with ExitStack() as ctx:
        m = Memory(nc, ctx)

        def sb(name, shape, dt=fp32):
            return ctx.enter_context(nc.sbuf_tensor(name, shape, dt))

        m.run_weight_i = m.run_weight.bitcast(i32)
        m.pick_pad = sb("pick_pad", [1, 2, P], i32)
        m.columns_i = sb("columns_i", [P, P], i32)
        m.step_number_i = sb("step_number_i", [P, GROUPS], i32)
        m.step_number = sb("step_number", [P, GROUPS])
        m.pick_group = sb("pick_group", [P, 2, GROUP], i32)
        flat = m.acc_flat
        size = GROUPS * P
        m.prep_float = flat[0:GROUP, 0:5 * size].rearrange("p (a g e) -> p a g e", a=5, g=GROUPS)
        loaned = m.gathered[0:GROUP].rearrange("p a b -> p (a b)")
        m.row_i = {"dst": loaned[:, 0:size].bitcast(i32), "src": loaned[:, size:2 * size].bitcast(i32),
                   "weight": flat[0:GROUP, 5 * size:6 * size].bitcast(i32)}
        m.match = m.stage[0:GROUP].rearrange("p a b -> p (a b)")[:, 0:GROUPS * TILES].rearrange("p (g t) -> p g t", g=GROUPS)

        params = []

        def weight(name, inputs, width):
            blocks = inputs // P
            t = sb("w_" + name, [P, blocks, width])
            params.append((t[:, :, :], w[name].rearrange("(k p) n -> p k n", p=P)))
            return t

        def row(name, width=D):
            t = sb("r_" + name, [P, width])
            source = w[name]
            if len(source.shape) == 2:
                source = source.rearrange("h c -> (h c)")
            params.append((t[:, :], spread(source)))
            return t[:, :]

        g0, g1, g2, g3 = "L0_gnn_", "L1_gnn_", "L2_gnn_", "L3_gnn_"
        W0 = weight(g0 + "W", D, D)
        s0, d0, b0 = row(g0 + "att_src"), row(g0 + "att_dst"), row(g0 + "bias")
        w0a, w0b = weight(g1 + "w0a", D, HID), weight(g1 + "w0b", HID, HID)
        w1a, w1b = weight(g1 + "w1a", HID, HID), weight(g1 + "w1b", HID, HID)
        w2a, w2b = weight(g1 + "w2a", HID, D), weight(g1 + "w2b", D, D)
        b0a, b0b = row(g1 + "b0a", HID), row(g1 + "b0b", HID)
        b1a, b1b = row(g1 + "b1a", HID), row(g1 + "b1b", HID)
        b2a, b2b = row(g1 + "b2a"), row(g1 + "b2b")
        W2, skip = weight(g2 + "W", D, D), weight(g2 + "skip_W", D, D)
        s2, d2 = row(g2 + "att_src"), row(g2 + "att_dst")
        gb, sbias, lng, lnb = row(g2 + "gat_bias"), row(g2 + "skip_b"), row(g2 + "ln_g"), row(g2 + "ln_b")
        G = [weight(g3 + f"W{n}", D, D) for n in (1, 2, 3)]
        gbias = [row(g3 + f"b{n}") for n in (1, 2, 3)]

        start_stage(m)
        count_dst = load_stage(m, w, params, w["x"])
        prepare_stage(m, count_dst)

        dense_stage(m, m.x, 1, W0, D, m.acc)
        head_stage(m, s0, d0, 8, m.rows[136])
        attention_stage(m, m.rows[136], 8)
        loop_stage(m, 8, m.rows[136])
        selu_stage(m, b0)

        store_stage(m, [(m.rows[128], m.acc[:, 0:TILES, 0:D])])
        sum_stage(m, m.rows[128], D, degree=True)
        degree_stage(m)
        dense_stage(m, m.acc, 1, w0a, HID, m.acc, b0a, relu=True)
        dense_stage(m, m.acc, 2, w0b, HID, m.acc, b0b, relu=True)
        store_stage(m, [(m.rows[256], m.acc[:, 0:TILES, 0:HID])])
        sum_stage(m, m.rows[256], HID)
        dense_stage(m, m.acc, 2, w1a, HID, m.acc, b1a, relu=True)
        dense_stage(m, m.acc, 2, w1b, HID, m.acc, b1b, relu=True)
        dense_stage(m, m.acc, 2, w2a, D, m.acc)
        store_stage(m, [(m.rows[128], m.acc[:, 0:TILES, 0:D])])
        sum_stage(m, m.rows[128], D)
        bias_relu_stage(m, b2a)
        dense_stage(m, m.acc, 1, w2b, D, m.acc, b2b, relu=True)
        residual_stage(m, m.acc)

        dense_stage(m, m.x, 1, W2, D, m.acc)
        head_stage(m, s2, d2, 4, m.rows[132])
        attention_stage(m, m.rows[132], 4)
        loop_stage(m, 4, m.rows[132])
        divide_stage(m, gb)
        dense_stage(m, m.x, 1, skip, D, m.tmp)
        skip_norm_stage(m, sbias, lng, lnb)
        residual_stage(m, m.sums)

        for n in range(3):
            dense_stage(m, m.x if n == 0 else m.acc, 1, G[n], D, m.acc)
            scale_stage(m)
            store_stage(m, [(m.rows[128], m.acc[:, 0:TILES, 0:D])])
            sum_stage(m, m.rows[128], D, weighted=True)
            scale_stage(m, gbias[n], relu=n < 2)
        residual_stage(m, m.acc)
        output_stage(m, out)


def kernel(**inputs):
    import numpy as _np
    import concourse.bacc as _bacc
    from concourse.bass_utils import run_bass_kernel_spmd as _run

    nc = _bacc.Bacc("TRN2", target_bir_lowering=False, num_devices=1)
    arrays, w = {}, {}
    for name, value in inputs.items():
        a = _np.ascontiguousarray(value)
        arrays[f"in_{name}"] = a
        w[name] = nc.dram_tensor(f"in_{name}", a.shape, mybir.dt.from_np(a.dtype), kind="ExternalInput").ap()
    nc.disable_value_cache = True
    out = nc.dram_tensor("out_x", (N, D), fp32, kind="ExternalOutput").ap()
    build(nc, w, out)
    return _run(nc, [arrays], core_ids=[0]).results[0]["out_x"]
```

```python
from contextlib import ExitStack

import concourse.bass as bass
from concourse import mybir

fp32 = mybir.dt.float32
bf16 = mybir.dt.bfloat16
i32 = mybir.dt.int32
ALU = mybir.AluOpType
ACT = mybir.ActivationFunctionType
AX = mybir.AxisListType
DVE_ONLY = [mybir.EngineType.DVE]
PE_ONLY = [mybir.EngineType.PE]

P = 128
N = 6250
D = 128
E = 100000
TILES = -(-N // P)
NPAD = TILES * P
RUNS = -(-E // P)
EPAD = RUNS * P
U = 16
QUAD = 4
QUADS = 13
GROUP = QUAD * QUADS
GROUPS = -(-(RUNS + TILES - 1) // GROUP)
STEPS = GROUPS * GROUP
TURNS = STEPS // U
BATCH = 7
BATCHES = TILES // BATCH
HID = 256
ACCW = HID + 1
BIG = 2.0 ** 100
LN_EPS = 1e-5
SOFTMAX_EPS = 1e-16
SLOPE = 0.2
SELU_SCALE = 1.0507009873554805
SELU_ALPHA = 1.6732632423543772
COUNT_ROWS = 125
COUNT_COLS = E // COUNT_ROWS
MOST = 20
SUM_ROW = 16
WIDE = D + 8
assert GROUPS % 2 == 0 and TILES % BATCH == 0 and COUNT_ROWS * COUNT_COLS == E and STEPS % U == 0


class Signal:

    def __init__(self, nc, name):
        self.sem = nc.alloc_semaphore(name)
        self.base = 0

    def at(self, n):
        return self.base + n

    def past(self, n):
        self.base += n


class Parts:

    def __init__(self, room):
        self.room, self.end = room, 0

    def take(self, a, b, c=1):
        begin, self.end = self.end, self.end + a * b * c
        part = self.room[:, begin:self.end]
        if c == 1:
            return part.rearrange("p (a b) -> p a b", a=a)
        return part.rearrange("p (a b c) -> p a b c", a=a, b=b)


class Memory:

    def __init__(self, nc, ctx):
        def sb(name, shape, dt=fp32):
            return ctx.enter_context(nc.sbuf_tensor(name, shape, dt))

        self.nc = nc
        self.rows = {w: nc.dram_tensor(f"rows_{w}", (NPAD, w), fp32, kind="Internal").ap()
                     for w in (128, 132, 136, 256)}
        self.runs = nc.dram_tensor("runs", (RUNS, 3 * P), i32, kind="Internal").ap()
        self.tile_list = nc.dram_tensor("tile_list", (1, STEPS), i32, kind="Internal").ap()
        self.x = sb("x", [P, TILES, D])
        acc = sb("acc", [P, (TILES + 1) * ACCW])
        self.acc_flat = acc[:, :]
        self.acc = acc[:, :].rearrange("p (t c) -> p t c", c=ACCW)
        parts = Parts(acc)
        self.sums = parts.take(TILES + 1, WIDE)
        self.new_top = parts.take(TILES + 1, 8)
        self.turned = parts.take(1, QUAD * P).bitcast(bf16).rearrange("p a (b c) -> p (a b) c", b=2)
        self.message = parts.take(2, QUAD, WIDE)
        self.arrived = parts.take(GROUP, 8)
        self.rest = parts.take(8, GROUP)
        self.lastone = parts.take(3 * QUAD // 2, P).bitcast(bf16).rearrange("p a (b c) -> p (a b) c", b=2)
        self.self_p = parts.take(TILES, 8)
        self.nodes = parts.take(2, QUAD, 16)
        self.group_local = parts.take(1, GROUP)[:, 0]
        self.group_last = parts.take(1, GROUP)[:, 0]
        self.scans = parts.take(8, P)[0:GROUP]
        room = sb("room", [P, 2 * GROUP * WIDE])
        self.room_flat = room[:, :]
        self.wide = room[:, :].rearrange("p (b s w) -> p b s w", b=2, w=WIDE)
        parts = Parts(room)
        self.tmp = parts.take(TILES, D)
        self.stage = parts.take(BATCH, HID)
        stageT = parts.take(2, BATCH * P)
        self.gathered = parts.take(U, HID)
        self.stageT = (stageT, self.gathered[:, 0:BATCH, :].rearrange("p a b -> p (a b)").rearrange("p (k n) -> p k n", k=2))
        self.shift = sb("shift", [P, TILES + 1, 16])
        self.top = sb("top", [P, TILES + 1, 8])
        self.self_a = sb("self_a", [P, TILES, 8])
        self.small = sb("small", [P, TILES + 1, 8])
        self.mean = sb("mean", [P, TILES])
        self.var = sb("var", [P, TILES])
        self.dinv = sb("dinv", [P, TILES])
        self.local = sb("local", [P, STEPS])
        self.last = sb("last", [P, STEPS])
        self.src = sb("src", [P, STEPS], i32)
        self.weight = sb("weight", [P, STEPS])
        self.tile_of = sb("tile_of", [1, STEPS], i32)
        self.reset = sb("reset", [GROUP, GROUPS + 1, P])
        self.identity = sb("identity", [P, P])
        self.columns = sb("columns", [P, P])
        self.ones = sb("ones", [P, P])
        self.pick = sb("pick", [P, 2, U // 2], i32)
        self.onehot = sb("onehot", [P, 5 * QUAD, P])
        self.columns_b = sb("columns_b", [P, P], bf16)
        self.maxima = sb("maxima", [P, 3, 8, GROUP], bf16)
        self.shift3 = sb("shift3", [P, TILES + 1, 3, 16], bf16)
        self.identity_b = sb("identity_b", [P, P], bf16)
        self.floor = sb("floor", [P, 8], bf16)
        self.lift = sb("lift", [P, 8], bf16)
        self.logit = sb("logit", [P, 2, QUAD, 8])
        self.logit2 = sb("logit2", [P, 2, QUAD, 8])
        self.below = sb("below", [P, 2, QUAD, 8])
        self.factor = sb("factor", [P, 8])
        self.psum = ctx.enter_context(nc.psum_tensor("psum", [P, 8, 512], fp32))
        self.signals = []

        def signal(name):
            self.signals.append(Signal(nc, name))
            return self.signals[-1]

        self.s_chain = signal("s_chain")
        self.s_loaded = signal("s_loaded")
        self.s_stored = signal("s_stored")
        self.s_const_ready = signal("s_const_ready")
        self.s_copied = signal("s_copied")
        self.s_turned_up = signal("s_turned_up")
        self.s_turned_copied = signal("s_turned_copied")
        self.s_multiplied = signal("s_multiplied")
        self.s_evacuated = signal("s_evacuated")
        self.s_final = signal("s_final")
        self.s_act_turn = signal("s_act_turn")
        self.s_dve_turn = signal("s_dve_turn")
        self.s_indices_ready = signal("s_indices_ready")
        self.s_picked = signal("s_picked")
        self.s_onehot_ready = signal("s_onehot_ready")
        self.s_degree_put = signal("s_degree_put")
        self.s_summed = signal("s_summed")
        self.s_added = signal("s_added")
        self.s_turned_ready = signal("s_turned_ready")
        self.s_expanded = signal("s_expanded")
        self.s_logits_ready = signal("s_logits_ready")
        self.s_probs_ready = signal("s_probs_ready")
        self.s_message_ready = signal("s_message_ready")
        self.s_heads_turned = signal("s_heads_turned")
        self.s_scanned = signal("s_scanned")
        self.s_turned_back = signal("s_turned_back")
        self.s_group_free = signal("s_group_free")
        self.s_landed = signal("s_landed")
        self.s_arrived = signal("s_arrived")
        self.s_last_ready = signal("s_last_ready")
        self.s_max_summed = signal("s_max_summed")
        self.s_high = signal("s_high")
        self.s_middle = signal("s_middle")
        self.s_rest = signal("s_rest")
        self.s_split = signal("s_split")
        self.s_below = signal("s_below")
        self.s_top = signal("s_top")
        self.s_factor = signal("s_factor")
        self.s_gate = signal("s_gate")
        self.s_rows = [Signal(nc, f"s_rows_{u}") for u in range(U)]


class Chain:

    def __init__(self, engine, done, turn=None, per_turn=0):
        self.engine, self.done, self.turn, self.per_turn, self.n = engine, done, turn, per_turn, 0

    def link(self, instruction):
        self.start(instruction)
        self.wait()

    def start(self, instruction):
        self.n += 1
        instruction.then_inc(self.done.sem, 1)

    def wait(self):
        before = self.done.at(self.n)
        if self.turn is not None:
            before = self.turn * self.per_turn + before
        self.engine.wait_ge(self.done.sem, before)


def start_stage(m):
    with m.nc.Block() as block:

        @block.sync
        def _(sp):
            for raised in m.signals:
                if raised is not m.s_loaded and raised is not m.s_stored:
                    sp.sem_inc(raised.sem, 1)
                    raised.past(1)


def gate(m, engine):
    engine.sem_inc(m.s_gate.sem, 1)


def spread(vector, *shape):
    return vector.partition_broadcast(P)


def over_tiles(ap, width, tiles=TILES):
    return ap.unsqueeze(2).broadcast_to([P, tiles, width])


def over_nodes(row, width, tiles=TILES):
    return row.unsqueeze(1).broadcast_to([P, tiles, width])


def by_head(ap, heads):
    return ap.rearrange("p t (h c) -> p t h c", h=heads)


def load_stage(m, w, params, x):
    nc = m.nc
    count_dst = m.gathered[0:COUNT_ROWS, 0:4, 0:HID].rearrange("p a b -> p (a b)")[:, 0:COUNT_COLS].bitcast(i32)
    pad = EPAD - E
    with nc.Block() as block:

        @block.sync
        def _(sp):
            n = 0
            full = (TILES - 1) * P
            sp.wait_ge(m.s_const_ready.sem, m.s_const_ready.at(2))
            sp.dma_start(m.x[:, 0:TILES - 1, :], x[0:full, :].rearrange("(t p) d -> p t d", p=P)).then_inc(m.s_loaded.sem, 16)
            sp.dma_start(m.x[0:N - full, TILES - 1, :], x[full:N, :]).then_inc(m.s_loaded.sem, 16)
            sp.dma_start(count_dst, w["dst"].rearrange("(p c) -> p c", c=COUNT_COLS)).then_inc(m.s_loaded.sem, 16)
            n += 3
            whole = RUNS - 1
            for a, edges in enumerate((w["dst"], w["src"], w["edge_weight"].bitcast(i32))):
                runs = m.runs[:, a * P:(a + 1) * P]
                sp.dma_start(runs[0:whole, :], edges[0:whole * P].rearrange("(r e) -> r e", e=P)).then_inc(m.s_loaded.sem, 16)
                sp.dma_start(runs[whole:RUNS, 0:P - pad], edges[whole * P:E].rearrange("(r e) -> r e", r=1)).then_inc(m.s_loaded.sem, 16)
                n += 2
            for a, row in enumerate((0, 1, 1)):
                sp.dma_start(m.runs[whole:RUNS, (a + 1) * P - pad:(a + 1) * P], m.pick_pad[0:1, row, 0:pad]).then_inc(m.s_loaded.sem, 16)
                n += 1
            for tile, source in params:
                sp.dma_start(tile, source).then_inc(m.s_loaded.sem, 16)
                n += 1
            sp.wait_ge(m.s_loaded.sem, m.s_loaded.at(16 * n))
            m.s_loaded.past(16 * n)

        @block.vector
        def _(dve):
            nc.vector.memset(m.pick_pad[0:1, 0, :], -1)
            nc.vector.memset(m.pick_pad[0:1, 1, :], 0).then_inc(m.s_const_ready.sem, 1)
            nc.vector.memset(m.ones[:, :], 1.0)
            nc.vector.memset(m.x[:, TILES - 1, :], 0.0).then_inc(m.s_const_ready.sem, 1)

        @block.gpsimd
        def _(pool):
            nc.gpsimd.memset(m.identity[:, :], 0.0).then_inc(m.s_copied.sem, 1)
            pool.wait_ge(m.s_copied.sem, m.s_copied.at(1))
            nc.gpsimd.affine_select(out=m.identity[:, :], in_=m.identity[:, :], compare_op=ALU.not_equal, fill=1.0,
                                    base=0, pattern=[[-1, P]], channel_multiplier=1)
            nc.gpsimd.iota(m.columns_i[:, :], pattern=[[1, P]], base=0, channel_multiplier=0)
            nc.gpsimd.iota(m.step_number_i[:, :], pattern=[[GROUP, GROUPS]], base=0, channel_multiplier=1)

    m.s_const_ready.past(2)
    m.s_copied.past(1)
    return count_dst


def prepare_stage(m, count_dst):
    nc = m.nc
    T1 = TILES + 1
    dstf = m.tmp[0:COUNT_ROWS, 0:7, :].rearrange("p a b -> p (a b)")[:, 0:COUNT_COLS]
    junk = [m.tmp[0:COUNT_ROWS, t:t + 7, :].rearrange("p a b -> p (a b)")[:, 0:COUNT_COLS] for t in (7, 14)]
    at = iter(range(21, TILES))

    def scratch(width, dt=fp32):
        s = m.tmp[:, next(at), 0:width]
        return s if dt is fp32 else s.bitcast(dt)

    bounds, below = scratch(T1), scratch(T1)
    start, start_i, first = scratch(T1), scratch(T1, i32), scratch(TILES)
    end_i, final, filled, length = scratch(TILES, i32), scratch(TILES), scratch(TILES), scratch(TILES)
    upto, lead, number = scratch(TILES), scratch(TILES), scratch(TILES)
    step = m.step_number
    tile = scratch(GROUPS)[0:GROUP, :]
    tile_i = scratch(GROUPS, i32)[0:GROUP, :]
    run = scratch(GROUPS)[0:GROUP, :]
    run_i = scratch(GROUPS, i32)[0:GROUP, :]
    tile128 = scratch(GROUPS)[0:GROUP, :]
    match = m.match
    rows = m.prep_rows
    row_f = m.prep_float
    GT = [GROUP, GROUPS, TILES]
    GP = [GROUP, GROUPS, P]

    with nc.Block() as block:

        @block.vector
        def _(dve):
            c = Chain(dve, m.s_chain)
            c.link(nc.vector.tensor_copy(m.columns[:, :], m.columns_i[:, :]))
            c.link(nc.vector.tensor_copy(m.columns_b[:, :], m.columns_i[:, :]))
            c.link(nc.vector.tensor_copy(m.step_number[:, :], m.step_number_i[:, :]))
            c.link(nc.vector.tensor_copy(dstf, count_dst))
            c.link(nc.vector.tensor_scalar(bounds, m.columns[:, 0:T1], float(P), None, ALU.mult))
            c.link(nc.vector.tensor_copy(number, m.columns[:, 0:TILES]))
            c.link(nc.vector.memset(below, 0.0))
            dve.sem_inc(m.s_dve_turn.sem, 1)
            with dve.Fori(0, T1 // 2) as pair:
                for b in range(2):
                    dve.wait_ge(m.s_dve_turn.sem, pair * 2 + m.s_dve_turn.at(b))
                    nc.vector.tensor_scalar(junk[b], dstf, bounds[0:COUNT_ROWS, bass.ds(pair * 2 + b, 1)], 0.0, ALU.is_lt, ALU.add,
                                            accum_out=below[0:COUNT_ROWS, bass.ds(pair * 2 + b, 1)]).then_inc(m.s_dve_turn.sem, 1)
            dve.wait_ge(m.s_dve_turn.sem, m.s_dve_turn.at(T1 + 1))
            nc.vector.tensor_copy(number, m.columns[:, 0:TILES]).then_inc(m.s_copied.sem, 1)
            dve.wait_ge(m.s_multiplied.sem, m.s_multiplied.at(1))
            c.link(nc.vector.tensor_copy(start, m.psum[:, 0, 0:T1]))
            c.link(nc.vector.tensor_copy(start_i, start))
            c.link(nc.vector.tensor_scalar(start_i, start_i, 7, None, ALU.arith_shift_right))
            c.link(nc.vector.tensor_copy(first, start_i[:, 0:TILES]))
            c.link(nc.vector.tensor_scalar(final, start[:, 1:T1], -1.0, None, ALU.add))
            c.link(nc.vector.tensor_copy(end_i, final))
            c.link(nc.vector.tensor_scalar(end_i, end_i, 7, None, ALU.arith_shift_right))
            c.link(nc.vector.tensor_copy(final, end_i))
            c.link(nc.vector.tensor_tensor(filled, start[:, 1:T1], start[:, 0:TILES], ALU.is_gt))
            c.link(nc.vector.tensor_tensor(length, final, first, ALU.subtract))
            c.link(nc.vector.tensor_scalar(length, length, 1.0, None, ALU.add))
            c.link(nc.vector.tensor_tensor(length, length, filled, ALU.mult))
            c.link(nc.vector.memset(lead, 0.0))
            c.link(nc.vector.tensor_tensor_scan(upto, length, lead, 0.0, ALU.add, ALU.add))
            c.link(nc.vector.tensor_tensor(lead, length, upto, ALU.subtract))
            c.link(nc.vector.tensor_tensor(lead, lead, first, ALU.add))
            steps3 = step[0:GROUP, :].unsqueeze(2).broadcast_to(GT)
            c.link(nc.vector.tensor_tensor(match, upto[0:GROUP, :].unsqueeze(1).broadcast_to(GT), steps3, ALU.is_le))
            c.link(nc.vector.tensor_reduce(tile, match, AX.X, ALU.add))
            c.link(nc.vector.tensor_tensor(match, number[0:GROUP, :].unsqueeze(1).broadcast_to(GT),
                                           tile.unsqueeze(2).broadcast_to(GT), ALU.is_equal))
            c.link(nc.vector.tensor_tensor(match, match, lead[0:GROUP, :].unsqueeze(1).broadcast_to(GT), ALU.mult))
            c.link(nc.vector.tensor_reduce(run, match, AX.X, ALU.add))
            c.link(nc.vector.tensor_tensor(run, run, step[0:GROUP, :], ALU.add))
            c.link(nc.vector.tensor_scalar(run, run, float(RUNS - 1), None, ALU.min))
            c.link(nc.vector.tensor_copy(run_i, run))
            c.link(nc.vector.tensor_copy(tile_i, tile))
            nc.vector.tensor_scalar(tile128, tile, float(P), None, ALU.mult).then_inc(m.s_indices_ready.sem, 1)
            for u in range(U):
                dve.wait_ge(m.s_rows[u].sem, m.s_rows[u].at(16 * len(range(GROUPS)[u::U])))
            c.link(nc.vector.tensor_copy(row_f[:, 0], rows[:, :, 0]))
            c.link(nc.vector.tensor_copy(row_f[:, 1], rows[:, :, 1]))
            c.link(nc.vector.tensor_copy(row_f[:, 2], rows[:, :, 2].bitcast(fp32)))
            c.link(nc.vector.memset(m.reset[:, GROUPS, :], 0.0))
            c.link(nc.vector.memset(m.reset[:, 0:GROUPS, 0:1], 0.0))
            c.link(nc.vector.tensor_tensor(m.reset[:, 0:GROUPS, 1:P], row_f[:, 0, :, 1:P], row_f[:, 0, :, 0:P - 1], ALU.is_equal))
            c.link(nc.vector.memset(row_f[:, 3], 1.0))
            c.link(nc.vector.tensor_scalar(row_f[:, 3, :, 0:P - 1], m.reset[:, 0:GROUPS, 1:P], -1.0, 1.0, ALU.mult, ALU.add))
            c.link(nc.vector.tensor_scalar(m.reset[:, 0:GROUPS, :], m.reset[:, 0:GROUPS, :], -1.0, BIG, ALU.add, ALU.mult))
            c.link(nc.vector.tensor_tensor(row_f[:, 0], row_f[:, 0], tile128.unsqueeze(2).broadcast_to(GP), ALU.subtract))
            c.link(nc.vector.tensor_scalar(row_f[:, 4], row_f[:, 0], float(2 * NPAD), None, ALU.add))
            c.link(nc.vector.tensor_tensor(row_f[:, 3], row_f[:, 3], row_f[:, 4], ALU.mult))
            nc.vector.tensor_scalar(row_f[:, 3], row_f[:, 3], float(-2 * NPAD), None, ALU.add).then_inc(m.s_copied.sem, 1)
            for a, target in enumerate((m.local, m.src, m.weight, m.last)):
                dve.wait_ge(m.s_turned_up.sem, m.s_turned_up.at(a + 1))
                nc.vector.tensor_copy(target[:, :].rearrange("p (a b) -> p a b", a=2),
                                      m.psum[:, 2 * a:2 * a + 2, 0:STEPS // 2]).then_inc(m.s_evacuated.sem, 1)
            nc.vector.memset(m.acc[:, :, :], 0.0)
            m.s_chain.past(c.n)

        @block.tensor
        def _(pe):
            pe.wait_ge(m.s_copied.sem, m.s_copied.at(1))
            nc.tensor.matmul(m.psum[:, 0, 0:T1], m.ones[:, :], below[:, :], start=True, stop=True).then_inc(m.s_multiplied.sem, 1)
            pe.wait_ge(m.s_copied.sem, m.s_copied.at(2))
            for a in range(4):
                for g in range(GROUPS):
                    at = g % (GROUPS // 2) * GROUP
                    turned = nc.tensor.transpose(m.psum[:, 2 * a + g // (GROUPS // 2), at:at + GROUP], row_f[:, a, g, :],
                                                 m.identity[0:GROUP, 0:GROUP])
                turned.then_inc(m.s_turned_up.sem, 1)

        @block.gpsimd
        def _(pool):
            pool.wait_ge(m.s_indices_ready.sem, m.s_indices_ready.at(1))
            for g in range(GROUPS):
                nc.gpsimd.indirect_dma_start(
                    rows[:, g].rearrange("p a e -> p (a e)"), None, m.runs, bass.IndirectOffsetOnAxis(ap=run_i[:, g:g + 1], axis=0)
                ).then_inc(m.s_rows[g % U].sem, 16)

        @block.sync
        def _(sp):
            sp.wait_ge(m.s_indices_ready.sem, m.s_indices_ready.at(1))
            with nc.allow_non_contiguous_dma("a small table"):
                sp.dma_start(m.tile_list.rearrange("o (g p) -> (o p) g", p=GROUP), tile_i,
                             allow_slow_non_contiguous=True).then_inc(m.s_stored.sem, 16)
            sp.wait_ge(m.s_stored.sem, m.s_stored.at(16))
            sp.dma_start(m.tile_of[:, :], m.tile_list).then_inc(m.s_loaded.sem, 16)
            sp.wait_ge(m.s_loaded.sem, m.s_loaded.at(16))

    m.s_dve_turn.past(1 + T1)
    m.s_copied.past(2)
    m.s_multiplied.past(1)
    m.s_indices_ready.past(1)
    for u in range(U):
        m.s_rows[u].past(16 * len(range(GROUPS)[u::U]))
    m.s_turned_up.past(4)
    m.s_evacuated.past(4)
    m.s_stored.past(16)
    m.s_loaded.past(16)


def dense_stage(m, source, blocks, weight, width, target, bias=None, relu=False, scale=False, table=None):
    nc = m.nc
    turned = m.psum[:, 0:4, :].rearrange("p b c -> p (b c)")
    product = m.psum[:, 4:8, :].rearrange("p b c -> p (b c)")
    final = m.s_evacuated if not relu else m.s_final

    def batches(engine, step):
        with engine.Fori(0, BATCHES // 2) as pair:
            for half in range(2):
                step(pair * 2 + half, half)
        step(BATCHES - 1, (BATCHES - 1) % 2)

    assert BATCHES % 2 == 1
    with nc.Block() as block:

        @block.scalar
        def _(act):
            def stage(b):
                act.wait_ge(m.s_turned_up.sem, b + m.s_turned_up.at(0))
                gate(m, act)
                nc.scalar.copy(m.stage[:, :, 0:blocks * P], source[:, bass.ds(b * BATCH, BATCH), 0:blocks * P]).then_inc(m.s_copied.sem, 1)

            def unload(b, half):
                act.wait_ge(m.s_turned_up.sem, b + m.s_turned_up.at(1))
                nc.scalar.copy(m.stageT[half][:, 0:blocks, :],
                               turned[:, 0:blocks * BATCH * P].rearrange("p (k n) -> p k n", k=blocks)).then_inc(m.s_turned_copied.sem, 1)

            stage(0)
            with act.Fori(0, BATCHES // 2) as pair:
                for half in range(2):
                    unload(pair * 2 + half, half)
                    stage(pair * 2 + half + 1)
            unload(BATCHES - 1, (BATCHES - 1) % 2)

        @block.vector
        def _(dve):
            def take(b, half):
                dve.wait_ge(m.s_multiplied.sem, b + m.s_multiplied.at(1))
                out = target[:, bass.ds(b * BATCH, BATCH), 0:width]
                got = product[:, 0:BATCH * width].rearrange("p (t n) -> p t n", n=width)
                if scale:
                    nc.vector.tensor_tensor(out, got, over_tiles(m.dinv[:, bass.ds(b * BATCH, BATCH)], width, BATCH), ALU.mult).then_inc(m.s_evacuated.sem, 1)
                elif bias is None:
                    nc.vector.tensor_scalar(out, got, 1.0, None, ALU.mult).then_inc(m.s_evacuated.sem, 1)
                else:
                    nc.vector.tensor_tensor(out, got, over_nodes(bias, width, BATCH), ALU.add).then_inc(m.s_evacuated.sem, 1)
                if relu:
                    dve.wait_ge(m.s_evacuated.sem, b + m.s_evacuated.at(1))
                    nc.vector.tensor_scalar(out, out, 0.0, None, ALU.max).then_inc(m.s_final.sem, 1)

            batches(dve, take)

        @block.tensor
        def _(pe):
            def turn(b):
                pe.wait_ge(m.s_copied.sem, b + m.s_copied.at(1))
                pe.wait_ge(m.s_turned_copied.sem, b + m.s_turned_copied.at(0))
                for k in range(blocks):
                    for t in range(BATCH):
                        up = nc.tensor.transpose(turned[:, (k * BATCH + t) * P:(k * BATCH + t + 1) * P],
                                                 m.stage[:, t, k * P:(k + 1) * P], m.identity[:, :])
                up.then_inc(m.s_turned_up.sem, 1)

            def multiply(b, half):
                pe.wait_ge(m.s_turned_copied.sem, b + m.s_turned_copied.at(1))
                pe.wait_ge(m.s_evacuated.sem, b + m.s_evacuated.at(0))
                for t in range(BATCH):
                    for k in range(blocks):
                        mm = nc.tensor.matmul(product[:, t * width:(t + 1) * width], m.stageT[half][:, k, t * P:(t + 1) * P],
                                              weight[:, k, 0:width], start=(k == 0), stop=(k == blocks - 1))
                mm.then_inc(m.s_multiplied.sem, 1)

            turn(0)
            with pe.Fori(0, BATCHES // 2) as pair:
                for half in range(2):
                    turn(pair * 2 + half + 1)
                    multiply(pair * 2 + half, half)
            multiply(BATCHES - 1, (BATCHES - 1) % 2)

        if table is not None:
            @block.sync
            def _(sp):
                rows = table.rearrange("(t p) d -> p t d", p=P)
                for b in range(BATCHES):
                    sp.wait_ge(final.sem, final.at(b + 1))
                    sp.dma_start(rows[:, b * BATCH:(b + 1) * BATCH, :], target[:, b * BATCH:(b + 1) * BATCH, 0:width]).then_inc(m.s_stored.sem, 16)
                sp.wait_ge(m.s_stored.sem, m.s_stored.at(16 * BATCHES))

    for s in (m.s_copied, m.s_turned_up, m.s_turned_copied, m.s_multiplied, m.s_evacuated):
        s.past(BATCHES)
    if relu:
        m.s_final.past(BATCHES)
    if table is not None:
        m.s_stored.past(16 * BATCHES)


def store_stage(m, stores):
    nc = m.nc
    with nc.Block() as block:

        @block.sync
        def _(sp):
            for target, source in stores:
                sp.dma_start(target.rearrange("(t p) d -> p t d", p=P), source).then_inc(m.s_stored.sem, 16)
            sp.wait_ge(m.s_stored.sem, m.s_stored.at(16 * len(stores)))

    m.s_stored.past(16 * len(stores))


def pool_gathers(m, pool, table, width):
    nc = m.nc
    half = U // 2
    with pool.Fori(0, TURNS) as i:
        for u in range(U):
            if u % half == 0:
                pool.wait_ge(m.s_picked.sem, i * 2 + m.s_picked.at(u // half + 1))
            pool.wait_ge(m.s_summed.sem, i * U + m.s_summed.at(u + 1))
            gate(m, pool)
            nc.gpsimd.indirect_dma_start(
                m.gathered[:, u, 0:width], None, table,
                bass.IndirectOffsetOnAxis(ap=m.pick[:, u // half, u % half:u % half + 1], axis=0)
            ).then_inc(m.s_rows[u].sem, 16)


def load_tiles(m, start, count=U, engines=DVE_ONLY):
    _, tiles = m.nc.values_load_multi_w_load_instructions(
        m.tile_of[0:1, bass.ds(start, count)], engines=engines, min_val=0, max_val=TILES,
        skip_runtime_bounds_check_because="prepare_stage counts the tiles that end before a step: 0 to TILES")
    return tiles


def tile_row(ap, tile, width):
    return ap[:, bass.ds(tile, 1), 0:width].rearrange("p o c -> p (o c)")


def sum_stage(m, table, width, weighted=False, degree=False):
    nc = m.nc
    S, L = 4, 3
    total = width + degree

    with nc.Block() as block:

        @block.gpsimd
        def _(pool):
            pool_gathers(m, pool, table, width)

        @block.vector
        def _(dve):
            dve.sem_inc(m.s_added.sem, S)
            with dve.Fori(0, TURNS) as i:
                tiles = load_tiles(m, i * U)
                for j in range(U + L):
                    if j < U:
                        dve.wait_ge(m.s_summed.sem, i * U + m.s_summed.at(U + j - S + 1))
                        one = (m.local[:, bass.ds(i * U + j, 1)], ALU.is_equal)
                        if weighted:
                            nc.vector.tensor_scalar(m.onehot[:, j % S, :], m.columns[:, :], one[0],
                                                    m.weight[:, bass.ds(i * U + j, 1)], one[1], ALU.mult).then_inc(m.s_onehot_ready.sem, 1)
                        else:
                            nc.vector.tensor_scalar(m.onehot[:, j % S, :], m.columns[:, :], one[0], None, one[1]).then_inc(m.s_onehot_ready.sem, 1)
                    if j >= L:
                        k = j - L
                        dve.wait_ge(m.s_summed.sem, i * U + m.s_summed.at(U + k + 1))
                        dve.wait_ge(m.s_added.sem, i * U + m.s_added.at(S + k))
                        row = tile_row(m.acc, tiles[k], total)
                        nc.vector.tensor_tensor(row, row, m.psum[:, k % S, 0:total], ALU.add).then_inc(m.s_added.sem, 1)

        @block.scalar
        def _(act):
            half = U // 2
            with act.Fori(0, TURNS) as i:
                for h in range(2):
                    for v in range(h * half, (h + 1) * half):
                        act.wait_ge(m.s_rows[v].sem, i * 16 + m.s_rows[v].at(0))
                    gate(m, act)
                    nc.scalar.copy(m.pick[:, h, :], m.src[:, bass.ds(i * U + h * half, half)]).then_inc(m.s_picked.sem, 1)
                    if not degree:
                        continue
                    for u in range(h * half, (h + 1) * half):
                        act.wait_ge(m.s_summed.sem, i * U + m.s_summed.at(u + 1))
                        nc.scalar.copy(m.gathered[:, u, width:width + 1], m.weight[:, bass.ds(i * U + u, 1)]).then_inc(m.s_degree_put.sem, 1)

        @block.tensor
        def _(pe):
            pe.sem_inc(m.s_summed.sem, U)
            with pe.Fori(0, TURNS) as i:
                for u in range(U):
                    pe.wait_ge(m.s_onehot_ready.sem, i * U + m.s_onehot_ready.at(u + 1))
                    pe.wait_ge(m.s_rows[u].sem, i * 16 + m.s_rows[u].at(16))
                    if degree:
                        pe.wait_ge(m.s_degree_put.sem, i * U + m.s_degree_put.at(u + 1))
                    pe.wait_ge(m.s_added.sem, i * U + m.s_added.at(u + 1))
                    nc.tensor.matmul(m.psum[:, u % S, 0:total], m.onehot[:, u % S, :], m.gathered[:, u, 0:total],
                                     start=True, stop=True).then_inc(m.s_summed.sem, 1)

    m.s_picked.past(2 * TURNS)
    m.s_summed.past(U + STEPS)
    m.s_added.past(S + STEPS)
    m.s_onehot_ready.past(STEPS)
    if degree:
        m.s_degree_put.past(STEPS)
    for s in m.s_rows:
        s.past(16 * TURNS)


def attention_stage(m, table, heads):
    nc = m.nc
    H = heads
    W = D + H
    C = D // H
    SLOTS = 5
    LAST_SLOTS = 3
    ROWS = U // 2
    LOGITS, MESSAGE, ADD = 2, 3, 5
    TAKE = 2
    LINKS = 6 + 3 * QUADS
    arrived = m.arrived[:, :, 0:H]
    scanned = m.psum[:, 6, 0:H * GROUP].rearrange("p (h k) -> p h k", h=H)
    rest = m.rest[:, 0:H, :]

    def columns(bank, width):
        return m.psum[:, bank, 0:QUAD * SUM_ROW].rearrange("p (j n) -> p j n", n=SUM_ROW)[:, :, 0:width]

    def expanded(bank):
        return m.psum[:, bank, 0:QUAD * 6 * H].rearrange("p (j a c) -> p j a c", j=QUAD, a=3)

    def at(signal, g, per_group, n):
        return g * per_group + signal.at(n)

    def gathers(r):
        return len(range(GROUP)[r::ROWS])

    with nc.Block() as block:

        @block.gpsimd
        def _(pool):
            with pool.Fori(0, GROUPS // 2) as pair:
                for b in range(2):
                    g = pair * 2 + b
                    pool.wait_ge(m.s_group_free.sem, at(m.s_group_free, g, 1, 1))
                    gate(m, pool)
                    nc.gpsimd.tensor_copy(m.pick_group[:, b, :], m.src[:, bass.ds(g * GROUP, GROUP)]).then_inc(m.s_picked.sem, 1)
                    pool.wait_ge(m.s_picked.sem, at(m.s_picked, g, 1, 1))
                    gate(m, pool)
                    for v in range(GROUP):
                        nc.gpsimd.indirect_dma_start(
                            m.wide[:, b, v, 0:W], None, table,
                            bass.IndirectOffsetOnAxis(ap=m.pick_group[:, b, v:v + 1], axis=0)).then_inc(m.s_rows[b * ROWS + v % ROWS].sem, 16)

        @block.sync
        def _(sp):
            with sp.Fori(0, GROUPS // 2) as pair:
                for b in range(2):
                    for r in range(ROWS):
                        landed = m.s_rows[b * ROWS + r]
                        sp.wait_ge(landed.sem, pair * 16 * gathers(r) + landed.at(16 * gathers(r)))
                    gate(m, sp)
                    sp.sem_inc(m.s_landed.sem, 1)
            sp.sem_inc(m.s_landed.sem, 1)

        @block.scalar
        def _(act):
            def arrive(b, group):
                act.wait_ge(m.s_landed.sem, at(m.s_landed, group, 1, 1))
                gate(m, act)
                nc.scalar.copy(arrived, m.wide[:, b, :, D:W]).then_inc(m.s_arrived.sem, 1)

            act.sem_inc(m.s_probs_ready.sem, 2)
            arrive(0, 0)
            with act.Fori(0, GROUPS // 2) as pair:
                for b in range(2):
                    g = pair * 2 + b
                    act.wait_ge(m.s_turned_back.sem, at(m.s_turned_back, g, 1, 1))
                    nc.scalar.copy(m.maxima[:, 0, 0:H, :], scanned).then_inc(m.s_high.sem, 1)
                    act.wait_ge(m.s_rest.sem, at(m.s_rest, g, 2, 1))
                    nc.scalar.copy(m.maxima[:, 1, 0:H, :], rest).then_inc(m.s_middle.sem, 1)
                    act.wait_ge(m.s_dve_turn.sem, at(m.s_dve_turn, g, 1, 1))
                    nc.scalar.copy(m.shift3[:, :, 0, H:2 * H], m.shift[:, :, H:2 * H]).then_inc(m.s_high.sem, 1)
                    nc.scalar.activation(m.factor[:, 0:H], m.factor[:, 0:H], ACT.Exp).then_inc(m.s_act_turn.sem, 1)
                    act.wait_ge(m.s_rest.sem, at(m.s_rest, g, 2, 2))
                    nc.scalar.copy(m.shift3[:, :, 1, H:2 * H], m.new_top[:, :, 0:H]).then_inc(m.s_middle.sem, 1)
                    for j in range(QUADS + LOGITS):
                        if j < QUADS:
                            act.wait_ge(m.s_turned_ready.sem, at(m.s_turned_ready, g, QUADS, j + 1))
                            act.wait_ge(m.s_expanded.sem, at(m.s_expanded, g, QUADS, j + 1))
                            nc.scalar.copy(m.turned[:, j % 2, :], m.psum[:, 4 + j % 2, :]).then_inc(m.s_turned_copied.sem, 1)
                        q = j - LOGITS
                        if q == QUADS - 1:
                            arrive(1 - b, g + 1)
                        if q >= 0:
                            act.wait_ge(m.s_logits_ready.sem, at(m.s_logits_ready, g, QUADS, 2 + q + 1))
                            act.wait_ge(m.s_summed.sem, at(m.s_summed, g, GROUP, QUAD * (SLOTS + q - 1)))
                            nc.scalar.activation(m.below[:, q % 2, :, 0:H], m.logit[:, q % 2, :, 0:H], ACT.Relu, scale=-1.0).then_inc(m.s_below.sem, 1)
                            act.wait_ge(m.s_below.sem, at(m.s_below, g, QUADS, q + 1))
                            nc.scalar.activation(m.message[:, q % 2, :, D:W], m.below[:, q % 2, :, 0:H], ACT.Exp, scale=-1.0).then_inc(m.s_probs_ready.sem, 1)

        @block.vector
        def _(dve):
            def scan(group, h):
                last = nc.vector.tensor_tensor_scan(
                    m.scans[:, h, :], m.reset[:, bass.ds(group, 1), :].rearrange("p o e -> p (o e)"),
                    m.psum[0:GROUP, 4 + h // 4, h % 4 * P:(h % 4 + 1) * P], -BIG, ALU.add, ALU.max)
                if h == H - 1:
                    last.then_inc(m.s_scanned.sem, 1)

            dve.sem_inc(m.s_added.sem, QUAD)
            dve.sem_inc(m.s_logits_ready.sem, 2)
            dve.sem_inc(m.s_top.sem, 2 * QUAD)
            dve.sem_inc(m.s_group_free.sem, 2)
            dve.wait_ge(m.s_heads_turned.sem, m.s_heads_turned.at(1))
            for h in range(H):
                scan(0, h)
            with dve.Fori(0, GROUPS // 2) as pair, dve.Fori(0, 2) as b:
                g = pair * 2 + b
                c = Chain(dve, m.s_chain, g, LINKS)
                c.start(nc.vector.tensor_scalar(m.group_last[:, :], m.last[:, bass.ds(g * GROUP, GROUP)], 1.0, None, ALU.mult))
                c.start(nc.vector.tensor_scalar(m.group_local[:, :], m.local[:, bass.ds(g * GROUP, GROUP)], 1.0, None, ALU.mult))
                dve.wait_ge(m.s_high.sem, at(m.s_high, g, 2, 1))
                nc.vector.tensor_tensor(rest, scanned, m.maxima[:, 0, 0:H, :], ALU.subtract).then_inc(m.s_rest.sem, 1)
                dve.wait_ge(m.s_middle.sem, at(m.s_middle, g, 2, 1))
                nc.vector.tensor_tensor(m.maxima[:, 2, 0:H, :], rest, m.maxima[:, 1, 0:H, :], ALU.subtract).then_inc(m.s_split.sem, 1)
                c.wait()
                for j in range(QUADS + TAKE):
                    q = j - TAKE
                    if q >= 0:
                        if q * QUAD % MOST == 0:
                            tiles = load_tiles(m, g * GROUP + q * QUAD, min(MOST, GROUP - q * QUAD))
                        dve.wait_ge(m.s_max_summed.sem, at(m.s_max_summed, g, QUADS, q + 1))
                    for u in range(QUAD):
                        if q >= 0:
                            row = tile_row(m.top, tiles[(q * QUAD + u) % MOST], H)
                            dve.wait_ge(m.s_top.sem, at(m.s_top, g, GROUP, 2 * QUAD + q * QUAD + u))
                            nc.vector.tensor_tensor(row, columns(q % 2, H)[:, u, :], row, ALU.max).then_inc(m.s_top.sem, 1)
                        if j < QUADS:
                            one = nc.vector.tensor_scalar(m.lastone[:, j % LAST_SLOTS * QUAD + u, :], m.columns_b[:, :],
                                                          m.group_last[:, j * QUAD + u:j * QUAD + u + 1], None, ALU.is_equal)
                            if u == QUAD - 1:
                                one.then_inc(m.s_last_ready.sem, 1)
                dve.wait_ge(m.s_top.sem, at(m.s_top, g, GROUP, 2 * QUAD + GROUP))
                tiles = load_tiles(m, g * GROUP, 1)
                c.link(nc.vector.tensor_tensor(m.new_top[:, :, 0:H], m.top[:, :, 0:H], m.shift[:, :, 0:H], ALU.add))
                c.link(nc.vector.scalar_tensor_tensor(m.new_top[:, :, 0:H], m.new_top[:, :, 0:H], SLOPE, m.new_top[:, :, 0:H],
                                                      ALU.mult, ALU.max))
                old = m.shift[:, bass.ds(tiles[0], 1), H:2 * H].rearrange("p o h -> p (o h)")
                nc.vector.tensor_tensor(m.factor[:, 0:H], old, tile_row(m.new_top, tiles[0], H), ALU.subtract).then_inc(m.s_factor.sem, 1)
                dve.wait_ge(m.s_factor.sem, at(m.s_factor, g, 1, 1))
                nc.vector.tensor_copy(m.shift[:, :, H:2 * H], m.new_top[:, :, 0:H]).then_inc(m.s_dve_turn.sem, 1)
                dve.wait_ge(m.s_dve_turn.sem, at(m.s_dve_turn, g, 1, 1))
                dve.wait_ge(m.s_high.sem, at(m.s_high, g, 2, 2))
                nc.vector.tensor_tensor(m.new_top[:, :, 0:H], m.shift[:, :, H:2 * H], m.shift3[:, :, 0, H:2 * H], ALU.subtract).then_inc(m.s_rest.sem, 1)
                dve.wait_ge(m.s_act_turn.sem, at(m.s_act_turn, g, 1, 1))
                dve.wait_ge(m.s_added.sem, at(m.s_added, g, GROUP, QUAD))
                row = tile_row(m.sums, tiles[0], D).rearrange("p (h c) -> p h c", h=H)
                c.link(nc.vector.tensor_tensor(row, row, m.factor[:, 0:H].unsqueeze(2).broadcast_to([P, H, C]), ALU.mult))
                row = m.sums[:, bass.ds(tiles[0], 1), D:W].rearrange("p o c -> p (o c)")
                c.link(nc.vector.tensor_tensor(row, row, m.factor[:, 0:H], ALU.mult))
                dve.wait_ge(m.s_middle.sem, at(m.s_middle, g, 2, 2))
                nc.vector.tensor_tensor(m.shift3[:, :, 2, H:2 * H], m.new_top[:, :, 0:H], m.shift3[:, :, 1, H:2 * H], ALU.subtract).then_inc(m.s_split.sem, 1)

                for j in range(QUADS + ADD):
                    add = j - ADD
                    q = j - LOGITS
                    if add >= 0 and add * QUAD % MOST == 0:
                        tiles = load_tiles(m, g * GROUP + add * QUAD, min(MOST, GROUP - add * QUAD))
                    if 0 <= q < QUADS:
                        logit, logit2 = m.logit[:, q % 2, :, 0:H], m.logit2[:, q % 2, :, 0:H]
                        nodes = m.nodes[:, q % 2, :, 0:2 * H]
                        a_src = m.wide[:, bass.ds(b, 1), q * QUAD:(q + 1) * QUAD, D:W].rearrange("p o s h -> p (o s) h")
                    for u in range(QUAD):
                        if add >= 0:
                            k = add * QUAD + u
                            dve.wait_ge(m.s_summed.sem, at(m.s_summed, g, GROUP, SLOTS * QUAD + k + 1))
                            dve.wait_ge(m.s_added.sem, at(m.s_added, g, GROUP, QUAD + k))
                            row = tile_row(m.sums, tiles[k % MOST], W)
                            nc.vector.tensor_tensor(row, row, m.psum[:, u, 0:W], ALU.add).then_inc(m.s_added.sem, 1)
                        h = (j - QUADS - LOGITS) * QUAD + u
                        if 0 <= h < H:
                            if h == 0:
                                dve.wait_ge(m.s_heads_turned.sem, at(m.s_heads_turned, g, 1, 2))
                            scan(g + 1, h)
                        if j < QUADS:
                            one = nc.vector.tensor_scalar(m.onehot[:, j % SLOTS * QUAD + u, :], m.columns[:, :],
                                                          m.group_local[:, j * QUAD + u:j * QUAD + u + 1], None, ALU.is_equal)
                            if u == QUAD - 1:
                                one.then_inc(m.s_onehot_ready.sem, 1)
                        if 0 <= q < QUADS:
                            if u == 0:
                                dve.wait_ge(m.s_expanded.sem, at(m.s_expanded, g, QUADS, 2 + q + 1))
                                c.start(nc.vector.tensor_reduce(nodes, expanded(6 + q % 2).rearrange("p j a c -> p j c a"), AX.X, ALU.add))
                            else:
                                c.wait()
                            if u == 1:
                                c.start(nc.vector.tensor_tensor(logit, a_src, nodes[:, :, 0:H], ALU.add))
                            if u == 2:
                                c.start(nc.vector.scalar_tensor_tensor(logit2, logit, SLOPE, logit, ALU.mult, ALU.max))
                            if u == 3:
                                nc.vector.tensor_tensor(logit, logit2, nodes[:, :, H:2 * H], ALU.subtract).then_inc(m.s_logits_ready.sem, 1)
                    q = j - MESSAGE
                    if 0 <= q < QUADS:
                        dve.wait_ge(m.s_probs_ready.sem, at(m.s_probs_ready, g, QUADS, 2 + q + 1))
                        rows = m.wide[:, bass.ds(b, 1), q * QUAD:(q + 1) * QUAD, 0:D].rearrange("p o s (h c) -> p (o s) h c", h=H)
                        nc.vector.tensor_tensor(
                            m.message[:, q % 2, :, 0:D].rearrange("p s (h c) -> p s h c", h=H), rows,
                            m.message[:, q % 2, :, D:W].unsqueeze(3).broadcast_to([P, QUAD, H, C]),
                            ALU.mult).then_inc(m.s_message_ready.sem, 1)
                        if q == QUADS - 1:
                            dve.wait_ge(m.s_message_ready.sem, at(m.s_message_ready, g, QUADS, QUADS))
                            dve.sem_inc(m.s_group_free.sem, 1)
                assert c.n == LINKS, c.n

        @block.tensor
        def _(pe):
            pe.sem_inc(m.s_summed.sem, SLOTS * QUAD)
            pe.sem_inc(m.s_expanded.sem, 2)

            def turn_heads():
                for h in range(H):
                    up = nc.tensor.transpose(m.psum[0:GROUP, 4 + h // 4, h % 4 * P:(h % 4 + 1) * P], arrived[:, :, h], m.identity[:, :])
                up.then_inc(m.s_heads_turned.sem, 1)

            pe.wait_ge(m.s_arrived.sem, m.s_arrived.at(1))
            turn_heads()
            with pe.Fori(0, GROUPS) as g:
                pe.wait_ge(m.s_scanned.sem, at(m.s_scanned, g, 1, 1))
                gate(m, pe)
                for h in range(H):
                    back = nc.tensor.transpose(m.psum[:, 6, h * GROUP:(h + 1) * GROUP], m.scans[:, h, :], m.identity[0:GROUP, 0:GROUP])
                back.then_inc(m.s_turned_back.sem, 1)
                pe.wait_ge(m.s_split.sem, at(m.s_split, g, 2, 1))
                for q in range(QUADS):
                    pe.wait_ge(m.s_last_ready.sem, at(m.s_last_ready, g, QUADS, q + 1))
                    pe.wait_ge(m.s_top.sem, at(m.s_top, g, GROUP, QUAD * (q + 1)))
                    for u in range(QUAD):
                        nc.tensor.matmul(columns(q % 2, H)[:, u, :], m.identity_b[:, :], m.floor[:, 0:H], start=True, stop=False)
                        nc.tensor.matmul(columns(q % 2, H)[:, u, :], m.lastone[:, q % LAST_SLOTS * QUAD + u, :], m.lift[:, 0:H],
                                         start=False, stop=False)
                        for part in range(3):
                            mm = nc.tensor.matmul(columns(q % 2, H)[:, u, :], m.lastone[:, q % LAST_SLOTS * QUAD + u, :],
                                                  m.maxima[:, part, 0:H, q * QUAD + u], start=False, stop=(part == 2))
                    mm.then_inc(m.s_max_summed.sem, 1)
                for j in range(QUADS + MESSAGE):
                    e = j - 1
                    if 0 <= e < QUADS:
                        pe.wait_ge(m.s_turned_copied.sem, at(m.s_turned_copied, g, QUADS, e + 1))
                        pe.wait_ge(m.s_logits_ready.sem, at(m.s_logits_ready, g, QUADS, e + 1))
                        if e == 0:
                            pe.wait_ge(m.s_split.sem, at(m.s_split, g, 2, 2))
                        if e * QUAD % MOST == 0:
                            tiles = load_tiles(m, g * GROUP + e * QUAD, min(MOST, GROUP - e * QUAD), PE_ONLY)
                        for u in range(QUAD):
                            parts = m.shift3[:, bass.ds(tiles[(e * QUAD + u) % MOST], 1), :, 0:2 * H].rearrange("p o a c -> p (o a) c")
                            mm = nc.tensor.matmul(expanded(6 + e % 2)[:, u], m.turned[:, e % 2, u * P:(u + 1) * P], parts,
                                                  start=True, stop=True)
                        mm.then_inc(m.s_expanded.sem, 1)
                    if j < QUADS:
                        pe.wait_ge(m.s_onehot_ready.sem, at(m.s_onehot_ready, g, QUADS, j + 1))
                        for u in range(QUAD):
                            up = nc.tensor.transpose(m.psum[:, 4 + j % 2, u * P:(u + 1) * P], m.onehot[:, j % SLOTS * QUAD + u, :], m.identity[:, :])
                        up.then_inc(m.s_turned_ready.sem, 1)
                    q = j - MESSAGE
                    if q == QUADS - 2:
                        pe.wait_ge(m.s_arrived.sem, at(m.s_arrived, g, 1, 2))
                        gate(m, pe)
                        turn_heads()
                    if 0 <= q < QUADS:
                        pe.wait_ge(m.s_message_ready.sem, at(m.s_message_ready, g, QUADS, q + 1))
                        for u in range(QUAD):
                            pe.wait_ge(m.s_added.sem, at(m.s_added, g, GROUP, q * QUAD + u + 1))
                            nc.tensor.matmul(m.psum[:, u, 0:W], m.onehot[:, q % SLOTS * QUAD + u, :], m.message[:, q % 2, u, 0:W],
                                             start=True, stop=True).then_inc(m.s_summed.sem, 1)

    for a, landed in enumerate(m.s_rows):
        landed.past(16 * gathers(a % ROWS) * (GROUPS // 2))
    m.s_picked.past(GROUPS)
    m.s_chain.past(LINKS * GROUPS)
    for s in (m.s_landed, m.s_arrived, m.s_heads_turned, m.s_scanned):
        s.past(GROUPS + 1)
    for s in (m.s_turned_back, m.s_factor, m.s_dve_turn, m.s_act_turn):
        s.past(GROUPS)
    for s in (m.s_high, m.s_middle, m.s_rest, m.s_split):
        s.past(2 * GROUPS)
    m.s_top.past(2 * QUAD + GROUP * GROUPS)
    m.s_group_free.past(2 + GROUPS)
    m.s_summed.past(SLOTS * QUAD + STEPS)
    m.s_added.past(QUAD + STEPS)
    for s in (m.s_expanded, m.s_logits_ready, m.s_probs_ready):
        s.past(2 + QUADS * GROUPS)
    for s in (m.s_turned_copied, m.s_max_summed, m.s_below, m.s_last_ready, m.s_onehot_ready, m.s_message_ready, m.s_turned_ready):
        s.past(QUADS * GROUPS)


def head_stage(m, att_src, att_dst, heads, wide):
    nc = m.nc
    H = heads
    h = m.acc[:, 0:TILES, 0:D]
    a_src, a_dst = m.acc[:, 0:TILES, D:D + H], m.shift[:, 0:TILES, 0:H]
    maximum, small = m.shift[:, 0:TILES, H:2 * H], m.small[:, 0:TILES, 0:H]
    with nc.Block() as block:

        @block.vector
        def _(dve):
            c = Chain(dve, m.s_chain)
            c.link(nc.vector.tensor_tensor(m.tmp[:, :, :], h, over_nodes(att_src, D), ALU.mult))
            nc.vector.tensor_reduce(a_src, by_head(m.tmp[:, :, :], H), AX.X, ALU.add).then_inc(m.s_dve_turn.sem, 1)
            dve.wait_ge(m.s_dve_turn.sem, m.s_dve_turn.at(1))
            c.link(nc.vector.tensor_tensor(m.tmp[:, :, :], h, over_nodes(att_dst, D), ALU.mult))
            c.link(nc.vector.memset(m.shift[:, :, :], 0.0))
            c.link(nc.vector.tensor_reduce(a_dst, by_head(m.tmp[:, :, :], H), AX.X, ALU.add))
            c.link(nc.vector.memset(m.top[:, :, :], 0.0))
            c.link(nc.vector.tensor_copy(m.top[:, 0:TILES, 0:H], a_src))
            c.link(nc.vector.tensor_copy(m.self_a[:, :, 0:H], a_src))
            c.link(nc.vector.tensor_copy(m.identity_b[:, :], m.identity[:, :]))
            c.link(nc.vector.memset(m.floor[:, :], -BIG))
            c.link(nc.vector.memset(m.lift[:, :], BIG))
            a_dst_all = m.shift[:, :, 0:H]
            c.link(nc.vector.tensor_copy(m.shift3[:, :, 0, 0:H], a_dst_all))
            c.link(nc.vector.tensor_tensor(m.small[:, :, 0:H], a_dst_all, m.shift3[:, :, 0, 0:H], ALU.subtract))
            c.link(nc.vector.tensor_copy(m.shift3[:, :, 1, 0:H], m.small[:, :, 0:H]))
            c.link(nc.vector.tensor_tensor(m.shift3[:, :, 2, 0:H], m.small[:, :, 0:H], m.shift3[:, :, 1, 0:H], ALU.subtract))
            c.link(nc.vector.tensor_tensor(small, a_src, a_dst, ALU.add))
            c.link(nc.vector.scalar_tensor_tensor(maximum, small, SLOPE, small, ALU.mult, ALU.max))
            dve.wait_ge(m.s_stored.sem, m.s_stored.at(16))
            nc.vector.memset(m.sums[:, :, :], 0.0)
            m.n = c.n

        @block.sync
        def _(sp):
            sp.wait_ge(m.s_dve_turn.sem, m.s_dve_turn.at(1))
            sp.dma_start(wide.rearrange("(t p) d -> p t d", p=P), m.acc[:, 0:TILES, 0:D + H]).then_inc(m.s_stored.sem, 16)
            sp.wait_ge(m.s_stored.sem, m.s_stored.at(16))

    m.s_chain.past(m.n)
    m.s_dve_turn.past(1)
    m.s_stored.past(16)


def loop_stage(m, heads, wide):
    nc = m.nc
    H = heads
    a_dst, maximum = m.shift[:, 0:TILES, 0:H], m.shift[:, 0:TILES, H:2 * H]
    small, p = m.small[:, 0:TILES, 0:H], m.self_p[:, :, 0:H]
    h = m.tmp[:, :, :]
    with nc.Block() as block:

        @block.sync
        def _(sp):
            sp.dma_start(h, wide.rearrange("(t p) d -> p t d", p=P)[:, :, 0:D]).then_inc(m.s_loaded.sem, 16)
            sp.wait_ge(m.s_loaded.sem, m.s_loaded.at(16))

        @block.vector
        def _(dve):
            c = Chain(dve, m.s_chain)
            c.link(nc.vector.tensor_tensor(p, m.self_a[:, :, 0:H], a_dst, ALU.add))
            c.link(nc.vector.scalar_tensor_tensor(small, p, SLOPE, p, ALU.mult, ALU.max))
            c.link(nc.vector.tensor_tensor(small, small, maximum, ALU.subtract))
            dve.wait_ge(m.s_act_turn.sem, m.s_act_turn.at(1))
            dve.wait_ge(m.s_loaded.sem, m.s_loaded.at(16))
            c.link(nc.vector.tensor_tensor(m.sums[:, 0:TILES, D:D + H], m.sums[:, 0:TILES, D:D + H], p, ALU.add))
            c.link(nc.vector.tensor_tensor(by_head(h, H), by_head(h, H), p.unsqueeze(3).broadcast_to([P, TILES, H, D // H]), ALU.mult))
            c.link(nc.vector.tensor_tensor(m.sums[:, 0:TILES, 0:D], m.sums[:, 0:TILES, 0:D], h, ALU.add))
            m.n = c.n

        @block.scalar
        def _(act):
            act.wait_ge(m.s_chain.sem, m.s_chain.at(3))
            nc.scalar.activation(p, small, ACT.Exp).then_inc(m.s_act_turn.sem, 1)

    m.s_chain.past(m.n)
    m.s_act_turn.past(1)
    m.s_loaded.past(16)


def divide_heads(m, c, heads, bias):
    nc = m.nc
    H = heads
    z, small, out = m.sums[:, 0:TILES, D:D + H], m.small[:, 0:TILES, 0:H], m.sums[:, 0:TILES, 0:D]
    c.link(nc.vector.tensor_scalar(small, z, SOFTMAX_EPS, None, ALU.add))
    c.link(nc.vector.reciprocal(small, small))
    c.link(nc.vector.tensor_tensor(by_head(out, H), by_head(out, H), small.unsqueeze(3).broadcast_to([P, TILES, H, D // H]), ALU.mult))
    c.link(nc.vector.tensor_tensor(out, out, over_nodes(bias, D), ALU.add))


def center(m, c, dve, value):
    nc = m.nc
    c.link(nc.vector.tensor_reduce(m.mean[:, :], value, AX.X, ALU.add))
    c.link(nc.vector.tensor_scalar(m.mean[:, :], m.mean[:, :], 1.0 / D, None, ALU.mult))
    c.link(nc.vector.tensor_tensor(value, value, over_tiles(m.mean[:, :], D), ALU.subtract))
    c.link(nc.vector.tensor_tensor(m.tmp[:, :, :], value, value, ALU.mult))
    c.link(nc.vector.tensor_reduce(m.var[:, :], m.tmp[:, :, :], AX.X, ALU.add))
    nc.vector.tensor_scalar(m.var[:, :], m.var[:, :], 1.0 / D, LN_EPS, ALU.mult, ALU.add).then_inc(m.s_dve_turn.sem, 1)


def rescale(m, c, dve, value, n):
    nc = m.nc
    dve.wait_ge(m.s_act_turn.sem, m.s_act_turn.at(n))
    c.link(nc.vector.reciprocal(m.mean[:, :], m.var[:, :]))
    c.link(nc.vector.tensor_tensor(value, value, over_tiles(m.mean[:, :], D), ALU.mult))


def root(m, act, n):
    act.wait_ge(m.s_dve_turn.sem, m.s_dve_turn.at(n))
    m.nc.scalar.activation(m.var[:, :], m.var[:, :], ACT.Sqrt).then_inc(m.s_act_turn.sem, 1)


def selu_stage(m, bias):
    nc = m.nc
    out, tmp, x = m.sums[:, 0:TILES, 0:D], m.tmp[:, :, :], m.x[:, :, :]
    with nc.Block() as block:

        @block.vector
        def _(dve):
            c = Chain(dve, m.s_chain)
            divide_heads(m, c, 8, bias)
            nc.vector.tensor_scalar(tmp, out, 0.0, None, ALU.min).then_inc(m.s_dve_turn.sem, 1)
            dve.wait_ge(m.s_act_turn.sem, m.s_act_turn.at(1))
            c.link(nc.vector.tensor_scalar(tmp, tmp, -1.0, SELU_SCALE * SELU_ALPHA, ALU.add, ALU.mult))
            c.link(nc.vector.tensor_tensor(x, x, tmp, ALU.add))
            c.link(nc.vector.tensor_scalar(out, out, 0.0, SELU_SCALE, ALU.max, ALU.mult))
            c.link(nc.vector.tensor_tensor(x, x, out, ALU.add))
            center(m, c, dve, x)
            rescale(m, c, dve, x, 2)
            c.link(nc.vector.tensor_copy(m.acc[:, 0:TILES, 0:D], x))
            c.link(nc.vector.memset(m.acc[:, :, D:D + 1], 1.0))
            m.n = c.n

        @block.scalar
        def _(act):
            act.wait_ge(m.s_dve_turn.sem, m.s_dve_turn.at(1))
            nc.scalar.activation(tmp, tmp, ACT.Exp).then_inc(m.s_act_turn.sem, 1)
            root(m, act, 2)

    m.s_chain.past(m.n)
    m.s_dve_turn.past(2)
    m.s_act_turn.past(2)


def degree_stage(m):
    nc = m.nc
    degree = m.acc[:, 0:TILES, D:D + 1].rearrange("p t o -> p (t o)")
    with nc.Block() as block:

        @block.vector
        def _(dve):
            c = Chain(dve, m.s_chain)
            c.link(nc.vector.tensor_scalar(m.mean[:, :], degree, 0.0, None, ALU.is_gt))
            nc.vector.tensor_scalar(m.var[:, :], degree, 1e-30, None, ALU.max).then_inc(m.s_dve_turn.sem, 1)
            dve.wait_ge(m.s_act_turn.sem, m.s_act_turn.at(1))
            c.link(nc.vector.reciprocal(m.dinv[:, :], m.var[:, :]))
            c.link(nc.vector.tensor_tensor(m.dinv[:, :], m.dinv[:, :], m.mean[:, :], ALU.mult))
            m.n = c.n

        @block.scalar
        def _(act):
            root(m, act, 1)

    m.s_chain.past(m.n)
    m.s_dve_turn.past(1)
    m.s_act_turn.past(1)


def bias_relu_stage(m, bias):
    nc = m.nc
    out = m.acc[:, 0:TILES, 0:D]
    with nc.Block() as block:

        @block.vector
        def _(dve):
            c = Chain(dve, m.s_chain)
            c.link(nc.vector.tensor_tensor(out, out, over_nodes(bias, D), ALU.add))
            c.link(nc.vector.tensor_scalar(out, out, 0.0, None, ALU.max))
            m.n = c.n

    m.s_chain.past(m.n)


def residual_stage(m, value):
    nc = m.nc
    x = m.x[:, :, :]
    with nc.Block() as block:

        @block.vector
        def _(dve):
            c = Chain(dve, m.s_chain)
            c.link(nc.vector.tensor_tensor(x, x, value[:, 0:TILES, 0:D], ALU.add))
            center(m, c, dve, x)
            rescale(m, c, dve, x, 1)
            m.n = c.n

        @block.scalar
        def _(act):
            root(m, act, 1)

    m.s_chain.past(m.n)
    m.s_dve_turn.past(1)
    m.s_act_turn.past(1)


def divide_stage(m, bias):
    nc = m.nc
    with nc.Block() as block:

        @block.vector
        def _(dve):
            c = Chain(dve, m.s_chain)
            divide_heads(m, c, 4, bias)
            m.n = c.n

    m.s_chain.past(m.n)


def skip_norm_stage(m, skip_bias, gain, offset):
    nc = m.nc
    out = m.sums[:, 0:TILES, 0:D]
    with nc.Block() as block:

        @block.vector
        def _(dve):
            c = Chain(dve, m.s_chain)
            c.link(nc.vector.tensor_tensor(out, out, m.tmp[:, :, :], ALU.add))
            c.link(nc.vector.tensor_tensor(out, out, over_nodes(skip_bias, D), ALU.add))
            center(m, c, dve, out)
            rescale(m, c, dve, out, 1)
            c.link(nc.vector.tensor_tensor(out, out, over_nodes(gain, D), ALU.mult))
            c.link(nc.vector.tensor_tensor(out, out, over_nodes(offset, D), ALU.add))
            m.n = c.n

        @block.scalar
        def _(act):
            root(m, act, 1)

    m.s_chain.past(m.n)
    m.s_dve_turn.past(1)
    m.s_act_turn.past(1)


def scale_stage(m, bias=None, relu=False):
    nc = m.nc
    out = m.acc[:, 0:TILES, 0:D]
    with nc.Block() as block:

        @block.vector
        def _(dve):
            c = Chain(dve, m.s_chain)
            c.link(nc.vector.tensor_tensor(out, out, over_tiles(m.dinv[:, :], D), ALU.mult))
            if bias is not None:
                c.link(nc.vector.tensor_tensor(out, out, over_nodes(bias, D), ALU.add))
            if relu:
                c.link(nc.vector.tensor_scalar(out, out, 0.0, None, ALU.max))
            m.n = c.n

    m.s_chain.past(m.n)


def output_stage(m, out):
    nc = m.nc
    full = (TILES - 1) * P
    with nc.Block() as block:

        @block.sync
        def _(sp):
            sp.dma_start(out[0:full, :].rearrange("(t p) d -> p t d", p=P), m.x[:, 0:TILES - 1, :]).then_inc(m.s_stored.sem, 16)
            sp.dma_start(out[full:N, :], m.x[0:N - full, TILES - 1, :]).then_inc(m.s_stored.sem, 16)
            sp.wait_ge(m.s_stored.sem, m.s_stored.at(32))

    m.s_stored.past(32)


def build(nc, w, out):
    with ExitStack() as ctx:
        m = Memory(nc, ctx)

        def sb(name, shape, dt=fp32):
            return ctx.enter_context(nc.sbuf_tensor(name, shape, dt))

        m.pick_pad = sb("pick_pad", [1, 2, P], i32)
        m.columns_i = sb("columns_i", [P, P], i32)
        m.step_number_i = sb("step_number_i", [P, GROUPS], i32)
        m.step_number = sb("step_number", [P, GROUPS])
        m.pick_group = sb("pick_group", [P, 2, GROUP], i32)
        flat = m.acc_flat
        size = GROUPS * P
        m.prep_float = flat[0:GROUP, 0:5 * size].rearrange("p (a g e) -> p a g e", a=5, g=GROUPS)
        room = m.room_flat
        m.prep_rows = room[0:GROUP, 2 * GROUP * WIDE - 3 * size:2 * GROUP * WIDE].bitcast(i32).rearrange("p (g a e) -> p g a e", g=GROUPS, a=3)
        assert TILES * D + GROUPS * TILES <= 2 * GROUP * WIDE - 3 * size
        m.match = m.stage[0:GROUP].rearrange("p a b -> p (a b)")[:, 0:GROUPS * TILES].rearrange("p (g t) -> p g t", g=GROUPS)

        params = []

        def weight(name, inputs, width):
            blocks = inputs // P
            t = sb("w_" + name, [P, blocks, width])
            params.append((t[:, :, :], w[name].rearrange("(k p) n -> p k n", p=P)))
            return t

        def row(name, width=D):
            t = sb("r_" + name, [P, width])
            source = w[name]
            if len(source.shape) == 2:
                source = source.rearrange("h c -> (h c)")
            params.append((t[:, :], spread(source)))
            return t[:, :]

        g0, g1, g2, g3 = "L0_gnn_", "L1_gnn_", "L2_gnn_", "L3_gnn_"
        W0 = weight(g0 + "W", D, D)
        s0, d0, b0 = row(g0 + "att_src"), row(g0 + "att_dst"), row(g0 + "bias")
        w0a, w0b = weight(g1 + "w0a", D, HID), weight(g1 + "w0b", HID, HID)
        w1a, w1b = weight(g1 + "w1a", HID, HID), weight(g1 + "w1b", HID, HID)
        w2a, w2b = weight(g1 + "w2a", HID, D), weight(g1 + "w2b", D, D)
        b0a, b0b = row(g1 + "b0a", HID), row(g1 + "b0b", HID)
        b1a, b1b = row(g1 + "b1a", HID), row(g1 + "b1b", HID)
        b2a, b2b = row(g1 + "b2a"), row(g1 + "b2b")
        W2, skip = weight(g2 + "W", D, D), weight(g2 + "skip_W", D, D)
        s2, d2 = row(g2 + "att_src"), row(g2 + "att_dst")
        gb, sbias, lng, lnb = row(g2 + "gat_bias"), row(g2 + "skip_b"), row(g2 + "ln_g"), row(g2 + "ln_b")
        G = [weight(g3 + f"W{n}", D, D) for n in (1, 2, 3)]
        gbias = [row(g3 + f"b{n}") for n in (1, 2, 3)]

        start_stage(m)
        count_dst = load_stage(m, w, params, w["x"])
        prepare_stage(m, count_dst)

        dense_stage(m, m.x, 1, W0, D, m.acc)
        head_stage(m, s0, d0, 8, m.rows[136])
        attention_stage(m, m.rows[136], 8)
        loop_stage(m, 8, m.rows[136])
        selu_stage(m, b0)

        store_stage(m, [(m.rows[128], m.acc[:, 0:TILES, 0:D])])
        sum_stage(m, m.rows[128], D, degree=True)
        degree_stage(m)
        dense_stage(m, m.acc, 1, w0a, HID, m.acc, b0a, relu=True)
        dense_stage(m, m.acc, 2, w0b, HID, m.acc, b0b, relu=True, table=m.rows[256])
        sum_stage(m, m.rows[256], HID)
        dense_stage(m, m.acc, 2, w1a, HID, m.acc, b1a, relu=True)
        dense_stage(m, m.acc, 2, w1b, HID, m.acc, b1b, relu=True)
        dense_stage(m, m.acc, 2, w2a, D, m.acc, table=m.rows[128])
        sum_stage(m, m.rows[128], D)
        bias_relu_stage(m, b2a)
        dense_stage(m, m.acc, 1, w2b, D, m.acc, b2b, relu=True)
        residual_stage(m, m.acc)

        dense_stage(m, m.x, 1, W2, D, m.acc)
        head_stage(m, s2, d2, 4, m.rows[132])
        attention_stage(m, m.rows[132], 4)
        loop_stage(m, 4, m.rows[132])
        divide_stage(m, gb)
        dense_stage(m, m.x, 1, skip, D, m.tmp)
        skip_norm_stage(m, sbias, lng, lnb)
        residual_stage(m, m.sums)

        for n in range(3):
            dense_stage(m, m.x if n == 0 else m.acc, 1, G[n], D, m.acc, scale=True, table=m.rows[128])
            sum_stage(m, m.rows[128], D, weighted=True)
            scale_stage(m, gbias[n], relu=n < 2)
        residual_stage(m, m.acc)
        output_stage(m, out)


def kernel(**inputs):
    import numpy as _np
    import concourse.bacc as _bacc
    from concourse.bass_utils import run_bass_kernel_spmd as _run

    nc = _bacc.Bacc("TRN2", target_bir_lowering=False, num_devices=1)
    arrays, w = {}, {}
    for name, value in inputs.items():
        a = _np.ascontiguousarray(value)
        arrays[f"in_{name}"] = a
        w[name] = nc.dram_tensor(f"in_{name}", a.shape, mybir.dt.from_np(a.dtype), kind="ExternalInput").ap()
    nc.disable_value_cache = True
    out = nc.dram_tensor("out_x", (N, D), fp32, kind="ExternalOutput").ap()
    build(nc, w, out)
    return _run(nc, [arrays], core_ids=[0]).results[0]["out_x"]
```
